# Optimizing a Trainium2 kernel written in Bass

```python
import numpy as np
import jax
import jax.numpy as jnp

def _softmax(x, axis=-1):
    return jax.nn.softmax(x, axis=axis)

def _gelu(x):
    return jax.nn.gelu(x, approximate=True)

def _silu(x):
    return jax.nn.silu(x)

def _sigmoid(x):
    return jax.nn.sigmoid(x)

def _layernorm(x, axis=-1, eps=1e-05):
    m = jnp.mean(x, axis=axis, keepdims=True)
    v = jnp.var(x, axis=axis, keepdims=True)
    return (x - m) / jnp.sqrt(v + eps)

def _scatter_add(tgt, idx, src, axis=0):
    return tgt.at[idx].add(src)

def _segment_sum(src, seg, n):
    return jax.ops.segment_sum(src, seg, n)
kernel_name = 'mk_gps_d1_gnn_r8_93bc4c'

def setup_inputs(seed: int=0):
    np.random.seed(seed)
    _w = jnp.asarray

    def _rec_inputs():
        import jax
        import jax.numpy as jnp
        _gk = jax.random.key(seed)
        x = -0.0003713 + 1 * jax.random.normal(jax.random.fold_in(_gk, 1), (6250, 256), jnp.float32)
        _s = jax.random.randint(jax.random.fold_in(_gk, 2), (50000,), 0, 6250, jnp.int32)
        _d = jax.random.randint(jax.random.fold_in(_gk, 3), (50000,), 0, 6250, jnp.int32)
        _loop = jnp.arange(6250, dtype=jnp.int32)
        src = jnp.concatenate([_s, _d, _loop])
        dst = jnp.concatenate([_d, _s, _loop])
        _o = jnp.argsort(dst, stable=True)
        src = src[_o]
        dst = dst[_o]
        edge_weight = jax.random.uniform(jax.random.fold_in(_gk, 12), (106250,), jnp.float32, 0.0, 0.0624999)
        edge_weight_n2 = jax.random.uniform(jax.random.fold_in(_gk, 13), (106250,), jnp.float32, 0.0, 0.0624999)
        return (x, src, dst, edge_weight, edge_weight_n2)
    x, src, dst, edge_weight, edge_weight_n2 = _rec_inputs()

    def _L0_gnn_setup():
        import jax, jax.numpy as jnp
        import numpy as np
        N = 6250
        E = 100000
        D_IN = 256
        D_OUT = 256

        def _spmm(row, col, val, h, n_nodes):
            return jax.ops.segment_sum(val[:, None] * h[col], row, num_segments=n_nodes)
        if __name__ == '__main__':
            out = reference(**setup_inputs())
            print(out.shape, out.dtype)
        key = jax.random.key(seed)
        ks = jax.random.split(key, 12)
        stdv = 1.0 / np.sqrt(D_OUT)
        u = lambda k, shape, s: jax.random.uniform(k, shape, jnp.float32, -s, s)
        return {'x': jax.random.normal(ks[0], (N, D_IN), jnp.float32), 'val_low': jax.random.uniform(ks[1], (E,), jnp.float32) * (1.0 / 16.0), 'val_high': jax.random.uniform(ks[2], (E,), jnp.float32) * (1.0 / 16.0), 'weight_low': u(ks[3], (D_IN, D_OUT), stdv), 'weight_high': u(ks[4], (D_IN, D_OUT), stdv), 'weight_mlp': u(ks[5], (D_IN, D_OUT), stdv), 'att_vec_low': u(ks[6], (D_OUT, 1), 1.0), 'att_vec_high': u(ks[7], (D_OUT, 1), 1.0), 'att_vec_mlp': u(ks[8], (D_OUT, 1), 1.0), 'att_vec': u(ks[9], (3, 3), 1.0 / np.sqrt(3.0)), 'row': jax.random.randint(ks[10], (E,), 0, N), 'col': jax.random.randint(ks[11], (E,), 0, N)}
    _L0_gnn_all = _L0_gnn_setup()
    _L0_gnn_in = {k: v for k, v in _L0_gnn_all.items() if k in ('weight_low', 'weight_high', 'weight_mlp', 'att_vec_low', 'att_vec_high', 'att_vec_mlp', 'att_vec')}
    del _L0_gnn_all

    def _L0_mix_setup():
        import jax, jax.numpy as jnp
        import numpy as np
        MIDC = 256
        HEADS = 8
        HEADC = MIDC // HEADS
        EPS = 1e-05

        def _ln(x, gamma, beta):
            mu = jnp.mean(x, axis=-1, keepdims=True)
            var = jnp.var(x, axis=-1, keepdims=True)
            return (x - mu) * jax.lax.rsqrt(var + EPS) * gamma + beta
        key = jax.random.key(seed)
        ks = jax.random.split(key, 8)
        B, HW, C = (8, 512, MIDC)
        s = 1.0 / np.sqrt(C)
        return {'x': jax.random.normal(ks[0], (B, HW, C), jnp.float32), 'w_qkv': jax.random.normal(ks[1], (C, 3 * C), jnp.float32) * s, 'b_qkv': jnp.zeros((3 * C,), jnp.float32), 'kln_g': jnp.ones((HEADC,), jnp.float32), 'kln_b': jnp.zeros((HEADC,), jnp.float32), 'vln_g': jnp.ones((HEADC,), jnp.float32), 'vln_b': jnp.zeros((HEADC,), jnp.float32), 'w1': jax.random.normal(ks[2], (C, C), jnp.float32) * s, 'b1': jnp.zeros((C,), jnp.float32), 'w2': jax.random.normal(ks[3], (C, C), jnp.float32) * s, 'b2': jnp.zeros((C,), jnp.float32)}
    _L0_mix_all = _L0_mix_setup()
    _L0_mix_in = {k: v for k, v in _L0_mix_all.items() if k in ('w_qkv', 'b_qkv', 'kln_g', 'kln_b', 'vln_g', 'vln_b', 'w1', 'b1', 'w2', 'b2')}
    del _L0_mix_all

    def _L0_ffn_setup():
        import jax, jax.numpy as jnp
        import numpy as np
        B, S, D = (8, 512, 256)
        H = 4 * D
        CAPACITY = 0.5
        key = jax.random.key(seed)
        ks = jax.random.split(key, 6)
        x = jax.random.normal(ks[0], (B, S, D), dtype=jnp.float32)
        attention_mask = jnp.zeros((B, 1, 1, S), dtype=jnp.float32)
        wr = jax.random.normal(ks[1], (D, 1), dtype=jnp.float32) * 0.02
        br = jnp.zeros((1,), dtype=jnp.float32)
        w1 = jax.random.normal(ks[2], (D, H), dtype=jnp.float32) * 0.02
        b1 = jnp.zeros((H,), dtype=jnp.float32)
        w2 = jax.random.normal(ks[3], (H, D), dtype=jnp.float32) * 0.02
        b2 = jnp.zeros((D,), dtype=jnp.float32)
        return {'x': x, 'attention_mask': attention_mask, 'wr': wr, 'br': br, 'w1': w1, 'b1': b1, 'w2': w2, 'b2': b2}
    _L0_ffn_all = _L0_ffn_setup()
    _L0_ffn_in = {k: v for k, v in _L0_ffn_all.items() if k in ('attention_mask', 'wr', 'br', 'w1', 'b1', 'w2', 'b2')}
    del _L0_ffn_all
    return {'x': x, 'src': src, 'dst': dst, 'edge_weight': edge_weight, 'edge_weight_n2': edge_weight_n2, 'L0_gnn_weight_low': _L0_gnn_in['weight_low'], 'L0_gnn_weight_high': _L0_gnn_in['weight_high'], 'L0_gnn_weight_mlp': _L0_gnn_in['weight_mlp'], 'L0_gnn_att_vec_low': _L0_gnn_in['att_vec_low'], 'L0_gnn_att_vec_high': _L0_gnn_in['att_vec_high'], 'L0_gnn_att_vec_mlp': _L0_gnn_in['att_vec_mlp'], 'L0_gnn_att_vec': _L0_gnn_in['att_vec'], 'L0_mix_w_qkv': _L0_mix_in['w_qkv'], 'L0_mix_b_qkv': _L0_mix_in['b_qkv'], 'L0_mix_kln_g': _L0_mix_in['kln_g'], 'L0_mix_kln_b': _L0_mix_in['kln_b'], 'L0_mix_vln_g': _L0_mix_in['vln_g'], 'L0_mix_vln_b': _L0_mix_in['vln_b'], 'L0_mix_w1': _L0_mix_in['w1'], 'L0_mix_b1': _L0_mix_in['b1'], 'L0_mix_w2': _L0_mix_in['w2'], 'L0_mix_b2': _L0_mix_in['b2'], 'L0_ffn_attention_mask': _L0_ffn_in['attention_mask'], 'L0_ffn_wr': _L0_ffn_in['wr'], 'L0_ffn_br': _L0_ffn_in['br'], 'L0_ffn_w1': _L0_ffn_in['w1'], 'L0_ffn_b1': _L0_ffn_in['b1'], 'L0_ffn_w2': _L0_ffn_in['w2'], 'L0_ffn_b2': _L0_ffn_in['b2']}

def reference(x, src, dst, edge_weight, edge_weight_n2, L0_gnn_weight_low, L0_gnn_weight_high, L0_gnn_weight_mlp, L0_gnn_att_vec_low, L0_gnn_att_vec_high, L0_gnn_att_vec_mlp, L0_gnn_att_vec, L0_mix_w_qkv, L0_mix_b_qkv, L0_mix_kln_g, L0_mix_kln_b, L0_mix_vln_g, L0_mix_vln_b, L0_mix_w1, L0_mix_b1, L0_mix_w2, L0_mix_b2, L0_ffn_attention_mask, L0_ffn_wr, L0_ffn_br, L0_ffn_w1, L0_ffn_b1, L0_ffn_w2, L0_ffn_b2):
    import jax
    import jax.numpy as jnp

    def _L0_gnn_ref(x, val_low, val_high, weight_low, weight_high, weight_mlp, att_vec_low, att_vec_high, att_vec_mlp, att_vec, row, col):
        import jax, jax.numpy as jnp
        import numpy as np
        N = 6250
        E = 100000
        D_IN = 256
        D_OUT = 256

        def _spmm(row, col, val, h, n_nodes):
            return jax.ops.segment_sum(val[:, None] * h[col], row, num_segments=n_nodes)
        if __name__ == '__main__':
            out = reference(**setup_inputs())
            print(out.shape, out.dtype)
        n = x.shape[0]
        output_low = jax.nn.relu(_spmm(row, col, val_low, x @ weight_low, n))
        output_high = jax.nn.relu(_spmm(row, col, val_high, x @ weight_high, n))
        output_mlp = jax.nn.relu(x @ weight_mlp)
        T = 3.0
        logits = jnp.concatenate([output_low @ att_vec_low, output_high @ att_vec_high, output_mlp @ att_vec_mlp], axis=1)
        att = jax.nn.softmax(jax.nn.sigmoid(logits) @ att_vec / T, axis=1)
        return 3.0 * (att[:, 0:1] * output_low + att[:, 1:2] * output_high + att[:, 2:3] * output_mlp)

    def _L0_mix_ref(x, w_qkv, b_qkv, kln_g, kln_b, vln_g, vln_b, w1, b1, w2, b2):
        import jax, jax.numpy as jnp
        import numpy as np
        MIDC = 256
        HEADS = 8
        HEADC = MIDC // HEADS
        EPS = 1e-05

        def _ln(x, gamma, beta):
            mu = jnp.mean(x, axis=-1, keepdims=True)
            var = jnp.var(x, axis=-1, keepdims=True)
            return (x - mu) * jax.lax.rsqrt(var + EPS) * gamma + beta
        B, HW, C = x.shape
        bias = x
        qkv = (x @ w_qkv + b_qkv).reshape(B, HW, HEADS, 3 * HEADC)
        qkv = qkv.transpose(0, 2, 1, 3)
        q, k, v = jnp.split(qkv, 3, axis=-1)
        k = _ln(k, kln_g, kln_b)
        v = _ln(v, vln_g, vln_b)
        kv = jnp.einsum('bhnd,bhne->bhde', k, v) / HW
        out = jnp.einsum('bhnd,bhde->bhne', q, kv)
        out = out.transpose(0, 2, 1, 3).reshape(B, HW, C)
        ret = out + bias
        h = jax.nn.gelu(ret @ w1 + b1, approximate=False)
        return h @ w2 + b2 + bias

    def _L0_ffn_ref(x, attention_mask, wr, br, w1, b1, w2, b2):
        import jax, jax.numpy as jnp
        import numpy as np
        B, S, D = (8, 512, 256)
        H = 4 * D
        CAPACITY = 0.5
        b, s, d = x.shape
        weights = (jnp.einsum('bsd,do->bso', x, wr) + br)[..., 0]
        k = max(1, int(CAPACITY * s))
        kk = k - 1 if k > 1 else 1
        _, idx = jax.lax.top_k(weights, k)
        sel_idx = idx[:, :kk]
        sel = jnp.take_along_axis(x, sel_idx[:, :, None], axis=1)
        h = jax.nn.gelu(jnp.einsum('bkd,dh->bkh', sel, w1) + b1)
        y = jnp.einsum('bkh,hd->bkd', h, w2) + b2
        w_sel = jnp.take_along_axis(weights, sel_idx, axis=1)
        y = y * w_sel[..., None]
        batch_idx = jnp.arange(b)[:, None]
        processed = jnp.zeros_like(x).at[batch_idx, sel_idx].set(y)
        return processed + x
    xn = _layernorm(x, axis=-1)
    x = x + _L0_gnn_ref(xn, edge_weight, edge_weight_n2, L0_gnn_weight_low, L0_gnn_weight_high, L0_gnn_weight_mlp, L0_gnn_att_vec_low, L0_gnn_att_vec_high, L0_gnn_att_vec_mlp, L0_gnn_att_vec, src, dst) + _L0_mix_ref(xn[None], L0_mix_w_qkv, L0_mix_b_qkv, L0_mix_kln_g, L0_mix_kln_b, L0_mix_vln_g, L0_mix_vln_b, L0_mix_w1, L0_mix_b1, L0_mix_w2, L0_mix_b2)[0]
    x = x + _L0_ffn_ref(_layernorm(x, axis=-1)[None], L0_ffn_attention_mask, L0_ffn_wr, L0_ffn_br, L0_ffn_w1, L0_ffn_b1, L0_ffn_w2, L0_ffn_b2)[0]
    return x

_drawn_inputs = setup_inputs


def setup_inputs(seed=0):
    import zlib

    import numpy as np

    out = dict(_drawn_inputs(seed))
    spreads = {'L0_mix_b_qkv': (0.0, 0.1),
     'L0_mix_kln_g': (1.0, 0.6),
     'L0_mix_kln_b': (0.0, 0.45),
     'L0_mix_vln_g': (1.0, 0.596),
     'L0_mix_vln_b': (0.0, 0.404),
     'L0_mix_b1': (0.0, 0.1),
     'L0_mix_b2': (0.0, 0.1),
     'L0_ffn_b1': (0.0, 0.8),
     'L0_ffn_b2': (0.0, 0.8)}
    factors = {'edge_weight': 4.446,
     'edge_weight_n2': 4.297,
     'L0_gnn_att_vec_low': 8.0,
     'L0_gnn_att_vec_high': 8.0,
     'L0_gnn_att_vec_mlp': 8.0,
     'L0_gnn_att_vec': 6.058,
     'L0_ffn_wr': 5.682,
     'L0_ffn_w1': 6.332,
     'L0_ffn_w2': 5.936}
    for name, (base, spread) in spreads.items():
        noise = np.random.default_rng([zlib.crc32(name.encode()), seed]).standard_normal(out[name].shape)
        drawn = base * np.exp(spread * noise) if base else spread * noise
        out[name] = jnp.asarray(drawn.astype(out[name].dtype))
    for name, factor in factors.items():
        out[name] = (out[name] * factor).astype(out[name].dtype)
    return out
```

```python
from contextlib import ExitStack

import concourse.bass as bass
from concourse import mybir

F32 = mybir.dt.float32
I32 = mybir.dt.int32
BF16 = mybir.dt.bfloat16
ALU = mybir.AluOpType
ACT = mybir.ActivationFunctionType
AX = mybir.AxisListType

P = 128
BK = 64
HALF = 8
H1, H2 = 13, 8
GR = 16
RR = 32
EPS = 1e-5
SENTINEL = -3.0e38


def ds(start, size):
    return bass.ds(start, size)


def wait(eng, sem, value):
    if isinstance(value, int) and value <= 0:
        return
    eng.wait_ge(sem, value)


def build(nc, a, out):
    N, D = a["x"].shape
    E = a["src"].shape[0]
    HID = a["L0_ffn_w1"].shape[1]
    T = -(-N // P)
    TAIL = N - (T - 1) * P
    NB = 2 * T
    KD = D // P
    KF = HID // P
    HEADS, HC = 8, 32
    SLOTS = -(-E // (P * 2 * HALF)) * 2 * HALF
    FULL = E // P
    REST = E - FULL * P
    HALVES = SLOTS // HALF
    SORTS = SLOTS // (2 * HALF)
    PAIRS = SLOTS // 2
    NG = SLOTS // HALF
    KEEP = max(1, int(0.5 * N)) - 1
    Q = T // 2
    assert D == 256 and HID == 1024 and T % 2 == 1 and NB <= H1 * H2 and SORTS == 2 * Q + 4
    assert HALVES % 8 == 0 and SLOTS % RR == 0 and FULL < SLOTS

    xn_dram = nc.dram_tensor("xn_rows", (N, D), F32).ap()
    rec_dram = nc.dram_tensor("sorted_records", (SLOTS * P, 4), F32).ap()

    with ExitStack() as ctx:
        sems = {}

        def S(name):
            if name not in sems:
                sems[name] = ctx.enter_context(nc.semaphore(name))
            return sems[name]

        def sb(name, shape, dt=F32):
            return ctx.enter_context(nc.sbuf_tensor(name, shape, dt))

        arena_a = sb("arena", [P, 12 * 1024 + 1024])
        arena_at = {}

        def carve(phase, name, shape, dt=F32):
            width = 1
            for n in shape[1:]:
                width *= n
            at = arena_at.get(phase, 0)
            arena_at[phase] = at + width
            assert at + width <= arena_a.shape[1], (phase, name, at + width)
            flat = arena_a[0:shape[0], at:at + width]
            if len(shape) == 2:
                return flat
            names = "abc"[:len(shape) - 1]
            return flat.rearrange(f"p ({' '.join(names)}) -> p {' '.join(names)}", **dict(zip(names, shape[1:])))

        rec = sb("rec", [P, SLOTS, 4])
        bkt = sb("bkt", [P, SLOTS], BF16)
        base = sb("base", [P, T * D])
        side = sb("side", [P, T * D])
        iota_nodes = sb("iota_nodes", [P, T * P], mybir.dt.uint16)
        raw = base[:, 0:4 * SLOTS].rearrange("p (a t) -> p a t", a=4)
        digit = base[:, 4 * SLOTS:8 * SLOTS].rearrange("p (a t) -> p a t", a=4)
        n1, n2 = SLOTS * H1, SLOTS * H2
        oh1 = side[:, 0:n1 // 2].bitcast(BF16)
        oh2 = base[:, 8 * SLOTS:8 * SLOTS + n2 // 2].bitcast(BF16)
        assert 8 * SLOTS + n2 // 2 <= T * D and n1 // 2 <= T * D

        ident = sb("ident", [P, P])
        ones_f = sb("ones_f", [P, P])
        ones_b = sb("ones_b", [P, P], BF16)
        before = sb("before", [P, P], BF16)
        notbefore = sb("notbefore", [P, P], BF16)
        zero_b = sb("zero_b", [P, D], BF16)
        iota_b = sb("iota_b", [P, H1 * H2], BF16)
        iota15 = sb("iota15", [P, 15])
        ramp = sb("ramp", [P, H1 * H2], I32)
        jmask = sb("jmask", [P, HALF])
        hmask = sb("hmask", [P, H1])

        wqkv = carve("first", "wqkv", [P, KD, 3 * D])
        wq = carve("first", "wq", [P, KD, D])
        wkv = carve("first", "wkv", [P, KD, 2 * D])
        wmean = sb("wmean", [P, 2 * KD * HEADS])
        bqkv = carve("first", "bqkv", [1, 3 * D])
        bkv = carve("first", "bkv", [1, 2 * D])
        bmean = sb("bmean", [1, 2 * HEADS])
        bq = sb("bq", [P, KD])
        gam = sb("gam", [P, 2, HC])
        bet = sb("bet", [P, 2, HC])
        w1m = carve("first", "w1m", [P, KD, D])
        w2m = carve("first", "w2m", [P, KD, D])
        b1m = sb("b1m", [P, KD])
        b2m = sb("b2m", [1, D])
        wmlp = carve("first", "wmlp", [P, KD, D])
        wlow = sb("wlow", [P, KD, D])
        whigh = sb("whigh", [P, KD, D])
        att_rows = sb("att_rows", [P, 3, D])
        att9 = sb("att9", [P, 9])
        wr = sb("wr", [P, D])
        br = sb("br", [P, 1])
        w1f = carve("second", "w1f", [P, KD, HID])
        w2f = carve("second", "w2f", [P, KF, D])
        b1f = sb("b1f", [P, KF])
        b2f = sb("b2f", [P, D])

        oh = sb("oh", [P, 2, HALF, NB], BF16)
        junk = sb("junk", [P, HALF, NB], BF16)
        pos = sb("pos", [P, 2, HALF])
        ibits = sb("ibits", [P, 6, HALF], I32)
        idx = sb("idx", [P, 2, HALF], I32)
        rstage = sb("rstage", [P, 2, HALF, 4])
        hsel = sb("hsel", [P, HALF, H2])
        hcnt = sb("hcnt", [P, H2])
        hexp = sb("hexp", [P, H1, H2])
        counts = sb("counts", [P, H1 * H2])
        incl = sb("incl", [P, H1 * H2])
        starts = sb("starts", [P, H1 * H2])
        pclip = sb("pclip", [1, H1 * H2])
        pint = sb("pint", [1, H1 * H2], I32)
        ptab = sb("ptab", [1, H1 * H2], I32)

        xl = carve("first", "xl", [P, 2, D])
        xs = carve("first", "xs", [P, 2, D])
        st6 = sb("st6", [P, 6])
        mv = sb("mv", [P, 2])
        sd = sb("sd", [P, 2])
        xt = carve("first", "xt", [P, 2, KD, P])
        kvc = carve("first", "kvc", [P, 2 * D])
        sq = carve("first", "sq", [P, 2 * D])
        kvs = sb("kvs", [P, 3, 2 * HEADS])
        kn = carve("first", "kn", [P, 2, 2, D])
        kvbd = carve("first", "kvbd", [P, KD, P])
        wqt = carve("first", "wqt", [P, KD, D])
        atm = carve("first", "atm", [P, KD, D])
        w1p = carve("first", "w1p", [P, KD, D])
        bp = sb("bp", [P, KD])
        b1p = sb("b1p", [P, KD])
        ht = carve("first", "ht", [P, 2, KD, P])
        ml = carve("first", "ml", [P, 2, D])
        tmp = sb("tmp", [P, D])
        lg = sb("lg", [P, 3])
        lgc = sb("lgc", [P, 3])
        l3 = sb("l3", [P, T])

        gring = carve("second", "gring", [P, GR, D])
        rring = sb("rring", [P, RR, 4])
        msel = sb("msel", [P, 2, P])
        agg = carve("second", "agg", [P, 2, D])
        aggt = carve("second", "aggt", [P, KD, 2, P])
        lh = carve("second", "lh", [P, 2 * D])
        sg = sb("sg", [P, 8, 3])
        x1 = carve("second", "x1", [P, D])
        x2n = carve("second", "x2n", [P, D])
        x2t = carve("second", "x2t", [P, KD, P])
        nr = sb("nr", [P, 8])
        nri = sb("nri", [P, 2], I32)
        fh = carve("second", "fh", [P, KF, P])
        wall = sb("wall", [P, T])
        ybuf = sb("ybuf", [P, D])
        keyi = sb("keyi", [P, 4, T], I32)
        keyf = sb("keyf", [P, 4, T])
        cand = sb("cand", [P, 15])
        cmpb = carve("second", "cmpb", [P, 15, T])
        cnt = sb("cnt", [P, 15])
        kc = sb("kc", [P, 16])
        thr = sb("thr", [P, 2, 5])
        eqb = sb("eqb", [P, T], BF16)
        mask = sb("mask", [P, T])

        bank = [ctx.enter_context(nc.psum_tensor(f"bank{i}", [P, 512], F32)) for i in range(8)]
        psT = [bank[2][:, 0:256], bank[2][:, 256:512]]
        R = [bank[0][:, 0:NB], bank[1][:, 0:NB]]

        block = ctx.enter_context(nc.Block())

        def each_tile(eng, body, first_peeled=True):
            body(0, 0)
            body(0, 1)
            with eng.Fori(1, Q) as q:
                body(q, 0)
                body(q, 1)
            body(Q, 0)

        def rows(dram, i, n=P):
            return dram[ds(i * P, n), :] if not isinstance(i, int) else dram[i * P:i * P + n, :]

        def last(q):
            return isinstance(q, int) and q == Q

        @block.sync
        def _(sp):
            sp.wait_ge(S("raw_padded"), 4)
            for k, name in enumerate(("src", "dst", "edge_weight", "edge_weight_n2")):
                v = a[name]
                dst = raw[:, k, :] if k > 1 else raw[:, k, :].bitcast(I32)
                with nc.allow_non_contiguous_dma(reason="the few edges beyond whole columns"):
                    sp.dma_start(dst[:, 0:FULL], v[0:FULL * P].rearrange("(p t) -> p t", p=P)).then_inc(S("raw_loaded"), 16)
                    sp.dma_start(dst[0:REST, FULL:FULL + 1], v[FULL * P:E].rearrange("(p t) -> p t", t=1)).then_inc(S("raw_loaded"), 16)
            sp.dma_start(wqkv[:, :, :], a["L0_mix_w_qkv"].rearrange("(k p) n -> p k n", p=P)).then_inc(S("qkv_loaded"), 16)
            sp.dma_start(bqkv[:, :], a["L0_mix_b_qkv"].rearrange("(o n) -> o n", o=1)).then_inc(S("qkv_loaded"), 16)
            for r, t in ((a["L0_mix_kln_g"], gam[:, 0, :]), (a["L0_mix_vln_g"], gam[:, 1, :]),
                         (a["L0_mix_kln_b"], bet[:, 0, :]), (a["L0_mix_vln_b"], bet[:, 1, :])):
                sp.dma_start(t, r.rearrange("(o n) -> o n", o=1).to_broadcast([P, HC])).then_inc(S("ln_loaded"), 16)

            def load_x(q, par):
                i = 2 * q + par
                wait(sp, S("xn_ready"), i - 1)
                n = TAIL if last(q) else P
                if last(q):
                    sp.wait_ge(S("tail_zeroed"), 1)
                sp.dma_start(xl[0:n, par, :], rows(a["x"], i, n)).then_inc(S(f"x_loaded{par}"), 16)

            def store_xn(q, par):
                i = 2 * q + par
                n = TAIL if last(q) else P
                sp.wait_ge(S("xn_ready"), i + 1)
                sp.dma_start(rows(xn_dram, i, n), xs[0:n, par, :]).then_inc(S(f"xn_stored{par}"), 16)

            load_x(0, 0)
            load_x(0, 1)
            store_xn(0, 0)
            load_x(1, 0)
            store_xn(0, 1)
            load_x(1, 1)
            with sp.Fori(1, Q - 1) as q:
                store_xn(q, 0)
                load_x(q + 1, 0)
                store_xn(q, 1)
                load_x(q + 1, 1)
            store_xn(Q - 1, 0)
            load_x(Q, 0)
            store_xn(Q - 1, 1)
            store_xn(Q, 0)

            cols = dict(reason="biases by partition")
            big = [(w1m, "L0_mix_w1"), (w2m, "L0_mix_w2"), (wmlp, "L0_gnn_weight_mlp"),
                   (wlow, "L0_gnn_weight_low"), (whigh, "L0_gnn_weight_high")]
            for t, name in big:
                sp.dma_start(t[:, :, :], a[name].rearrange("(k p) n -> p k n", p=P)).then_inc(S("w_loaded"), 16)
            for k, name in enumerate(("L0_gnn_att_vec_low", "L0_gnn_att_vec_high", "L0_gnn_att_vec_mlp")):
                sp.dma_start(att_rows[:, k, :], a[name].rearrange("d o -> o d").to_broadcast([P, D])).then_inc(S("w_loaded"), 16)
            sp.dma_start(wr[:, :], a["L0_ffn_wr"].rearrange("d o -> o d").to_broadcast([P, D])).then_inc(S("w_loaded"), 16)
            sp.dma_start(br[:, :], a["L0_ffn_br"].rearrange("(o n) -> o n", o=1).to_broadcast([P, 1])).then_inc(S("w_loaded"), 16)
            sp.dma_start(b2f[:, :], a["L0_ffn_b2"].rearrange("(o n) -> o n", o=1).to_broadcast([P, D])).then_inc(S("w_loaded"), 16)
            sp.dma_start(att9[:, :], a["L0_gnn_att_vec"].rearrange("(o a) b -> o (a b)", o=1).to_broadcast([P, 9])).then_inc(S("w_loaded"), 16)
            sp.dma_start(b2m[:, :], a["L0_mix_b2"].rearrange("(o n) -> o n", o=1)).then_inc(S("w_loaded"), 16)
            with nc.allow_non_contiguous_dma(**cols):
                sp.dma_start(b1m[:, :], a["L0_mix_b1"].rearrange("(k p) -> p k", p=P)).then_inc(S("w_loaded"), 16)
                sp.dma_start(b1f[:, :], a["L0_ffn_b1"].rearrange("(k p) -> p k", p=P)).then_inc(S("w_loaded"), 16)
                for h in range(HEADS):
                    j, hh = h // 4, h % 4
                    sp.dma_start(bq[hh * HC:hh * HC + HC, j:j + 1],
                                 a["L0_mix_b_qkv"][h * 3 * HC:h * 3 * HC + HC].rearrange("(p o) -> p o", o=1)).then_inc(S("w_loaded"), 16)

            sp.wait_ge(S("xn_stored0"), 16 * (Q + 1))
            sp.wait_ge(S("xn_stored1"), 16 * Q)

            def load_mix(q, par):
                i = 2 * q + par
                wait(sp, S("mix_read"), i - 1)
                n = TAIL if last(q) else P
                if isinstance(q, int) and q == 0:
                    sp.wait_ge(S("kv_summed"), 1)
                sp.dma_start(xs[0:n, par, :], rows(xn_dram, i, n)).then_inc(S(f"mix_loaded{par}"), 16)
                sp.dma_start(xl[0:n, par, :], rows(a["x"], i, n)).then_inc(S(f"mix_loaded{par}"), 16)

            each_tile(sp, load_mix)

            sp.wait_ge(S("mix_read"), T)
            sp.wait_ge(S("l3_ready"), T)
            for t, name in ((w1f, "L0_ffn_w1"), (w2f, "L0_ffn_w2")):
                sp.dma_start(t[:, :, :], a[name].rearrange("(k p) n -> p k n", p=P)).then_inc(S("ffn_loaded"), 16)

            for hf in range(2):
                sp.wait_ge(S(f"scattered{hf}"), 16 * HALF * SORTS)

            def load_records(group, ring):
                src = rec_dram[ds(group * (P * HALF), P * HALF), :] if not isinstance(group, int) else \
                    rec_dram[group * P * HALF:(group + 1) * P * HALF, :]
                sp.dma_start(rring[:, ring * HALF:(ring + 1) * HALF, :].rearrange("p s f -> p (s f)"),
                             src.rearrange("(p s) f -> p (s f)", p=P)).then_inc(S(f"records{ring}"), 16)

            for r in range(4):
                load_records(r, r)

            def relay(kk, u):
                k = 2 * kk + u
                for j in range(GR):
                    sp.wait_ge(S(f"gathered{j}"), 16 * k + 16)
                    sp.sem_inc(S("g_ready"), 1)
                    if j == GR // 2 - 1 and not (isinstance(k, int) and k in (0, NG // 2 - 1)):
                        sp.wait_ge(S("pair_free"), 8 * k)
                        for v in range(2):
                            load_records(2 * k + 2 + v, 2 * (1 - u) + v)

            relay(0, 0)
            relay(0, 1)
            with sp.Fori(1, SLOTS // RR - 1) as kk:
                relay(kk, 0)
                relay(kk, 1)
            relay(SLOTS // RR - 1, 0)
            relay(SLOTS // RR - 1, 1)

            for g in range(T // 7):
                sp.wait_ge(S("out_ready"), 7 * (g + 1))
                t0, t1 = 7 * g, 7 * (g + 1)
                full = min(t1, T - 1)
                sp.dma_start(out[t0 * P:full * P, :].rearrange("(t p) d -> p t d", p=P),
                             base[:, t0 * D:full * D].rearrange("p (t d) -> p t d", d=D)).then_inc(S("out_stored"), 16)
            sp.dma_start(out[(T - 1) * P:N, :], base[0:TAIL, (T - 1) * D:T * D]).then_inc(S("out_stored"), 16)
            sp.wait_ge(S("out_stored"), 16 * (T // 7 + 1))

        @block.gpsimd
        def _(pool):
            def const(ins):
                ins.then_inc(S("const"), 1)

            pool.memset(raw[:, 0, :].bitcast(I32)[:, FULL:SLOTS], N - 1).then_inc(S("raw_padded"), 1)
            pool.memset(raw[:, 1, :].bitcast(I32)[:, FULL:SLOTS], 0).then_inc(S("raw_padded"), 1)
            pool.memset(raw[:, 2:4, FULL:SLOTS], 0.0).then_inc(S("raw_padded"), 1)
            pool.iota(ramp[:, :], pattern=[[1, H1 * H2]], base=0, channel_multiplier=0).then_inc(S("raw_padded"), 1)
            const(pool.memset(ident[:, :], 0.0))
            const(pool.memset(ones_f[:, :], 1.0))
            const(pool.memset(ones_b[:, :], 1.0))
            const(pool.memset(before[:, :], 1.0))
            const(pool.memset(notbefore[:, :], 1.0))
            const(pool.memset(zero_b[:, :], 0.0))
            const(pool.memset(hmask[:, :], 1.0))
            const(pool.iota(ibits[:, 0, :], pattern=[[-1, HALF]], base=HALF * P, channel_multiplier=1))
            const(pool.iota(ibits[:, 1, :], pattern=[[1, HALF]], base=1, channel_multiplier=0))
            const(pool.iota(ibits[:, 2, :], pattern=[[1, HALF]], base=1 + HALF, channel_multiplier=0))
            pool.wait_ge(S("const"), 10)
            const(pool.affine_select(out=ident[:, :], in_=ident[:, :], compare_op=ALU.not_equal, fill=1.0,
                                     base=0, pattern=[[-1, P]], channel_multiplier=1))
            const(pool.affine_select(out=before[:, :], in_=before[:, :], compare_op=ALU.is_ge, fill=0.0,
                                     base=-1, pattern=[[1, P]], channel_multiplier=-1))
            const(pool.affine_select(out=notbefore[:, :], in_=notbefore[:, :], compare_op=ALU.is_ge, fill=0.0,
                                     base=0, pattern=[[-1, P]], channel_multiplier=1))
            const(pool.affine_select(out=hmask[:, :], in_=hmask[:, :], compare_op=ALU.is_ge, fill=0.0,
                                     base=0, pattern=[[-HALF, H1]], channel_multiplier=1))
            pool.wait_ge(S("const"), 14)
            const(pool.affine_select(out=hmask[:, :], in_=hmask[:, :], compare_op=ALU.is_ge, fill=0.0,
                                     base=HALF - 1, pattern=[[HALF, H1]], channel_multiplier=-1))
            pool.iota(iota_nodes[:, :], pattern=[[1, T * P]], base=0, channel_multiplier=0,
                      allow_small_or_imprecise_dtypes=True).then_inc(S("nodes_ready"), 1)

            def scatter(g, hf):
                pool.wait_ge(S(f"idx_ready{hf}"), 2 * g + 2)
                pool.sem_inc(S("pool_tick"), 1)
                for j in range(HALF):
                    pool.indirect_dma_start(
                        rec_dram, bass.IndirectOffsetOnAxis(ap=idx[:, hf, j:j + 1], axis=0),
                        rstage[:, hf, j, :], None).then_inc(S(f"scattered{hf}"), 16)

            with pool.Fori(0, SORTS) as g:
                scatter(g, 0)
                scatter(g, 1)

            pool.wait_ge(S("xn_stored0"), 16 * (Q + 1))
            pool.wait_ge(S("xn_stored1"), 16 * Q)
            pool.wait_ge(S("mix_read"), T)
            pool.wait_ge(S("l3_ready"), T)

            def gather(kk):
                for v in range(RR):
                    if v % HALF == 0:
                        pool.wait_ge(S(f"records{v // HALF}"), 16 * kk + 16)
                        pool.sem_inc(S("pool_tick"), 1)
                    free = 16 * kk + v // 2 - GR // 2 + 1
                    if v % 2 == 0 and not (isinstance(free, int) and free <= 0):
                        pool.wait_ge(S("pair_free"), free)
                        pool.sem_inc(S("pool_tick"), 1)
                    pool.indirect_dma_start(
                        gring[:, v % GR, :], None, xn_dram,
                        bass.IndirectOffsetOnAxis(ap=rring[:, v, 1:2].bitcast(I32), axis=0)).then_inc(S(f"gathered{v % GR}"), 16)

            gather(0)
            with pool.Fori(1, SLOTS // RR) as kk:
                gather(kk)

            pool.wait_ge(S("y_ready"), T)
            pool.affine_select(out=wall[:, T - 1:T], in_=wall[:, T - 1:T], compare_op=ALU.is_ge, fill=SENTINEL,
                               base=TAIL - 1, pattern=[[0, 1]], channel_multiplier=-1).then_inc(S("w_masked"), 1)

        @block.vector
        def _(dve):
            chain = [0]

            def step(ins, do_wait=True):
                chain[0] += 1
                ins.then_inc(S("dve_step"), 1)
                if do_wait:
                    dve.wait_ge(S("dve_step"), chain[0])

            dve.wait_ge(S("raw_padded"), 4)
            dve.wait_ge(S("const"), 15)
            dve.wait_ge(S("raw_loaded"), 16 * 8)
            src_i = raw[:, 0, :].bitcast(I32)
            dig_i = [digit[:, k, :].bitcast(I32) for k in range(3)]
            step(dve.tensor_scalar(dig_i[0], src_i, 6, None, ALU.logical_shift_right), False)
            step(dve.tensor_scalar(dig_i[1], src_i, 9, None, ALU.logical_shift_right), False)
            step(dve.tensor_scalar(dig_i[2], src_i, 6, H2 - 1, ALU.logical_shift_right, ALU.bitwise_and), False)
            step(dve.tensor_copy(iota_b[:, :], ramp[:, :]))
            h12 = digit[:, 3, :].bitcast(BF16).rearrange("p (a t) -> p a t", a=2)
            step(dve.tensor_copy(h12[:, 0, :], dig_i[1]), False)
            step(dve.tensor_copy(h12[:, 1, :], dig_i[2]))
            n = SLOTS // HALF
            for k, (o, w) in enumerate(((oh1, H1), (oh2, H2))):
                hv = h12[:, k, :].rearrange("p (g j) -> p g j", j=HALF)
                for j in range(HALF):
                    ov = o.rearrange("p (g h j) -> p g h j", h=w, j=HALF)[:, :, :, j] if k == 0 else \
                        o.rearrange("p (g j h) -> p g j h", h=w, j=HALF)[:, :, j, :]
                    ins = dve.tensor_tensor(ov, hv[:, :, j:j + 1].to_broadcast([P, n, w]),
                                            iota_b[:, 0:w].unsqueeze(1).to_broadcast([P, n, w]), ALU.is_equal)
                    ins.then_inc(S("digits_ready"), 1)
            step(dve.tensor_copy(bkt[:, :], dig_i[0]), False)
            step(dve.tensor_copy(rec[:, :, 0], src_i), False)
            step(dve.tensor_copy(rec[:, :, 1], raw[:, 1, :]), False)
            step(dve.tensor_copy(rec[:, :, 2], raw[:, 2, :]), False)
            step(dve.tensor_copy(rec[:, :, 3], raw[:, 3, :]), False)
            step(dve.tensor_scalar(ibits[:, 3, :], ibits[:, 0, :], HALF - 1, None, ALU.bitwise_and))
            step(dve.tensor_scalar(jmask[:, :], ibits[:, 3, :], 0.0, None, ALU.is_equal))

            M = H1 * HALF
            dve.wait_ge(S("hist_done"), 1)
            step(dve.tensor_tensor(hsel[0:M, :, :], bank[7][0:M, 0:HALF * H2].rearrange("p (j h) -> p j h", j=HALF),
                                   jmask[0:M, :].unsqueeze(2).to_broadcast([M, HALF, H2]), ALU.mult))
            step(dve.tensor_reduce(hcnt[0:M, :], hsel[0:M, :, :].rearrange("p j h -> p h j"), AX.X, ALU.add))
            dve.tensor_tensor(hexp[0:M, :, :], hcnt[0:M, :].unsqueeze(1).to_broadcast([M, H1, H2]),
                              hmask[0:M, :].unsqueeze(2).to_broadcast([M, H1, H2]), ALU.mult).then_inc(S("hist_expanded"), 1)
            dve.wait_ge(S("counts_ready"), 1)
            step(dve.tensor_copy(counts[:, :], bank[6][:, 0:H1 * H2]))
            step(dve.tensor_tensor_scan(incl[:, :], counts[:, :], ones_f[:, 0:H1 * H2], 0.0, ALU.add, ALU.mult))
            dve.tensor_tensor(starts[:, :], incl[:, :], counts[:, :], ALU.subtract).then_inc(S("starts_ready"), 1)
            dve.wait_ge(S("starts_ready"), 1)
            step(dve.tensor_scalar(pclip[:, :], starts[0:1, :], float(SLOTS * P - 1), None, ALU.min))
            step(dve.tensor_copy(pint[:, :], pclip[:, :]))
            dve.tensor_scalar(ptab[:, :], pint[:, :], 8, None, ALU.logical_shift_right).then_inc(S("ptab_ready"), 1)

            dve.wait_ge(S("qkv_loaded"), 32)
            dve.wait_ge(S("ln_loaded"), 64)
            for k in range(KD):
                wv = wqkv[:, k, :].rearrange("p (h s c) -> p h s c", h=HEADS, s=3)[:, :, 1:3, :]
                mk = wmean[:, k * 16:(k + 1) * 16].rearrange("p (h s) -> p h s", s=2)
                step(dve.tensor_reduce(mk, wv, AX.X, ALU.add))
                step(dve.tensor_scalar(mk, mk, 1.0 / HC, None, ALU.mult))
                step(dve.tensor_tensor(wkv[:, k, :].rearrange("p (h s c) -> p h s c", h=HEADS, s=2), wv,
                                       mk.unsqueeze(3).to_broadcast([P, HEADS, 2, HC]), ALU.subtract), False)
                step(dve.tensor_copy(wq[:, k, :].rearrange("p (h c) -> p h c", h=HEADS),
                                     wqkv[:, k, :].rearrange("p (h s c) -> p h s c", h=HEADS, s=3)[:, :, 0, :]), False)
            bv = bqkv[:, :].rearrange("p (h s c) -> p h s c", h=HEADS, s=3)[:, :, 1:3, :]
            bm = bmean[:, :].rearrange("p (h s) -> p h s", s=2)
            step(dve.tensor_reduce(bm, bv, AX.X, ALU.add))
            step(dve.tensor_scalar(bm, bm, 1.0 / HC, None, ALU.mult))
            step(dve.tensor_tensor(bkv[:, :].rearrange("p (h s c) -> p h s c", h=HEADS, s=2), bv,
                                   bm.unsqueeze(3).to_broadcast([1, HEADS, 2, HC]), ALU.subtract))
            dve.memset(kvbd[:, :, :], 0.0).then_inc(S("wkv_ready"), 1)

            def rank(g, hf):
                h = 2 * g + hf
                tile0 = h * HALF
                wait(dve, S(f"oh_used{hf}"), g)
                dve.tensor_tensor(oh[:, hf, :, :], bkt[:, ds(tile0, HALF)].unsqueeze(2).to_broadcast([P, HALF, NB]),
                                  iota_b[:, 0:NB].unsqueeze(1).to_broadcast([P, HALF, NB]), ALU.is_equal).then_inc(S(f"oh_ready{hf}"), 1)
                dve.wait_ge(S(f"oh_ready{hf}"), g + 1)
                for j in range(HALF):
                    dve.wait_ge(S("rank_ready"), tile0 + j + 1)
                    dve.tensor_tensor_reduce(out=junk[:, j, :], in0=R[j % 2], in1=oh[:, hf, j, :], scale=1.0, scalar=0.0,
                                             op0=ALU.mult, op1=ALU.add, accum_out=pos[:, hf, j:j + 1]).then_inc(S("rank_read"), 1)
                dve.wait_ge(S("rank_read"), tile0 + HALF)
                wait(dve, S(f"scattered{hf}"), 16 * HALF * g)
                dve.tensor_copy(rstage[:, hf, :, :].rearrange("p j f -> p (j f)"),
                                rec[:, :, :].rearrange("p t f -> p (t f)")[:, ds(tile0 * 4, HALF * 4)]).then_inc(S(f"idx_ready{hf}"), 1)
                dve.tensor_copy(ibits[:, 0, :], pos[:, hf, :]).then_inc(S("idx_step"), 1)
                dve.wait_ge(S("idx_step"), 3 * h + 1)
                dve.tensor_scalar(ibits[:, 1, :], ibits[:, 0, :], 10, 10, ALU.logical_shift_right, ALU.logical_shift_left)
                dve.tensor_scalar(ibits[:, 2, :], ibits[:, 0, :], P - 1, 3, ALU.bitwise_and, ALU.logical_shift_left)
                dve.tensor_scalar(ibits[:, 3, :], ibits[:, 0, :], 7, HALF - 1, ALU.logical_shift_right, ALU.bitwise_and).then_inc(S("idx_step"), 1)
                dve.wait_ge(S("idx_step"), 3 * h + 2)
                dve.tensor_tensor(ibits[:, 4, :], ibits[:, 1, :], ibits[:, 2, :], ALU.bitwise_or).then_inc(S("idx_step"), 1)
                dve.wait_ge(S("idx_step"), 3 * h + 3)
                dve.tensor_tensor(idx[:, hf, :], ibits[:, 4, :], ibits[:, 3, :], ALU.bitwise_or).then_inc(S(f"idx_ready{hf}"), 1)

            def normalise(q, par):
                i = 2 * q + par
                if last(q):
                    dve.wait_ge(S("xn_ready"), i)
                    dve.memset(xl[:, par, :], 0.0).then_inc(S("tail_zeroed"), 1)
                dve.wait_ge(S(f"x_loaded{par}"), 16 * q + 16)
                dve.bn_stats(st6[:, :], xl[:, par, :]).then_inc(S("ln_stats"), 1)
                dve.wait_ge(S("ln_stats"), i + 1)
                dve.sem_inc(S("dve_tick"), 1)
                dve.bn_aggr(mv[:, :], st6[:, :]).then_inc(S("ln_aggr"), 1)
                dve.wait_ge(S("ln_aggr"), i + 1)
                dve.tensor_scalar(sd[:, 0:1], mv[:, 1:2], EPS, None, ALU.add).then_inc(S("ln_var"), 1)
                dve.wait_ge(S("ln_sd"), i + 1)
                dve.reciprocal(sd[:, 0:1], sd[:, 1:2]).then_inc(S("ln_rs"), 1)
                dve.wait_ge(S("ln_rs"), i + 1)
                if not (isinstance(q, int) and q == 0):
                    dve.wait_ge(S(f"xn_stored{par}"), 16 * q)
                dve.wait_ge(S("kv_psum"), i - 1) if not (isinstance(q, int) and q == 0) else None
                dve.tensor_scalar(xs[:, par, :], xl[:, par, :], mv[:, 0:1], sd[:, 0:1], ALU.subtract, ALU.mult).then_inc(S("xn_ready"), 1)
                dve.wait_ge(S("kv_sq"), i + 1)
                dve.tensor_reduce(kvs[:, 0, :], sq[:, :].rearrange("p (g c) -> p g c", c=HC), AX.X, ALU.add).then_inc(S("kv_ss"), 1)
                dve.wait_ge(S("kv_ss"), i + 1)
                dve.tensor_scalar(kvs[:, 1, :], kvs[:, 0, :], 1.0 / HC, EPS, ALU.mult, ALU.add).then_inc(S("kv_var"), 1)
                dve.wait_ge(S("kv_sd"), i + 1)
                dve.reciprocal(kvs[:, 0, :], kvs[:, 2, :]).then_inc(S("kv_rs"), 1)
                dve.wait_ge(S("kv_rs"), i + 1)
                v4 = kvc[:, :].rearrange("p (h s c) -> p h s c", h=HEADS, s=2)
                dve.tensor_tensor(v4, bank[3 + par][:, :].rearrange("p (h s c) -> p h s c", h=HEADS, s=2),
                                  kvs[:, 0, :].rearrange("p (h s) -> p h s", s=2).unsqueeze(3).to_broadcast([P, HEADS, 2, HC]),
                                  ALU.mult).then_inc(S("kv_scaled"), 1)
                dve.wait_ge(S("kv_scaled"), i + 1)
                dve.tensor_tensor(v4, v4, gam[:, :, :].unsqueeze(1).to_broadcast([P, HEADS, 2, HC]), ALU.mult).then_inc(S("kv_gam"), 1)
                dve.wait_ge(S("kv_gam"), i + 1)
                wait(dve, S("kv_added"), i - 1)
                dve.tensor_tensor(kn[:, par, :, :].rearrange("p s (h c) -> p h s c", h=HEADS), v4,
                                  bet[:, :, :].unsqueeze(1).to_broadcast([P, HEADS, 2, HC]), ALU.add).then_inc(S("kn_ready"), 1)

            def mix_out(q, par):
                i = 2 * q + par
                dve.wait_ge(S(f"mix_loaded{par}"), 32 * q + 32)
                dve.tensor_tensor(tmp[:, :], xl[:, par, :], xs[:, par, :], ALU.add).then_inc(S("mix_sum"), 1)
                dve.wait_ge(S("mlp_ready"), i + 1)
                dve.tensor_tensor_reduce(out=ybuf[:, :], in0=ml[:, par, :], in1=att_rows[:, 2, :], scale=1.0, scalar=0.0,
                                         op0=ALU.mult, op1=ALU.add, accum_out=lg[:, 2:3]).then_inc(S("l3_sum"), 1)
                dve.wait_ge(S("mix_sum"), i + 1)
                dve.wait_ge(S("mix_psum"), i + 1)
                dve.tensor_tensor(base[:, ds(i * D, D)], tmp[:, :], bank[6 + par][:, 0:D], ALU.add).then_inc(S("mix_read"), 1)
                dve.wait_ge(S("l3_sum"), i + 1)
                dve.tensor_copy(l3[:, ds(i, 1)], lg[:, 2:3]).then_inc(S("l3_ready"), 1)
                dve.wait_ge(S("l3_ready"), i + 1)

            def sort_and(g0, body):
                def both(q):
                    rank(g0 + q, 0)
                    body(q, 0)
                    rank(g0 + q, 1)
                    if not last(q):
                        body(q, 1)
                both(0)
                with dve.Fori(1, Q) as q:
                    both(q)
                both(Q)

            sort_and(0, normalise)

            dve.wait_ge(S("w_loaded"), 16 * 23)
            dve.wait_ge(S("kv_summed"), 1)
            for j in range(KD):
                for hh in range(4):
                    s = slice(hh * HC, (hh + 1) * HC)
                    step(dve.tensor_scalar(kvbd[s, j, s], bank[5][s, j * P + hh * HC:j * P + (hh + 1) * HC], 1.0 / N, None, ALU.mult), False)
            dve.wait_ge(S("dve_step"), chain[0])
            dve.wait_ge(S("wq_transposed"), 1)
            dve.tensor_copy(wqt[:, :, :].rearrange("p j c -> p (j c)"), bank[6][:, :]).then_inc(S("wqt_ready"), 1)
            dve.wait_ge(S("at_done"), 1)
            step(dve.tensor_copy(atm[:, :, :].rearrange("p j c -> p (j c)"), bank[7][:, :]), False)
            step(dve.tensor_copy(bp[:, :], bank[3][:, 0:KD]))
            for j in range(KD):
                step(dve.tensor_tensor(atm[:, j, j * P:(j + 1) * P], atm[:, j, j * P:(j + 1) * P], ident[:, :], ALU.add))
            dve.memset(nr[:, :], 0.0).then_inc(S("at_ready"), 1)
            dve.wait_ge(S("w1p_done"), 1)
            step(dve.tensor_copy(w1p[:, :, :].rearrange("p j c -> p (j c)"), bank[6][:, :]), False)
            step(dve.tensor_tensor(b1p[:, :], bank[3][:, 8:8 + KD], b1m[:, :], ALU.add))
            dve.memset(nr[:, 0:1], 0.0).then_inc(S("w1p_ready"), 1)

            sort_and(Q + 1, mix_out)
            rank(SORTS - 2, 0)
            rank(SORTS - 2, 1)
            rank(SORTS - 1, 0)
            rank(SORTS - 1, 1)

            dve.wait_ge(S("ptab_ready"), 1)
            dve.wait_ge(S("nodes_ready"), 1)

            def select(b, pair, free):
                it = pair + b
                for j in range(2):
                    dve.wait_ge(S("g_ready"), 2 * pair + j + 1)
                    dve.wait_ge(S(f"sel_used{j}"), it + 1)
                    slot = (pair % (RR // 2)) * 2 + j
                    flat = rring[:, :, :].rearrange("p s f -> p (s f)")
                    for v in range(2):
                        ins = dve.tensor_scalar(msel[:, j, v * BK:(v + 1) * BK], iota_nodes[:, ds(b * BK, BK)],
                                                flat[:, ds(slot * 4, 1)], flat[:, ds(slot * 4 + 2 + v, 1)],
                                                ALU.is_equal, ALU.mult)
                    ins.then_inc(S(f"sel_ready{j}"), 1)
                if free:
                    dve.sem_inc(S("pair_free"), 1)

            def bucket(eng, b, one):
                eng.sem_inc(S("dve_tick"), 1)
                lo = eng.value_load(ptab[0:1, ds(b, 1)], min_val=0, max_val=PAIRS - 1)
                hi = eng.value_load(ptab[0:1, ds(b + 1, 1)], min_val=0, max_val=PAIRS - 1)
                one(lo, False)
                with eng.If(lo < hi):
                    with eng.Fori(lo + 1, hi + 1) as pair:
                        one(pair, True)

            def post_a(i):
                dve.wait_ge(S("lh_ready"), i + 1)
                for k in range(2):
                    dve.tensor_tensor_reduce(out=ybuf[:, :], in0=lh[:, k * D:(k + 1) * D], in1=att_rows[:, k, :], scale=1.0,
                                             scalar=0.0, op0=ALU.mult, op1=ALU.add, accum_out=lg[:, k:k + 1]).then_inc(S("pa"), 1)
                    dve.wait_ge(S("pa"), 9 * i + k + 1)
                dve.tensor_scalar(lgc[:, 2:3], l3[:, ds(i, 1)], -87.0, None, ALU.max)
                dve.tensor_scalar(lgc[:, 0:2], lg[:, 0:2], -87.0, None, ALU.max).then_inc(S("lg_ready"), 1)
                dve.wait_ge(S("sig_exp"), i + 1)
                dve.tensor_scalar(sg[:, 1, :], sg[:, 0, :], 1.0, None, ALU.add).then_inc(S("pa"), 1)
                dve.wait_ge(S("pa"), 9 * i + 3)
                dve.reciprocal(sg[:, 2, :], sg[:, 1, :]).then_inc(S("pa"), 1)
                dve.wait_ge(S("pa"), 9 * i + 4)
                dve.tensor_scalar(sg[:, 3, :], att9[:, 0:3], sg[:, 2, 0:1], None, ALU.mult).then_inc(S("pa"), 1)
                dve.wait_ge(S("pa"), 9 * i + 5)
                dve.scalar_tensor_tensor(sg[:, 4, :], att9[:, 3:6], sg[:, 2, 1:2], sg[:, 3, :], ALU.mult, ALU.add).then_inc(S("pa"), 1)
                dve.wait_ge(S("pa"), 9 * i + 6)
                dve.scalar_tensor_tensor(sg[:, 3, :], att9[:, 6:9], sg[:, 2, 2:3], sg[:, 4, :], ALU.mult, ALU.add).then_inc(S("pa"), 1)
                dve.wait_ge(S("pa"), 9 * i + 7)
                dve.tensor_reduce(sg[:, 5, 0:1], sg[:, 3, :], AX.X, ALU.max).then_inc(S("pa"), 1)
                dve.wait_ge(S("pa"), 9 * i + 8)
                dve.tensor_scalar(sg[:, 5, 1:2], sg[:, 5, 0:1], -1.0 / 3.0, None, ALU.mult).then_inc(S("att_in"), 1)
                dve.wait_ge(S("att_exp"), i + 1)
                dve.reciprocal(sg[:, 7, 1:2], sg[:, 7, 0:1]).then_inc(S("pa"), 1)
                dve.wait_ge(S("pa"), 9 * i + 9)
                dve.tensor_scalar(sg[:, 4, :], sg[:, 6, :], sg[:, 7, 1:2], 3.0, ALU.mult, ALU.mult).then_inc(S("pb"), 1)
                dve.wait_ge(S("pb"), 4 * i + 1)
                dve.scalar_tensor_tensor(x1[:, :], lh[:, 0:D], sg[:, 4, 0:1], base[:, ds(i * D, D)], ALU.mult, ALU.add).then_inc(S("pb"), 1)
                dve.wait_ge(S("pb"), 4 * i + 2)
                dve.scalar_tensor_tensor(ybuf[:, :], lh[:, D:2 * D], sg[:, 4, 1:2], x1[:, :], ALU.mult, ALU.add).then_inc(S("lh_used"), 1)
                dve.wait_ge(S("lh_used"), i + 1)
                dve.scalar_tensor_tensor(x1[:, :], side[:, ds(i * D, D)], sg[:, 4, 2:3], ybuf[:, :], ALU.mult, ALU.add).then_inc(S("pb"), 1)
                dve.wait_ge(S("pb"), 4 * i + 3)
                dve.bn_stats(st6[:, :], x1[:, :]).then_inc(S("pb"), 1)
                dve.wait_ge(S("pb"), 4 * i + 4)

            def post_b(i):
                n0 = 15 * i

                def nxt(ins, k):
                    ins.then_inc(S("pc"), 1)
                    dve.wait_ge(S("pc"), n0 + k)

                dve.sem_inc(S("dve_tick"), 1)
                nxt(dve.bn_aggr(mv[:, :], st6[:, :]), 1)
                nxt(dve.tensor_scalar(nr[:, 0:1], mv[:, 1:2], EPS, None, ALU.add), 2)
                nxt(dve.tensor_scalar(nri[:, 0:1], nr[:, 0:1].bitcast(I32), 1, None, ALU.logical_shift_right), 3)
                nxt(dve.tensor_scalar(nri[:, 1:2], nri[:, 0:1], -1.0, float(0x5F3759DF), ALU.mult, ALU.add), 4)
                y = nri[:, 1:2].bitcast(F32)
                for r in range(3):
                    nxt(dve.tensor_tensor(nr[:, 1:2], y, y, ALU.mult), 5 + 3 * r)
                    nxt(dve.tensor_scalar(nr[:, 2:3], nr[:, 1:2], nr[:, 0:1], -0.5, ALU.mult, ALU.mult), 6 + 3 * r)
                    o = nr[:, 3 + r % 2:4 + r % 2]
                    nxt(dve.scalar_tensor_tensor(o, nr[:, 2:3], 1.5, y, ALU.add, ALU.mult), 7 + 3 * r)
                    y = o
                wait(dve, S("xt_psum"), i)
                nxt(dve.tensor_scalar(x2n[:, :], x1[:, :], mv[:, 0:1], y, ALU.subtract, ALU.mult), 14)
                dve.tensor_tensor(base[:, ds(i * D, D)], x1[:, :], x2n[:, :], ALU.add).then_inc(S("x2_ready"), 1)
                nxt(dve.tensor_tensor_reduce(out=ybuf[:, :], in0=x2n[:, :], in1=wr[:, :], scale=1.0, scalar=0.0,
                                             op0=ALU.mult, op1=ALU.add, accum_out=nr[:, 5:6]), 15)
                dve.tensor_scalar(wall[:, ds(i, 1)], nr[:, 5:6], br[:, 0:1], None, ALU.add).then_inc(S("w_ready"), 1)
                dve.wait_ge(S("w_ready"), i + 1)

            def ffn_out(i):
                dve.wait_ge(S("y_psum"), i + 1)
                dve.tensor_tensor(tmp[:, :], bank[7][:, 0:D], b2f[:, :], ALU.add).then_inc(S("y_read"), 1)
                dve.wait_ge(S("y_read"), i + 1)
                dve.tensor_scalar(side[:, ds(i * D, D)], tmp[:, :], wall[:, ds(i, 1)], None, ALU.mult).then_inc(S("y_ready"), 1)
                dve.wait_ge(S("y_ready"), i + 1)

            def stage(i, here, before1, before2):
                if here:
                    bucket(dve, 2 * i, lambda pair, free: select(2 * i, pair, free))
                if before1:
                    post_a(i - 1)
                if here:
                    bucket(dve, 2 * i + 1, lambda pair, free: select(2 * i + 1, pair, free))
                if before1:
                    post_b(i - 1)
                if before2:
                    ffn_out(i - 2)

            def pipeline(eng, stage):
                stage(0, True, False, False)
                stage(1, True, True, False)
                with eng.Fori(2, T) as i:
                    stage(i, True, True, True)
                stage(T, False, True, True)
                stage(T + 1, False, False, True)

            pipeline(dve, stage)

            dve.wait_ge(S("w_masked"), 1)
            wb = wall[:, :].bitcast(I32)
            step(dve.tensor_scalar(keyi[:, 0, :], wb, 31, -2147483648, ALU.arith_shift_right, ALU.bitwise_or))
            step(dve.tensor_tensor(keyi[:, 1, :], wb, keyi[:, 0, :], ALU.bitwise_xor))
            step(dve.tensor_scalar(keyi[:, 2, :], keyi[:, 1, :], 16, None, ALU.logical_shift_right), False)
            step(dve.tensor_scalar(keyi[:, 3, :], keyi[:, 1, :], 65535, None, ALU.bitwise_and), False)
            step(dve.tensor_copy(iota15[:, :], iota_b[:, 1:16]))
            step(dve.tensor_copy(keyf[:, 0, :], keyi[:, 2, :]), False)
            step(dve.tensor_copy(keyf[:, 1, :], keyi[:, 3, :]), False)
            step(dve.memset(thr[:, :, :], 0.0))
            rounds = 0
            for part in range(2):
                key = keyf[:, 0 if part == 0 else 2, :]
                for r in range(4):
                    unit = float(16 ** (3 - r))
                    step(dve.tensor_scalar(cand[:, :], iota15[:, :], unit, thr[:, part, r:r + 1], ALU.mult, ALU.add))
                    step(dve.tensor_tensor(cmpb[:, :, :], key.unsqueeze(1).to_broadcast([P, 15, T]),
                                           cand[:, :].unsqueeze(2).to_broadcast([P, 15, T]), ALU.is_ge))
                    dve.tensor_reduce(cnt[:, :], cmpb[:, :, :], AX.X, ALU.add).then_inc(S("cnt_ready"), 1)
                    rounds += 1
                    dve.wait_ge(S("cnt_total"), rounds)
                    step(dve.tensor_scalar(kc[:, 0:15], bank[0][:, 0:15], float(KEEP), None, ALU.is_ge))
                    step(dve.tensor_reduce(kc[:, 15:16], kc[:, 0:15], AX.X, ALU.add))
                    step(dve.tensor_scalar(thr[:, part, r + 1:r + 2], kc[:, 15:16], unit, thr[:, part, r:r + 1], ALU.mult, ALU.add))
                if part == 0:
                    t = thr[:, 0, 4:5]
                    step(dve.tensor_scalar(keyf[:, 3, :], keyf[:, 0, :], t, 131072.0, ALU.is_gt, ALU.mult), False)
                    step(dve.tensor_scalar(keyf[:, 2, :], keyf[:, 0, :], t, None, ALU.is_equal))
                    step(dve.tensor_scalar(keyf[:, 1, :], keyf[:, 1, :], 1.0, None, ALU.add))
                    step(dve.tensor_tensor(keyf[:, 1, :], keyf[:, 1, :], keyf[:, 2, :], ALU.mult))
                    step(dve.tensor_tensor(keyf[:, 2, :], keyf[:, 1, :], keyf[:, 3, :], ALU.add))
                    step(dve.tensor_scalar(keyf[:, 2, :], keyf[:, 2, :], -1.0, None, ALU.add))
            t = thr[:, 1, 4:5]
            step(dve.tensor_scalar(mask[:, :], keyf[:, 2, :], t, None, ALU.is_gt), False)
            step(dve.tensor_scalar(keyf[:, 0, :], keyf[:, 2, :], t, None, ALU.is_equal), False)
            step(dve.tensor_scalar(eqb[:, :], keyf[:, 2, :], t, None, ALU.is_equal))
            step(dve.tensor_reduce(kc[:, 0:1], mask[:, :], AX.X, ALU.add))
            dve.tensor_scalar(kc[:, 1:2], kc[:, 0:1], 1.0, None, ALU.mult).then_inc(S("eq_ready"), 1)
            dve.wait_ge(S("eq_done"), 1)
            step(dve.tensor_copy(keyf[:, 1, :], bank[0][:, 128:128 + T]))
            step(dve.tensor_tensor_scan(keyf[:, 3, :], keyf[:, 1, :], ones_f[:, 0:T], 0.0, ALU.add, ALU.mult))
            step(dve.tensor_tensor(keyf[:, 3, :], keyf[:, 3, :], keyf[:, 1, :], ALU.subtract))
            step(dve.tensor_tensor(keyf[:, 3, :], keyf[:, 3, :], bank[0][:, 64:64 + T], ALU.add))
            step(dve.tensor_scalar(keyf[:, 3, :], keyf[:, 3, :], bank[0][:, 200:201], float(KEEP), ALU.add, ALU.is_lt))
            step(dve.tensor_tensor(keyf[:, 3, :], keyf[:, 3, :], keyf[:, 0, :], ALU.mult))
            step(dve.tensor_tensor(mask[:, :], mask[:, :], keyf[:, 3, :], ALU.add))
            with dve.Fori(0, T) as i:
                dve.scalar_tensor_tensor(base[:, ds(i * D, D)], side[:, ds(i * D, D)], mask[:, ds(i, 1)],
                                         base[:, ds(i * D, D)], ALU.mult, ALU.add).then_inc(S("out_ready"), 1)

        @block.scalar
        def _(act):
            def dense_ln(q, par):
                i = 2 * q + par
                act.wait_ge(S("ln_var"), i + 1)
                act.activation(sd[:, 1:2], sd[:, 0:1], ACT.Sqrt).then_inc(S("ln_sd"), 1)
                act.wait_ge(S("xt_done"), i + 1)
                act.activation(xt[:, par, :, :].rearrange("p k n -> p (k n)"), psT[par], ACT.Copy).then_inc(S("xt_ready"), 1)
                act.wait_ge(S("kv_psum"), i + 1)
                wait(act, S("kv_ss"), i)
                act.activation(sq[:, :], bank[3 + par][:, :], ACT.Square).then_inc(S("kv_sq"), 1)
                act.wait_ge(S("kv_var"), i + 1)
                act.activation(kvs[:, 2, :], kvs[:, 1, :], ACT.Sqrt).then_inc(S("kv_sd"), 1)

            def mix(q, par):
                i = 2 * q + par
                act.wait_ge(S("mxt_done"), i + 1)
                act.activation(xt[:, par, :, :].rearrange("p k n -> p (k n)"), psT[par], ACT.Copy).then_inc(S("mxt_ready"), 1)
                act.wait_ge(S("h_psum"), i + 1)
                for f in range(KD):
                    act.activation(ht[:, par, f, :], bank[3][:, par * D + f * P:par * D + (f + 1) * P], ACT.Gelu,
                                   bias=b1p[:, f:f + 1]).then_inc(S("h_ready"), 1)
                act.wait_ge(S("mlp_psum"), i + 1)
                mp = bank[4 + par][:, 0:D]
                wait(act, S("l3_sum"), i - 1)
                act.activation(side[:, ds(i * D, D)], mp, ACT.Relu)
                act.activation(ml[:, par, :], mp, ACT.Relu).then_inc(S("mlp_ready"), 1)

            each_tile(act, dense_ln)
            act.wait_ge(S("w1p_ready"), 1)
            each_tile(act, mix)

            def stage(i, here, before1, before2):
                if before2:
                    act.wait_ge(S("xt_psum"), i - 1)
                    act.activation(x2t[:, :, :].rearrange("p k n -> p (k n)"), bank[6][:, 0:D], ACT.Copy).then_inc(S("x2t_ready"), 1)
                if before1:
                    act.wait_ge(S("lg_ready"), i)
                    act.activation(sg[:, 0, :], lgc[:, :], ACT.Exp, scale=-1.0).then_inc(S("sig_exp"), 1)
                    act.wait_ge(S("att_in"), i)
                    act.activation(sg[:, 6, :], sg[:, 3, :], ACT.Exp, bias=sg[:, 5, 1:2], scale=1.0 / 3.0,
                                   accum_out=sg[:, 7, 0:1]).then_inc(S("att_exp"), 1)
                if here:
                    act.wait_ge(S("acc_a"), i + 1)
                    act.activation(agg[:, 0, :], bank[0][:, 0:D], ACT.Copy).then_inc(S("agg_a"), 1)
                if before2:
                    act.wait_ge(S("f1_psum"), i - 1)
                    for f in range(KF):
                        act.activation(fh[:, f, :], bank[4 + f // 4][:, (f % 4) * P:(f % 4 + 1) * P], ACT.Gelu_apprx_tanh,
                                       bias=b1f[:, f:f + 1]).then_inc(S("fh_ready"), 1)
                if here:
                    act.wait_ge(S("acc_b"), i + 1)
                    act.activation(agg[:, 1, :], bank[1][:, 0:D], ACT.Copy).then_inc(S("agg_b"), 1)
                    act.wait_ge(S("at_psum"), i + 1)
                    for k in range(KD):
                        ins = act.activation(aggt[:, k, :, :].rearrange("p v (h n) -> p v h n", h=2),
                                             bank[2][:, k * D:(k + 1) * D].rearrange("p (h v n) -> p v h n", h=2, v=2), ACT.Copy)
                    ins.then_inc(S("aggt_ready"), 1)
                    act.wait_ge(S("lh_psum"), i + 1)
                    wait(act, S("lh_used"), i)
                    act.activation(lh[:, :], bank[3][:, :], ACT.Relu).then_inc(S("lh_ready"), 1)

            stage(0, True, False, False)
            stage(1, True, True, False)
            with act.Fori(2, T) as i:
                stage(i, True, True, True)
            stage(T, False, True, True)
            stage(T + 1, False, False, True)

        @block.tensor
        def _(pe):
            def mm(out_, lhsT, rhs, start, stop, **kw):
                return pe.matmul(out_, lhsT, rhs, start=start, stop=stop, **kw)

            M = H1 * HALF
            pe.wait_ge(S("digits_ready"), 2 * HALF)
            mm(bank[7][0:M, 0:HALF * H2], oh1[:, 0:M], oh2[:, 0:HALF * H2], True, False, skip_group_check=True)
            with pe.Fori(1, SLOTS // HALF) as g:
                mm(bank[7][0:M, 0:HALF * H2], oh1[:, ds(g * M, M)], oh2[:, ds(g * (HALF * H2), HALF * H2)], False, False, skip_group_check=True)
            mm(bank[7][0:M, 0:HALF * H2], zero_b[:, 0:M], zero_b[:, 0:HALF * H2], False, True, skip_group_check=True).then_inc(S("hist_done"), 1)
            pe.wait_ge(S("hist_expanded"), 1)
            mm(bank[6][:, 0:H1 * H2], ones_f[0:M, :], hexp[0:M, :, :].rearrange("p a b -> p (a b)"), True, True).then_inc(S("counts_ready"), 1)
            pe.wait_ge(S("starts_ready"), 1)
            for r in range(2):
                mm(R[r], ones_f[0:1, :], starts[0:1, 0:NB], True, False, skip_group_check=True)
            pe.wait_ge(S("wkv_ready"), 1)
            mm(bank[5][:, 0:D], zero_b[:, 0:P], zero_b[:, :], True, False, skip_group_check=True)

            def rank(g, hf):
                tile0 = (2 * g + hf) * HALF
                o = [oh[:, hf, j, :] for j in range(HALF)]

                def add(r, w, j):
                    return mm(R[r], w[:, :], o[j], False, False, skip_group_check=True)

                pe.wait_ge(S(f"oh_ready{hf}"), g + 1)
                for j in range(HALF):
                    if j >= 2:
                        pe.wait_ge(S("rank_read"), tile0 + j - 1)
                        add(j % 2, notbefore, j - 2)
                    if j >= 1:
                        add(j % 2, ones_b, j - 1)
                    add(j % 2, before, j).then_inc(S("rank_ready"), 1)
                pe.wait_ge(S("rank_read"), tile0 + HALF - 1)
                add(0, notbefore, HALF - 2)
                add(0, ones_b, HALF - 1)
                pe.wait_ge(S("rank_read"), tile0 + HALF)
                add(1, notbefore, HALF - 1).then_inc(S(f"oh_used{hf}"), 1)

            def dense_kv(q, par):
                i = 2 * q + par
                n = TAIL if last(q) else P
                pe.wait_ge(S("xn_ready"), i + 1)
                for k in range(KD):
                    ins = pe.transpose(psT[par][:, k * P:(k + 1) * P], xs[:, par, k * P:(k + 1) * P], ident[:, :])
                ins.then_inc(S("xt_done"), 1)
                pe.wait_ge(S("xt_ready"), i + 1)
                wait(pe, S("kv_scaled"), i - 1)
                kv = bank[3 + par][:, :]
                mm(kv, ones_f[0:1, :], bkv[:, :], True, False)
                for k in range(KD):
                    ins = mm(kv, xt[:, par, k, :], wkv[:, k, :], False, k == KD - 1)
                ins.then_inc(S("kv_psum"), 1)

            def add_kv(q, par):
                i = 2 * q + par
                n = TAIL if last(q) else P
                pe.wait_ge(S("kn_ready"), i + 1)
                for j in range(KD):
                    ins = mm(bank[5][:, j * P:(j + 1) * P], kn[0:n, par, 0, j * P:(j + 1) * P], kn[0:n, par, 1, j * P:(j + 1) * P],
                             False, False, skip_group_check=True)
                ins.then_inc(S("kv_added"), 1)

            def mix(q, par):
                i = 2 * q + par
                pe.wait_ge(S(f"mix_loaded{par}"), 32 * q + 32)
                for k in range(KD):
                    ins = pe.transpose(psT[par][:, k * P:(k + 1) * P], xs[:, par, k * P:(k + 1) * P], ident[:, :])
                ins.then_inc(S("mxt_done"), 1)
                pe.wait_ge(S("mxt_ready"), i + 1)
                wait(pe, S("h_ready"), 2 * i - 2)
                for f in range(KD):
                    for k in range(KD):
                        ins = mm(bank[3][:, par * D + f * P:par * D + (f + 1) * P], w1p[:, k, f * P:(f + 1) * P], xt[:, par, k, :],
                                 k == 0, k == KD - 1)
                ins.then_inc(S("h_psum"), 1)
                wait(pe, S("mlp_ready"), i - 1)
                for k in range(KD):
                    ins = mm(bank[4 + par][:, 0:D], xt[:, par, k, :], wmlp[:, k, :], k == 0, k == KD - 1)
                ins.then_inc(S("mlp_psum"), 1)
                wait(pe, S("mix_read"), i - 1)
                mm(bank[6 + par][:, 0:D], ones_f[0:1, :], b2m[:, :], True, False)
                pe.wait_ge(S("h_ready"), 2 * i + 2)
                for f in range(KD):
                    ins = mm(bank[6 + par][:, 0:D], ht[:, par, f, :], w2m[:, f, :], False, f == KD - 1)
                ins.then_inc(S("mix_psum"), 1)

            def loop1(q):
                rank(q, 0)
                dense_kv(q, 0)
                add_kv(q, 0)
                rank(q, 1)
                if not last(q):
                    dense_kv(q, 1)
                    add_kv(q, 1)

            loop1(0)
            with pe.Fori(1, Q) as q:
                loop1(q)
            loop1(Q)
            mm(bank[5][:, 0:D], zero_b[:, 0:P], zero_b[:, :], False, True, skip_group_check=True).then_inc(S("kv_summed"), 1)

            for j in range(KD):
                for k in range(KD):
                    ins = pe.transpose(bank[6][:, j * D + k * P:j * D + (k + 1) * P], wq[:, k, j * P:(j + 1) * P], ident[:, :])
            ins.then_inc(S("wq_transposed"), 1)
            pe.wait_ge(S("wqt_ready"), 1)
            for j in range(KD):
                mm(bank[7][:, j * D:(j + 1) * D], kvbd[:, j, :], wqt[:, j, :], True, True)
            pe.wait_ge(S("w_loaded"), 16 * 23)
            for j in range(KD):
                ins = mm(bank[3][:, j:j + 1], kvbd[:, j, :], bq[:, j:j + 1], True, True)
            ins.then_inc(S("at_done"), 1)
            pe.wait_ge(S("at_ready"), 1)
            for k in range(KD):
                for j in range(KD):
                    mm(bank[6][:, k * D:(k + 1) * D], atm[:, j, k * P:(k + 1) * P], w1m[:, j, :], j == 0, j == KD - 1)
            for f in range(KD):
                for j in range(KD):
                    ins = mm(bank[3][:, 8 + f:9 + f], w1m[:, j, f * P:(f + 1) * P], bp[:, j:j + 1], j == 0, j == KD - 1)
            ins.then_inc(S("w1p_done"), 1)
            pe.wait_ge(S("w1p_ready"), 1)

            def loop2(q):
                rank(Q + 1 + q, 0)
                mix(q, 0)
                rank(Q + 1 + q, 1)
                if not last(q):
                    mix(q, 1)

            loop2(0)
            with pe.Fori(1, Q) as q:
                loop2(q)
            loop2(Q)
            for g in (SORTS - 2, SORTS - 1):
                rank(g, 0)
                rank(g, 1)

            pe.wait_ge(S("ptab_ready"), 1)
            for j in range(2):
                pe.sem_inc(S(f"sel_used{j}"), 1)
            pe.wait_ge(S("ffn_loaded"), 32)
            pe.wait_ge(S("rank_read"), SLOTS)

            def sum_pair(b, pair, acc):
                it = pair + b
                for j in range(2):
                    pe.wait_ge(S(f"sel_ready{j}"), it + 1)
                    mm(acc[:, 0:D], msel[:, j, :], gring[:, :, :].rearrange("p s d -> p (s d)")[:, ds((pair % (GR // 2)) * (2 * D) + j * D, D)],
                       False, False, skip_group_check=True).then_inc(S(f"sel_used{j}"), 1)

            def bucket(b, acc, done):
                mm(acc[:, 0:D], zero_b[:, 0:P], zero_b[:, :], True, False, skip_group_check=True)
                lo = pe.value_load(ptab[0:1, ds(b, 1)], min_val=0, max_val=PAIRS - 1)
                hi = pe.value_load(ptab[0:1, ds(b + 1, 1)], min_val=0, max_val=PAIRS - 1)
                sum_pair(b, lo, acc)
                with pe.If(lo < hi):
                    with pe.Fori(lo + 1, hi + 1) as pair:
                        sum_pair(b, pair, acc)
                mm(acc[:, 0:D], zero_b[:, 0:P], zero_b[:, :], False, True, skip_group_check=True).then_inc(S(done), 1)

            def stage(i, here, before1, before2):
                if before1:
                    pe.wait_ge(S("x2t_ready"), i - 1) if before2 else None
                if here:
                    wait(pe, S("agg_a"), i)
                    bucket(2 * i, bank[0], "acc_a")
                if before2:
                    pe.wait_ge(S("x2t_ready"), i - 1)
                    for f in range(KF):
                        for k in range(KD):
                            ins = mm(bank[4 + f // 4][:, (f % 4) * P:(f % 4 + 1) * P], w1f[:, k, f * P:(f + 1) * P], x2t[:, k, :],
                                     k == 0, k == KD - 1)
                    ins.then_inc(S("f1_psum"), 1)
                if here:
                    wait(pe, S("agg_b"), i)
                    bucket(2 * i + 1, bank[1], "acc_b")

                def down(f0, f1):
                    for f in range(f0, f1):
                        pe.wait_ge(S("fh_ready"), (i - 2) * KF + f + 1)
                        ins = mm(bank[7][:, 0:D], fh[:, f, :], w2f[:, f, :], f == 0, f == KF - 1)
                    return ins

                if before2:
                    wait(pe, S("y_read"), i - 2)
                    down(0, KF // 2)
                if here:
                    pe.wait_ge(S("agg_b"), i + 1)
                    for k in range(KD):
                        for h in range(2):
                            ins = pe.transpose(bank[2][:, k * D + h * P:k * D + (h + 1) * P], agg[:, h, k * P:(k + 1) * P], ident[:, :])
                    ins.then_inc(S("at_psum"), 1)
                if before2:
                    down(KF // 2, KF).then_inc(S("y_psum"), 1)
                if here:
                    pe.wait_ge(S("aggt_ready"), i + 1)
                    wait(pe, S("lh_ready"), i)
                    for v, w in enumerate((wlow, whigh)):
                        for k in range(KD):
                            ins = mm(bank[3][:, v * D:(v + 1) * D], aggt[:, k, v, :], w[:, k, :], k == 0, k == KD - 1)
                    ins.then_inc(S("lh_psum"), 1)
                if before1:
                    pe.wait_ge(S("x2_ready"), i)
                    for k in range(KD):
                        ins = pe.transpose(bank[6][:, k * P:(k + 1) * P], x2n[:, k * P:(k + 1) * P], ident[:, :])
                    ins.then_inc(S("xt_psum"), 1)

            stage(0, True, False, False)
            stage(1, True, True, False)
            with pe.Fori(2, T) as i:
                stage(i, True, True, True)
            stage(T, False, True, True)
            stage(T + 1, False, False, True)

            for r in range(8):
                pe.wait_ge(S("cnt_ready"), r + 1)
                mm(bank[0][:, 0:15], ones_f[:, :], cnt[:, :], True, True).then_inc(S("cnt_total"), 1)
            pe.wait_ge(S("eq_ready"), 1)
            mm(bank[0][:, 64:64 + T], before[:, :], eqb[:, :], True, True)
            mm(bank[0][:, 128:128 + T], ones_b[:, :], eqb[:, :], True, True)
            mm(bank[0][:, 200:201], ones_f[:, :], kc[:, 1:2], True, True).then_inc(S("eq_done"), 1)


_INS = ["x", "src", "dst", "edge_weight", "edge_weight_n2",
        "L0_gnn_weight_low", "L0_gnn_weight_high", "L0_gnn_weight_mlp",
        "L0_gnn_att_vec_low", "L0_gnn_att_vec_high", "L0_gnn_att_vec_mlp", "L0_gnn_att_vec",
        "L0_mix_w_qkv", "L0_mix_b_qkv", "L0_mix_kln_g", "L0_mix_kln_b", "L0_mix_vln_g", "L0_mix_vln_b",
        "L0_mix_w1", "L0_mix_b1", "L0_mix_w2", "L0_mix_b2",
        "L0_ffn_wr", "L0_ffn_br", "L0_ffn_w1", "L0_ffn_b1", "L0_ffn_w2", "L0_ffn_b2"]


def kernel(**inputs):
    import numpy as np
    import concourse.bacc as bacc
    from concourse.bass_utils import run_bass_kernel_spmd

    nc = bacc.Bacc("TRN2", target_bir_lowering=False, num_devices=1)
    arrays, args = {}, {}
    for name in _INS:
        v = np.ascontiguousarray(inputs[name])
        arrays[f"in_{name}"] = v
        args[name] = nc.dram_tensor(f"in_{name}", v.shape, mybir.dt.from_np(v.dtype), kind="ExternalInput").ap()
    out = nc.dram_tensor("out_0", inputs["x"].shape, F32, kind="ExternalOutput").ap()
    build(nc, args, out)
    r = run_bass_kernel_spmd(nc, [arrays], core_ids=[0])
    return r.results[0]["out_0"]
```

```python
from contextlib import ExitStack

import concourse.bass as bass
from concourse import mybir

F32 = mybir.dt.float32
I32 = mybir.dt.int32
BF16 = mybir.dt.bfloat16
ALU = mybir.AluOpType
ACT = mybir.ActivationFunctionType
AX = mybir.AxisListType

P = 128
BK = 64
HALF = 8
H1, H2 = 13, 8
GR = 16
RR = 32
EPS = 1e-5
SENTINEL = -3.0e38


def ds(start, size):
    return bass.ds(start, size)


def wait(eng, sem, value):
    if isinstance(value, int) and value <= 0:
        return
    eng.wait_ge(sem, value)


def build(nc, a, out):
    N, D = a["x"].shape
    E = a["src"].shape[0]
    HID = a["L0_ffn_w1"].shape[1]
    T = -(-N // P)
    TAIL = N - (T - 1) * P
    NB = 2 * T
    KD = D // P
    KF = HID // P
    HEADS, HC = 8, 32
    SLOTS = -(-E // (P * 2 * HALF)) * 2 * HALF
    FULL = E // P
    REST = E - FULL * P
    HALVES = SLOTS // HALF
    SORTS = SLOTS // (2 * HALF)
    PAIRS = SLOTS // 2
    PBITS = (PAIRS - 1).bit_length()
    NG = SLOTS // HALF
    KEEP = max(1, int(0.5 * N)) - 1
    Q = T // 2
    assert D == 256 and HID == 1024 and T % 2 == 1 and NB < H1 * H2 and SORTS == 2 * Q + 4
    assert HALVES % 8 == 0 and SLOTS % RR == 0 and FULL < SLOTS

    xn_dram = nc.dram_tensor("xn_rows", (N, D), F32).ap()
    rec_dram = nc.dram_tensor("sorted_records", (SLOTS * P, 4), F32).ap()

    with ExitStack() as ctx:
        sems = {}

        def S(name):
            if name not in sems:
                sems[name] = ctx.enter_context(nc.semaphore(name))
            return sems[name]

        def sb(name, shape, dt=F32):
            return ctx.enter_context(nc.sbuf_tensor(name, shape, dt))

        arena_a = sb("arena", [P, 12 * 1024 + 1024])
        arena_at = {}

        def carve(phase, name, shape, dt=F32):
            width = 1
            for n in shape[1:]:
                width *= n
            at = arena_at.get(phase, 0)
            arena_at[phase] = at + width
            assert at + width <= arena_a.shape[1], (phase, name, at + width)
            flat = arena_a[0:shape[0], at:at + width]
            if len(shape) == 2:
                return flat
            names = "abc"[:len(shape) - 1]
            return flat.rearrange(f"p ({' '.join(names)}) -> p {' '.join(names)}", **dict(zip(names, shape[1:])))

        rec = sb("rec", [P, SLOTS, 4])
        bkt = sb("bkt", [P, SLOTS], BF16)
        base = sb("base", [P, T * D])
        side = sb("side", [P, T * D])
        iota_nodes = sb("iota_nodes", [P, T * P], mybir.dt.uint16)
        raw = base[:, 0:4 * SLOTS].rearrange("p (a t) -> p a t", a=4)
        digit = base[:, 4 * SLOTS:8 * SLOTS].rearrange("p (a t) -> p a t", a=4)
        n1, n2 = SLOTS * H1, SLOTS * H2
        oh1 = side[:, 0:n1 // 2].bitcast(BF16)
        oh2 = base[:, 8 * SLOTS:8 * SLOTS + n2 // 2].bitcast(BF16)
        assert 8 * SLOTS + n2 // 2 <= T * D and n1 // 2 <= T * D

        ident = sb("ident", [P, P])
        ones_f = sb("ones_f", [P, P])
        ones_b = sb("ones_b", [P, P], BF16)
        before = sb("before", [P, P], BF16)
        notbefore = sb("notbefore", [P, P], BF16)
        zero_b = sb("zero_b", [P, D], BF16)
        iota_b = sb("iota_b", [P, H1 * H2], BF16)
        iota15 = sb("iota15", [P, 15])
        ramp = sb("ramp", [P, H1 * H2], I32)
        jmask = sb("jmask", [P, HALF])
        hmask = sb("hmask", [P, H1])

        wqkv = carve("first", "wqkv", [P, KD, 3 * D])
        wq = carve("first", "wq", [P, KD, D])
        wkv = carve("first", "wkv", [P, KD, 2 * D])
        wmean = sb("wmean", [P, 2 * KD * HEADS])
        bqkv = carve("first", "bqkv", [1, 3 * D])
        bkv = carve("first", "bkv", [1, 2 * D])
        bmean = sb("bmean", [1, 2 * HEADS])
        bq = sb("bq", [P, KD])
        gam = sb("gam", [P, 2, HC])
        bet = sb("bet", [P, 2, HC])
        w1m = carve("first", "w1m", [P, KD, D])
        w2m = carve("first", "w2m", [P, KD, D])
        b1m = sb("b1m", [P, KD])
        b2m = sb("b2m", [1, D])
        wmlp = carve("first", "wmlp", [P, KD, D])
        wlow = sb("wlow", [P, KD, D])
        whigh = sb("whigh", [P, KD, D])
        att_rows = sb("att_rows", [P, 3, D])
        att9 = sb("att9", [P, 9])
        wr = sb("wr", [P, D])
        br = sb("br", [P, 1])
        w1f = carve("second", "w1f", [P, KD, HID])
        w2f = carve("second", "w2f", [P, KF, D])
        b1f = sb("b1f", [P, KF])
        b2f = sb("b2f", [P, D])

        oh = sb("oh", [P, 2, HALF, NB], BF16)
        junk = sb("junk", [P, HALF, NB], BF16)
        pos = sb("pos", [P, 2, HALF])
        ibits = sb("ibits", [P, 6, HALF], I32)
        idx = sb("idx", [P, 2, HALF], I32)
        rstage = sb("rstage", [P, 2, HALF, 4])
        hsel = sb("hsel", [P, HALF, H2])
        hcnt = sb("hcnt", [P, H2])
        hexp = sb("hexp", [P, H1, H2])
        counts = sb("counts", [P, H1 * H2])
        incl = sb("incl", [P, H1 * H2])
        starts = sb("starts", [P, H1 * H2])
        pclip = sb("pclip", [1, H1 * H2])
        pint = sb("pint", [1, H1 * H2], I32)
        ptab = sb("ptab", [1, H1 * H2], I32)
        pparts = sb("pparts", [1, 3, T], I32)
        packed = sb("packed", [1, T], I32)

        xl = carve("first", "xl", [P, 2, D])
        xs = carve("first", "xs", [P, 2, D])
        st6 = sb("st6", [P, 6])
        mv = sb("mv", [P, 2])
        sd = sb("sd", [P, 2])
        xt = carve("first", "xt", [P, 2, KD, P])
        kvc = carve("first", "kvc", [P, 2 * D])
        sq = carve("first", "sq", [P, 2 * D])
        kvs = sb("kvs", [P, 3, 2 * HEADS])
        kn = carve("first", "kn", [P, 2, 2, D])
        kvbd = carve("first", "kvbd", [P, KD, P])
        wqt = carve("first", "wqt", [P, KD, D])
        atm = carve("first", "atm", [P, KD, D])
        w1p = carve("first", "w1p", [P, KD, D])
        bp = sb("bp", [P, KD])
        b1p = sb("b1p", [P, KD])
        ht = carve("first", "ht", [P, 2, KD, P])
        ml = carve("first", "ml", [P, 2, D])
        tmp = sb("tmp", [P, D])
        lg = sb("lg", [P, 3])
        lgc = sb("lgc", [P, 3])
        l3 = sb("l3", [P, T])

        gring = carve("second", "gring", [P, GR, D])
        rring = sb("rring", [P, RR, 4])
        msel = carve("second", "msel", [P, 4, P])
        cur = sb("cur", [P, 2, 2, 4])
        here_nodes = sb("here_nodes", [P, 2, BK])
        agg = carve("second", "agg", [P, 2, D])
        aggt = carve("second", "aggt", [P, KD, 2, P])
        lh = carve("second", "lh", [P, 2 * D])
        sg = sb("sg", [P, 8, 3])
        x1 = carve("second", "x1", [P, D])
        x2n = carve("second", "x2n", [P, D])
        x2t = carve("second", "x2t", [P, KD, P])
        nr = sb("nr", [P, 8])
        nri = sb("nri", [P, 2], I32)
        const_1_5 = sb("const_1_5", [P, 1])
        lg_prod = carve("second", "lg_prod", [P, 2, D])
        att_neg = sb("att_neg", [P, 3, 3])
        att_prod = sb("att_prod", [P, 3, 3])
        fh = carve("second", "fh", [P, KF, P])
        wall = sb("wall", [P, T])
        ybuf = sb("ybuf", [P, D])
        keyi = sb("keyi", [P, 4, T], I32)
        keyf = sb("keyf", [P, 4, T])
        cand = sb("cand", [P, 15])
        cmpb = carve("second", "cmpb", [P, 15, T])
        cnt = sb("cnt", [P, 15])
        kc = sb("kc", [P, 16])
        thr = sb("thr", [P, 2, 5])
        eqb = sb("eqb", [P, T], BF16)
        mask = sb("mask", [P, T])

        bank = [ctx.enter_context(nc.psum_tensor(f"bank{i}", [P, 512], F32)) for i in range(8)]
        psT = [bank[2][:, 0:256], bank[2][:, 256:512]]
        R = [bank[0][:, 0:NB], bank[1][:, 0:NB]]

        block = ctx.enter_context(nc.Block())

        def each_tile(eng, body, first_peeled=True):
            body(0, 0)
            body(0, 1)
            with eng.Fori(1, Q) as q:
                body(q, 0)
                body(q, 1)
            body(Q, 0)

        def pair_ranges(eng, i):
            v = eng.value_load(packed[0:1, ds(i, 1)], min_val=0, max_val=2 ** (3 * PBITS) - 1)
            one = 2 ** PBITS
            return [eng.snap(e, min_val=0, max_val=PAIRS - 1) for e in (v % one, (v // one) % one, v // (one * one))]

        def bucket_pairs(eng, lo, hi, body):
            body(lo, 0, True)
            more = eng.snap(hi - lo, min_val=0, max_val=PAIRS - 1)
            twos = eng.snap(more // 2, min_val=0, max_val=PAIRS // 2)
            with eng.If(twos > 0):
                with eng.Fori(0, twos) as t:
                    body(lo + 2 * t + 1, 1, False)
                    body(lo + 2 * t + 2, 0, False)
            with eng.If(more % 2 > 0):
                body(hi, 1, False)

        def pipeline(eng, stage):
            stage(0, True, False, False, False)
            stage(1, True, True, False, False)
            stage(2, True, True, True, False)
            with eng.Fori(3, T) as i:
                stage(i, True, True, True, True)
            stage(T, False, True, True, True)
            stage(T + 1, False, False, True, True)
            stage(T + 2, False, False, False, True)

        def rows(dram, i, n=P):
            return dram[ds(i * P, n), :] if not isinstance(i, int) else dram[i * P:i * P + n, :]

        def last(q):
            return isinstance(q, int) and q == Q

        @block.sync
        def _(sp):
            sp.wait_ge(S("raw_padded"), 4)
            for k, name in enumerate(("src", "dst", "edge_weight", "edge_weight_n2")):
                v = a[name]
                dst = raw[:, k, :] if k > 1 else raw[:, k, :].bitcast(I32)
                with nc.allow_non_contiguous_dma(reason="the few edges beyond whole columns"):
                    sp.dma_start(dst[:, 0:FULL], v[0:FULL * P].rearrange("(p t) -> p t", p=P)).then_inc(S("raw_loaded"), 16)
                    sp.dma_start(dst[0:REST, FULL:FULL + 1], v[FULL * P:E].rearrange("(p t) -> p t", t=1)).then_inc(S("raw_loaded"), 16)
            sp.dma_start(wqkv[:, :, :], a["L0_mix_w_qkv"].rearrange("(k p) n -> p k n", p=P)).then_inc(S("qkv_loaded"), 16)
            sp.dma_start(bqkv[:, :], a["L0_mix_b_qkv"].rearrange("(o n) -> o n", o=1)).then_inc(S("qkv_loaded"), 16)
            for r, t in ((a["L0_mix_kln_g"], gam[:, 0, :]), (a["L0_mix_vln_g"], gam[:, 1, :]),
                         (a["L0_mix_kln_b"], bet[:, 0, :]), (a["L0_mix_vln_b"], bet[:, 1, :])):
                sp.dma_start(t, r.rearrange("(o n) -> o n", o=1).to_broadcast([P, HC])).then_inc(S("ln_loaded"), 16)

            def load_x(q, par):
                i = 2 * q + par
                wait(sp, S("xn_ready"), i - 1)
                n = TAIL if last(q) else P
                if last(q):
                    sp.wait_ge(S("tail_zeroed"), 1)
                sp.dma_start(xl[0:n, par, :], rows(a["x"], i, n)).then_inc(S(f"x_loaded{par}"), 16)

            def store_xn(q, par):
                i = 2 * q + par
                n = TAIL if last(q) else P
                sp.wait_ge(S("xn_ready"), i + 1)
                sp.dma_start(rows(xn_dram, i, n), xs[0:n, par, :]).then_inc(S(f"xn_stored{par}"), 16)

            load_x(0, 0)
            load_x(0, 1)
            store_xn(0, 0)
            load_x(1, 0)
            store_xn(0, 1)
            load_x(1, 1)
            with sp.Fori(1, Q - 1) as q:
                store_xn(q, 0)
                load_x(q + 1, 0)
                store_xn(q, 1)
                load_x(q + 1, 1)
            store_xn(Q - 1, 0)
            load_x(Q, 0)
            store_xn(Q - 1, 1)
            store_xn(Q, 0)

            cols = dict(reason="biases by partition")
            big = [(w1m, "L0_mix_w1"), (w2m, "L0_mix_w2"), (wmlp, "L0_gnn_weight_mlp"),
                   (wlow, "L0_gnn_weight_low"), (whigh, "L0_gnn_weight_high")]
            for t, name in big:
                sp.dma_start(t[:, :, :], a[name].rearrange("(k p) n -> p k n", p=P)).then_inc(S("w_loaded"), 16)
            for k, name in enumerate(("L0_gnn_att_vec_low", "L0_gnn_att_vec_high", "L0_gnn_att_vec_mlp")):
                sp.dma_start(att_rows[:, k, :], a[name].rearrange("d o -> o d").to_broadcast([P, D])).then_inc(S("w_loaded"), 16)
            sp.dma_start(wr[:, :], a["L0_ffn_wr"].rearrange("d o -> o d").to_broadcast([P, D])).then_inc(S("w_loaded"), 16)
            sp.dma_start(br[:, :], a["L0_ffn_br"].rearrange("(o n) -> o n", o=1).to_broadcast([P, 1])).then_inc(S("w_loaded"), 16)
            sp.dma_start(b2f[:, :], a["L0_ffn_b2"].rearrange("(o n) -> o n", o=1).to_broadcast([P, D])).then_inc(S("w_loaded"), 16)
            sp.dma_start(att9[:, :], a["L0_gnn_att_vec"].rearrange("(o a) b -> o (a b)", o=1).to_broadcast([P, 9])).then_inc(S("w_loaded"), 16)
            sp.dma_start(b2m[:, :], a["L0_mix_b2"].rearrange("(o n) -> o n", o=1)).then_inc(S("w_loaded"), 16)
            with nc.allow_non_contiguous_dma(**cols):
                sp.dma_start(b1m[:, :], a["L0_mix_b1"].rearrange("(k p) -> p k", p=P)).then_inc(S("w_loaded"), 16)
                sp.dma_start(b1f[:, :], a["L0_ffn_b1"].rearrange("(k p) -> p k", p=P)).then_inc(S("w_loaded"), 16)
                for h in range(HEADS):
                    j, hh = h // 4, h % 4
                    sp.dma_start(bq[hh * HC:hh * HC + HC, j:j + 1],
                                 a["L0_mix_b_qkv"][h * 3 * HC:h * 3 * HC + HC].rearrange("(p o) -> p o", o=1)).then_inc(S("w_loaded"), 16)

            sp.wait_ge(S("xn_stored0"), 16 * (Q + 1))
            sp.wait_ge(S("xn_stored1"), 16 * Q)

            def load_mix(q, par):
                i = 2 * q + par
                wait(sp, S("mix_read"), i - 1)
                n = TAIL if last(q) else P
                if isinstance(q, int) and q == 0:
                    sp.wait_ge(S("kv_summed"), 1)
                sp.dma_start(xs[0:n, par, :], rows(xn_dram, i, n)).then_inc(S(f"mix_loaded{par}"), 16)
                sp.dma_start(xl[0:n, par, :], rows(a["x"], i, n)).then_inc(S(f"mix_loaded{par}"), 16)

            each_tile(sp, load_mix)

            sp.wait_ge(S("mix_read"), T)
            sp.wait_ge(S("l3_ready"), T)
            for t, name in ((w1f, "L0_ffn_w1"), (w2f, "L0_ffn_w2")):
                sp.dma_start(t[:, :, :], a[name].rearrange("(k p) n -> p k n", p=P)).then_inc(S("ffn_loaded"), 16)

            for hf in range(2):
                sp.wait_ge(S(f"scattered{hf}"), 16 * HALF * SORTS)

            def load_records(group, ring):
                src = rec_dram[ds(group * (P * HALF), P * HALF), :] if not isinstance(group, int) else \
                    rec_dram[group * P * HALF:(group + 1) * P * HALF, :]
                sp.dma_start(rring[:, ring * HALF:(ring + 1) * HALF, :].rearrange("p s f -> p (s f)"),
                             src.rearrange("(p s) f -> p (s f)", p=P)).then_inc(S(f"records{ring}"), 16)

            for r in range(4):
                load_records(r, r)

            def relay(kk, u):
                k = 2 * kk + u
                for j in range(GR):
                    sp.wait_ge(S(f"gathered{j}"), 16 * k + 16)
                    sp.sem_inc(S("g_ready"), 1)
                    if j == GR // 2 - 1 and not (isinstance(k, int) and k in (0, NG // 2 - 1)):
                        sp.wait_ge(S("pair_free"), 8 * k + 1)
                        for v in range(2):
                            load_records(2 * k + 2 + v, 2 * (1 - u) + v)

            relay(0, 0)
            relay(0, 1)
            with sp.Fori(1, SLOTS // RR - 1) as kk:
                relay(kk, 0)
                relay(kk, 1)
            relay(SLOTS // RR - 1, 0)
            relay(SLOTS // RR - 1, 1)

            for g in range(T // 7):
                sp.wait_ge(S("out_ready"), 7 * (g + 1))
                t0, t1 = 7 * g, 7 * (g + 1)
                full = min(t1, T - 1)
                sp.dma_start(out[t0 * P:full * P, :].rearrange("(t p) d -> p t d", p=P),
                             base[:, t0 * D:full * D].rearrange("p (t d) -> p t d", d=D)).then_inc(S("out_stored"), 16)
            sp.dma_start(out[(T - 1) * P:N, :], base[0:TAIL, (T - 1) * D:T * D]).then_inc(S("out_stored"), 16)
            sp.wait_ge(S("out_stored"), 16 * (T // 7 + 1))

        @block.gpsimd
        def _(pool):
            def const(ins):
                ins.then_inc(S("const"), 1)

            pool.memset(raw[:, 0, :].bitcast(I32)[:, FULL:SLOTS], N - 1).then_inc(S("raw_padded"), 1)
            pool.memset(raw[:, 1, :].bitcast(I32)[:, FULL:SLOTS], 0).then_inc(S("raw_padded"), 1)
            pool.memset(raw[:, 2:4, FULL:SLOTS], 0.0).then_inc(S("raw_padded"), 1)
            pool.iota(ramp[:, :], pattern=[[1, H1 * H2]], base=0, channel_multiplier=0).then_inc(S("raw_padded"), 1)
            const(pool.memset(ident[:, :], 0.0))
            const(pool.memset(ones_f[:, :], 1.0))
            const(pool.memset(ones_b[:, :], 1.0))
            const(pool.memset(before[:, :], 1.0))
            const(pool.memset(notbefore[:, :], 1.0))
            const(pool.memset(zero_b[:, :], 0.0))
            const(pool.memset(hmask[:, :], 1.0))
            const(pool.iota(ibits[:, 0, :], pattern=[[-1, HALF]], base=HALF * P, channel_multiplier=1))
            const(pool.iota(ibits[:, 1, :], pattern=[[1, HALF]], base=1, channel_multiplier=0))
            const(pool.iota(ibits[:, 2, :], pattern=[[1, HALF]], base=1 + HALF, channel_multiplier=0))
            pool.wait_ge(S("const"), 10)
            const(pool.affine_select(out=ident[:, :], in_=ident[:, :], compare_op=ALU.not_equal, fill=1.0,
                                     base=0, pattern=[[-1, P]], channel_multiplier=1))
            const(pool.affine_select(out=before[:, :], in_=before[:, :], compare_op=ALU.is_ge, fill=0.0,
                                     base=-1, pattern=[[1, P]], channel_multiplier=-1))
            const(pool.affine_select(out=notbefore[:, :], in_=notbefore[:, :], compare_op=ALU.is_ge, fill=0.0,
                                     base=0, pattern=[[-1, P]], channel_multiplier=1))
            const(pool.affine_select(out=hmask[:, :], in_=hmask[:, :], compare_op=ALU.is_ge, fill=0.0,
                                     base=0, pattern=[[-HALF, H1]], channel_multiplier=1))
            pool.wait_ge(S("const"), 14)
            const(pool.affine_select(out=hmask[:, :], in_=hmask[:, :], compare_op=ALU.is_ge, fill=0.0,
                                     base=HALF - 1, pattern=[[HALF, H1]], channel_multiplier=-1))
            pool.iota(iota_nodes[:, :], pattern=[[1, T * P]], base=0, channel_multiplier=0,
                      allow_small_or_imprecise_dtypes=True).then_inc(S("nodes_ready"), 1)

            def scatter(g, hf):
                pool.wait_ge(S(f"idx_ready{hf}"), 2 * g + 2)
                pool.sem_inc(S("pool_tick"), 1)
                for j in range(HALF):
                    pool.indirect_dma_start(
                        rec_dram, bass.IndirectOffsetOnAxis(ap=idx[:, hf, j:j + 1], axis=0),
                        rstage[:, hf, j, :], None).then_inc(S(f"scattered{hf}"), 16)

            with pool.Fori(0, SORTS) as g:
                scatter(g, 0)
                scatter(g, 1)

            pool.wait_ge(S("xn_stored0"), 16 * (Q + 1))
            pool.wait_ge(S("xn_stored1"), 16 * Q)
            pool.wait_ge(S("mix_read"), T)
            pool.wait_ge(S("l3_ready"), T)

            def gather(kk):
                for v in range(RR):
                    if v % HALF == 0:
                        pool.wait_ge(S(f"records{v // HALF}"), 16 * kk + 16)
                        pool.sem_inc(S("pool_tick"), 1)
                    free = 16 * kk + v // 2 - GR // 2 + 2
                    if v % 2 == 0 and not (isinstance(free, int) and free <= 1):
                        pool.wait_ge(S("pair_free"), free)
                        pool.sem_inc(S("pool_tick"), 1)
                    pool.indirect_dma_start(
                        gring[:, v % GR, :], None, xn_dram,
                        bass.IndirectOffsetOnAxis(ap=rring[:, v, 1:2].bitcast(I32), axis=0)).then_inc(S(f"gathered{v % GR}"), 16)

            gather(0)
            with pool.Fori(1, SLOTS // RR) as kk:
                gather(kk)

            pool.wait_ge(S("y_ready"), T)
            pool.affine_select(out=wall[:, T - 1:T], in_=wall[:, T - 1:T], compare_op=ALU.is_ge, fill=SENTINEL,
                               base=TAIL - 1, pattern=[[0, 1]], channel_multiplier=-1).then_inc(S("w_masked"), 1)

        @block.vector
        def _(dve):
            chain = [0]

            def step(ins, do_wait=True):
                chain[0] += 1
                ins.then_inc(S("dve_step"), 1)
                if do_wait:
                    dve.wait_ge(S("dve_step"), chain[0])

            dve.wait_ge(S("raw_padded"), 4)
            dve.wait_ge(S("const"), 15)
            dve.wait_ge(S("raw_loaded"), 16 * 8)
            src_i = raw[:, 0, :].bitcast(I32)
            dig_i = [digit[:, k, :].bitcast(I32) for k in range(3)]
            step(dve.tensor_scalar(dig_i[0], src_i, 6, None, ALU.logical_shift_right), False)
            step(dve.tensor_scalar(dig_i[1], src_i, 9, None, ALU.logical_shift_right), False)
            step(dve.tensor_scalar(dig_i[2], src_i, 6, H2 - 1, ALU.logical_shift_right, ALU.bitwise_and), False)
            step(dve.tensor_copy(iota_b[:, :], ramp[:, :]))
            h12 = digit[:, 3, :].bitcast(BF16).rearrange("p (a t) -> p a t", a=2)
            step(dve.tensor_copy(h12[:, 0, :], dig_i[1]), False)
            step(dve.tensor_copy(h12[:, 1, :], dig_i[2]))
            n = SLOTS // HALF
            for k, (o, w) in enumerate(((oh1, H1), (oh2, H2))):
                hv = h12[:, k, :].rearrange("p (g j) -> p g j", j=HALF)
                for j in range(HALF):
                    ov = o.rearrange("p (g h j) -> p g h j", h=w, j=HALF)[:, :, :, j] if k == 0 else \
                        o.rearrange("p (g j h) -> p g j h", h=w, j=HALF)[:, :, j, :]
                    ins = dve.tensor_tensor(ov, hv[:, :, j:j + 1].to_broadcast([P, n, w]),
                                            iota_b[:, 0:w].unsqueeze(1).to_broadcast([P, n, w]), ALU.is_equal)
                    ins.then_inc(S("digits_ready"), 1)
            step(dve.tensor_copy(bkt[:, :], dig_i[0]), False)
            step(dve.tensor_copy(rec[:, :, 0], src_i), False)
            step(dve.tensor_copy(rec[:, :, 1], raw[:, 1, :]), False)
            step(dve.tensor_copy(rec[:, :, 2], raw[:, 2, :]), False)
            step(dve.tensor_copy(rec[:, :, 3], raw[:, 3, :]), False)
            step(dve.tensor_scalar(ibits[:, 3, :], ibits[:, 0, :], HALF - 1, None, ALU.bitwise_and))
            step(dve.tensor_scalar(jmask[:, :], ibits[:, 3, :], 0.0, None, ALU.is_equal))

            M = H1 * HALF
            dve.wait_ge(S("hist_done"), 1)
            step(dve.tensor_tensor(hsel[0:M, :, :], bank[7][0:M, 0:HALF * H2].rearrange("p (j h) -> p j h", j=HALF),
                                   jmask[0:M, :].unsqueeze(2).to_broadcast([M, HALF, H2]), ALU.mult))
            step(dve.tensor_reduce(hcnt[0:M, :], hsel[0:M, :, :].rearrange("p j h -> p h j"), AX.X, ALU.add))
            dve.tensor_tensor(hexp[0:M, :, :], hcnt[0:M, :].unsqueeze(1).to_broadcast([M, H1, H2]),
                              hmask[0:M, :].unsqueeze(2).to_broadcast([M, H1, H2]), ALU.mult).then_inc(S("hist_expanded"), 1)
            dve.wait_ge(S("counts_ready"), 1)
            step(dve.tensor_copy(counts[:, :], bank[6][:, 0:H1 * H2]))
            step(dve.tensor_tensor_scan(incl[:, :], counts[:, :], ones_f[:, 0:H1 * H2], 0.0, ALU.add, ALU.mult))
            dve.tensor_tensor(starts[:, :], incl[:, :], counts[:, :], ALU.subtract).then_inc(S("starts_ready"), 1)
            dve.wait_ge(S("starts_ready"), 1)
            step(dve.tensor_scalar(pclip[:, :], starts[0:1, :], float(SLOTS * P - 1), None, ALU.min))
            step(dve.tensor_copy(pint[:, :], pclip[:, :]))
            step(dve.tensor_scalar(ptab[:, :], pint[:, :], 8, None, ALU.logical_shift_right))
            for k in range(3):
                part = ptab[:, k:k + 2 * T].rearrange("p (t u) -> p t u", u=2)[:, :, 0]
                step(dve.tensor_scalar(pparts[:, k, :], part, PBITS * k, None, ALU.logical_shift_left))
            step(dve.tensor_tensor(packed[:, :], pparts[:, 0, :], pparts[:, 1, :], ALU.bitwise_or))
            dve.tensor_tensor(packed[:, :], packed[:, :], pparts[:, 2, :], ALU.bitwise_or).then_inc(S("ptab_ready"), 1)

            dve.wait_ge(S("qkv_loaded"), 32)
            dve.wait_ge(S("ln_loaded"), 64)
            for k in range(KD):
                wv = wqkv[:, k, :].rearrange("p (h s c) -> p h s c", h=HEADS, s=3)[:, :, 1:3, :]
                mk = wmean[:, k * 16:(k + 1) * 16].rearrange("p (h s) -> p h s", s=2)
                step(dve.tensor_reduce(mk, wv, AX.X, ALU.add))
                step(dve.tensor_scalar(mk, mk, 1.0 / HC, None, ALU.mult))
                step(dve.tensor_tensor(wkv[:, k, :].rearrange("p (h s c) -> p h s c", h=HEADS, s=2), wv,
                                       mk.unsqueeze(3).to_broadcast([P, HEADS, 2, HC]), ALU.subtract), False)
                step(dve.tensor_copy(wq[:, k, :].rearrange("p (h c) -> p h c", h=HEADS),
                                     wqkv[:, k, :].rearrange("p (h s c) -> p h s c", h=HEADS, s=3)[:, :, 0, :]), False)
            bv = bqkv[:, :].rearrange("p (h s c) -> p h s c", h=HEADS, s=3)[:, :, 1:3, :]
            bm = bmean[:, :].rearrange("p (h s) -> p h s", s=2)
            step(dve.tensor_reduce(bm, bv, AX.X, ALU.add))
            step(dve.tensor_scalar(bm, bm, 1.0 / HC, None, ALU.mult))
            step(dve.tensor_tensor(bkv[:, :].rearrange("p (h s c) -> p h s c", h=HEADS, s=2), bv,
                                   bm.unsqueeze(3).to_broadcast([1, HEADS, 2, HC]), ALU.subtract))
            dve.memset(kvbd[:, :, :], 0.0).then_inc(S("wkv_ready"), 1)

            def rank(g, hf):
                h = 2 * g + hf
                tile0 = h * HALF
                wait(dve, S(f"oh_used{hf}"), g)
                dve.tensor_tensor(oh[:, hf, :, :], bkt[:, ds(tile0, HALF)].unsqueeze(2).to_broadcast([P, HALF, NB]),
                                  iota_b[:, 0:NB].unsqueeze(1).to_broadcast([P, HALF, NB]), ALU.is_equal).then_inc(S(f"oh_ready{hf}"), 1)
                dve.wait_ge(S(f"oh_ready{hf}"), g + 1)
                for j in range(HALF):
                    dve.wait_ge(S("rank_ready"), tile0 + j + 1)
                    dve.tensor_tensor_reduce(out=junk[:, j, :], in0=R[j % 2], in1=oh[:, hf, j, :], scale=1.0, scalar=0.0,
                                             op0=ALU.mult, op1=ALU.add, accum_out=pos[:, hf, j:j + 1]).then_inc(S("rank_read"), 1)
                dve.wait_ge(S("rank_read"), tile0 + HALF)
                wait(dve, S(f"scattered{hf}"), 16 * HALF * g)
                dve.tensor_copy(rstage[:, hf, :, :].rearrange("p j f -> p (j f)"),
                                rec[:, :, :].rearrange("p t f -> p (t f)")[:, ds(tile0 * 4, HALF * 4)]).then_inc(S(f"idx_ready{hf}"), 1)
                dve.tensor_copy(ibits[:, 0, :], pos[:, hf, :]).then_inc(S("idx_step"), 1)
                dve.wait_ge(S("idx_step"), 3 * h + 1)
                dve.tensor_scalar(ibits[:, 1, :], ibits[:, 0, :], 10, 10, ALU.logical_shift_right, ALU.logical_shift_left)
                dve.tensor_scalar(ibits[:, 2, :], ibits[:, 0, :], P - 1, 3, ALU.bitwise_and, ALU.logical_shift_left)
                dve.tensor_scalar(ibits[:, 3, :], ibits[:, 0, :], 7, HALF - 1, ALU.logical_shift_right, ALU.bitwise_and).then_inc(S("idx_step"), 1)
                dve.wait_ge(S("idx_step"), 3 * h + 2)
                dve.tensor_tensor(ibits[:, 4, :], ibits[:, 1, :], ibits[:, 2, :], ALU.bitwise_or).then_inc(S("idx_step"), 1)
                dve.wait_ge(S("idx_step"), 3 * h + 3)
                dve.tensor_tensor(idx[:, hf, :], ibits[:, 4, :], ibits[:, 3, :], ALU.bitwise_or).then_inc(S(f"idx_ready{hf}"), 1)

            def normalise(q, par):
                i = 2 * q + par
                if last(q):
                    dve.wait_ge(S("xn_ready"), i)
                    dve.memset(xl[:, par, :], 0.0).then_inc(S("tail_zeroed"), 1)
                dve.wait_ge(S(f"x_loaded{par}"), 16 * q + 16)
                dve.bn_stats(st6[:, :], xl[:, par, :]).then_inc(S("ln_stats"), 1)
                dve.wait_ge(S("ln_stats"), i + 1)
                dve.sem_inc(S("dve_tick"), 1)
                dve.bn_aggr(mv[:, :], st6[:, :]).then_inc(S("ln_aggr"), 1)
                dve.wait_ge(S("ln_aggr"), i + 1)
                dve.tensor_scalar(sd[:, 0:1], mv[:, 1:2], EPS, None, ALU.add).then_inc(S("ln_var"), 1)
                dve.wait_ge(S("ln_sd"), i + 1)
                dve.reciprocal(sd[:, 0:1], sd[:, 1:2]).then_inc(S("ln_rs"), 1)
                dve.wait_ge(S("ln_rs"), i + 1)
                if not (isinstance(q, int) and q == 0):
                    dve.wait_ge(S(f"xn_stored{par}"), 16 * q)
                dve.wait_ge(S("kv_psum"), i - 1) if not (isinstance(q, int) and q == 0) else None
                dve.tensor_scalar(xs[:, par, :], xl[:, par, :], mv[:, 0:1], sd[:, 0:1], ALU.subtract, ALU.mult).then_inc(S("xn_ready"), 1)
                dve.wait_ge(S("kv_sq"), i + 1)
                dve.tensor_reduce(kvs[:, 0, :], sq[:, :].rearrange("p (g c) -> p g c", c=HC), AX.X, ALU.add).then_inc(S("kv_ss"), 1)
                dve.wait_ge(S("kv_ss"), i + 1)
                dve.tensor_scalar(kvs[:, 1, :], kvs[:, 0, :], 1.0 / HC, EPS, ALU.mult, ALU.add).then_inc(S("kv_var"), 1)
                dve.wait_ge(S("kv_sd"), i + 1)
                dve.reciprocal(kvs[:, 0, :], kvs[:, 2, :]).then_inc(S("kv_rs"), 1)
                dve.wait_ge(S("kv_rs"), i + 1)
                v4 = kvc[:, :].rearrange("p (h s c) -> p h s c", h=HEADS, s=2)
                dve.tensor_tensor(v4, bank[3 + par][:, :].rearrange("p (h s c) -> p h s c", h=HEADS, s=2),
                                  kvs[:, 0, :].rearrange("p (h s) -> p h s", s=2).unsqueeze(3).to_broadcast([P, HEADS, 2, HC]),
                                  ALU.mult).then_inc(S("kv_scaled"), 1)
                dve.wait_ge(S("kv_scaled"), i + 1)
                dve.tensor_tensor(v4, v4, gam[:, :, :].unsqueeze(1).to_broadcast([P, HEADS, 2, HC]), ALU.mult).then_inc(S("kv_gam"), 1)
                dve.wait_ge(S("kv_gam"), i + 1)
                wait(dve, S("kv_added"), i - 1)
                dve.tensor_tensor(kn[:, par, :, :].rearrange("p s (h c) -> p h s c", h=HEADS), v4,
                                  bet[:, :, :].unsqueeze(1).to_broadcast([P, HEADS, 2, HC]), ALU.add).then_inc(S("kn_ready"), 1)

            def mix_out(q, par):
                i = 2 * q + par
                dve.wait_ge(S(f"mix_loaded{par}"), 32 * q + 32)
                dve.tensor_tensor(tmp[:, :], xl[:, par, :], xs[:, par, :], ALU.add).then_inc(S("mix_sum"), 1)
                dve.wait_ge(S("mlp_ready"), i + 1)
                dve.tensor_tensor_reduce(out=ybuf[:, :], in0=ml[:, par, :], in1=att_rows[:, 2, :], scale=1.0, scalar=0.0,
                                         op0=ALU.mult, op1=ALU.add, accum_out=lg[:, 2:3]).then_inc(S("l3_sum"), 1)
                dve.wait_ge(S("mix_sum"), i + 1)
                dve.wait_ge(S("mix_psum"), i + 1)
                dve.tensor_tensor(base[:, ds(i * D, D)], tmp[:, :], bank[6 + par][:, 0:D], ALU.add).then_inc(S("mix_read"), 1)
                dve.wait_ge(S("l3_sum"), i + 1)
                dve.tensor_copy(l3[:, ds(i, 1)], lg[:, 2:3]).then_inc(S("l3_ready"), 1)
                dve.wait_ge(S("l3_ready"), i + 1)

            def sort_and(g0, body):
                def both(q):
                    rank(g0 + q, 0)
                    body(q, 0)
                    rank(g0 + q, 1)
                    if not last(q):
                        body(q, 1)
                both(0)
                with dve.Fori(1, Q) as q:
                    both(q)
                both(Q)

            sort_and(0, normalise)

            dve.wait_ge(S("w_loaded"), 16 * 23)
            dve.wait_ge(S("kv_summed"), 1)
            for j in range(KD):
                for hh in range(4):
                    s = slice(hh * HC, (hh + 1) * HC)
                    step(dve.tensor_scalar(kvbd[s, j, s], bank[5][s, j * P + hh * HC:j * P + (hh + 1) * HC], 1.0 / N, None, ALU.mult), False)
            dve.wait_ge(S("dve_step"), chain[0])
            dve.wait_ge(S("wq_transposed"), 1)
            dve.tensor_copy(wqt[:, :, :].rearrange("p j c -> p (j c)"), bank[6][:, :]).then_inc(S("wqt_ready"), 1)
            dve.wait_ge(S("at_done"), 1)
            step(dve.tensor_copy(atm[:, :, :].rearrange("p j c -> p (j c)"), bank[7][:, :]), False)
            step(dve.tensor_copy(bp[:, :], bank[3][:, 0:KD]))
            for j in range(KD):
                step(dve.tensor_tensor(atm[:, j, j * P:(j + 1) * P], atm[:, j, j * P:(j + 1) * P], ident[:, :], ALU.add))
            dve.memset(nr[:, :], 0.0).then_inc(S("at_ready"), 1)
            dve.wait_ge(S("w1p_done"), 1)
            step(dve.tensor_copy(w1p[:, :, :].rearrange("p j c -> p (j c)"), bank[6][:, :]), False)
            step(dve.tensor_tensor(b1p[:, :], bank[3][:, 8:8 + KD], b1m[:, :], ALU.add))
            dve.memset(nr[:, 0:1], 0.0).then_inc(S("w1p_ready"), 1)

            sort_and(Q + 1, mix_out)
            rank(SORTS - 2, 0)
            rank(SORTS - 2, 1)
            rank(SORTS - 1, 0)
            rank(SORTS - 1, 1)

            dve.wait_ge(S("ptab_ready"), 1)
            dve.wait_ge(S("nodes_ready"), 1)

            def select(b, pair, k, first):
                it = dve.snap(pair + b)
                gathered = dve.snap(2 * pair + 2)
                at = (pair % (RR // 2)) * 8
                free = dve.snap(2 * it + 2 if first else 2 * it)
                copied = dve.snap(it + 1)
                dve.wait_ge(S("g_ready"), gathered)
                dve.wait_ge(S("sel_ready"), free)
                dve.tensor_copy(cur[:, k, :, :].rearrange("p s f -> p (s f)"),
                                rring[:, :, :].rearrange("p s f -> p (s f)")[:, ds(at, 8)]).then_inc(S("rec_copied"), 1)
                dve.wait_ge(S("rec_copied"), copied)
                dve.wait_ge(S("sel_used"), free)
                for j in range(2):
                    dve.scalar_tensor_tensor(msel[:, 2 * k + j, :].rearrange("p (v n) -> p v n", v=2), here_nodes[:, :, :],
                                             cur[:, k, j, 0:1], cur[:, k, j, 2:4].unsqueeze(2).to_broadcast([P, 2, BK]),
                                             ALU.is_equal, ALU.mult).then_inc(S("sel_ready"), 1)
                if not first:
                    dve.sem_inc(S("pair_free"), 1)

            def bucket(b, lo, hi):
                if not (isinstance(b, int) and b == 0):
                    dve.wait_ge(S("sel_ready"), 2 * (lo + b) + 2)
                dve.tensor_copy(here_nodes[:, :, :], iota_nodes[:, ds(b * BK, BK)].unsqueeze(1).to_broadcast([P, 2, BK])).then_inc(S("nodes_set"), 1)
                dve.wait_ge(S("nodes_set"), b + 1)
                bucket_pairs(dve, lo, hi, lambda pair, k, first: select(b, pair, k, first))

            def post_a(i):
                n0 = 13 * i

                def nxt(ins, k):
                    ins.then_inc(S("pa"), 1)
                    dve.wait_ge(S("pa"), n0 + k)

                dve.tensor_copy(lg[:, 2:3], l3[:, ds(i, 1)])
                dve.wait_ge(S("lh_ready"), i + 1)
                for k in range(2):
                    ins = dve.tensor_tensor_reduce(out=lg_prod[:, k, :], in0=lh[:, k * D:(k + 1) * D], in1=att_rows[:, k, :], scale=1.0,
                                                   scalar=0.0, op0=ALU.mult, op1=ALU.add, accum_out=lg[:, k:k + 1])
                ins.then_inc(S("lg_ready"), 1)
                dve.wait_ge(S("sig_tanh"), i + 1)
                nxt(dve.scalar_tensor_tensor(att_prod[:, :, :], sg[:, 0, :].unsqueeze(1).to_broadcast([P, 3, 3]), 1.0, att_neg[:, :, :],
                                             ALU.add, ALU.mult), 1)
                nxt(dve.tensor_reduce(sg[:, 3, :], att_prod[:, :, :], AX.X, ALU.add), 2)
                dve.tensor_reduce(sg[:, 5, 0:1], sg[:, 3, :], AX.X, ALU.min).then_inc(S("att_in"), 1)
                dve.wait_ge(S("att_tanh"), i + 1)
                dve.tensor_scalar(sg[:, 1, :], sg[:, 6, :], 1.0, None, ALU.add)
                nxt(dve.tensor_scalar(sg[:, 2, :], sg[:, 6, :], -1.0, 1.0, ALU.mult, ALU.add), 3)
                nxt(dve.reciprocal(sg[:, 0, :], sg[:, 2, :]), 4)
                nxt(dve.tensor_tensor_reduce(out=sg[:, 4, :], in0=sg[:, 0, :], in1=sg[:, 1, :], scale=1.0, scalar=0.0,
                                             op0=ALU.mult, op1=ALU.add, accum_out=sg[:, 7, 0:1]), 5)
                nxt(dve.reciprocal(sg[:, 7, 1:2], sg[:, 7, 0:1]), 6)
                nxt(dve.tensor_scalar(sg[:, 1, :], sg[:, 4, :], sg[:, 7, 1:2], 3.0, ALU.mult, ALU.mult), 7)
                nxt(dve.scalar_tensor_tensor(x1[:, :], lh[:, 0:D], sg[:, 1, 0:1], base[:, ds(i * D, D)], ALU.mult, ALU.add), 8)
                dve.scalar_tensor_tensor(ybuf[:, :], lh[:, D:2 * D], sg[:, 1, 1:2], x1[:, :], ALU.mult, ALU.add).then_inc(S("lh_used"), 1)
                dve.wait_ge(S("lh_used"), i + 1)
                nxt(dve.scalar_tensor_tensor(x1[:, :], side[:, ds(i * D, D)], sg[:, 1, 2:3], ybuf[:, :], ALU.mult, ALU.add), 9)
                nxt(dve.bn_stats(st6[:, :], x1[:, :]), 10)
                dve.sem_inc(S("dve_tick"), 1)
                nxt(dve.bn_aggr(mv[:, :], st6[:, :]), 11)
                dve.tensor_scalar(nr[:, 1:2], mv[:, 1:2], EPS, -0.5, ALU.add, ALU.mult)
                nxt(dve.tensor_scalar(nr[:, 0:1], mv[:, 1:2], EPS, None, ALU.add), 12)
                nxt(dve.tensor_scalar(nri[:, 0:1], nr[:, 0:1].bitcast(I32), 1, None, ALU.logical_shift_right), 13)
                dve.tensor_scalar(nri[:, 1:2], nri[:, 0:1], -1.0, float(0x5F3759DF), ALU.mult, ALU.add).then_inc(S("x1_guess"), 1)

            def post_b(i):
                dve.wait_ge(S("x1_rs"), i + 1)
                wait(dve, S("xt_psum"), i)
                dve.tensor_scalar(x2n[:, :], x1[:, :], mv[:, 0:1], nr[:, 4:5], ALU.subtract, ALU.mult).then_inc(S("x2_ready"), 1)
                dve.wait_ge(S("x2_ready"), i + 1)
                dve.tensor_tensor(base[:, ds(i * D, D)], x1[:, :], x2n[:, :], ALU.add)
                dve.tensor_tensor_reduce(out=ybuf[:, :], in0=x2n[:, :], in1=wr[:, :], scale=1.0, scalar=0.0,
                                         op0=ALU.mult, op1=ALU.add, accum_out=nr[:, 5:6]).then_inc(S("w_sum"), 1)
                dve.wait_ge(S("w_sum"), i + 1)
                dve.tensor_scalar(wall[:, ds(i, 1)], nr[:, 5:6], br[:, 0:1], None, ALU.add).then_inc(S("w_ready"), 1)
                dve.wait_ge(S("w_ready"), i + 1)

            def ffn_out(i):
                dve.wait_ge(S("y_psum"), i + 1)
                dve.tensor_tensor(tmp[:, :], bank[7][:, 0:D], b2f[:, :], ALU.add).then_inc(S("y_read"), 1)
                dve.wait_ge(S("y_read"), i + 1)
                dve.tensor_scalar(side[:, ds(i * D, D)], tmp[:, :], wall[:, ds(i, 1)], None, ALU.mult).then_inc(S("y_ready"), 1)
                dve.wait_ge(S("y_ready"), i + 1)

            def stage(i, here, before1, before2, before3):
                if here:
                    dve.sem_inc(S("dve_tick"), 1)
                    lo, mid, hi = pair_ranges(dve, i)
                    bucket(2 * i, lo, mid)
                if before1:
                    post_a(i - 1)
                if here:
                    bucket(2 * i + 1, mid, hi)
                if before3:
                    ffn_out(i - 3)
                if before1:
                    post_b(i - 1)

            step(dve.tensor_scalar(att_neg[:, :, :], att9[:, :].rearrange("p (a b) -> p b a", a=3), -1.0 / 12.0, None, ALU.mult))
            step(dve.memset(const_1_5[:, :], 1.5))
            dve.sem_inc(S("sel_ready"), 2)
            pipeline(dve, stage)

            dve.wait_ge(S("w_masked"), 1)
            wb = wall[:, :].bitcast(I32)
            step(dve.tensor_scalar(keyi[:, 0, :], wb, 31, -2147483648, ALU.arith_shift_right, ALU.bitwise_or))
            step(dve.tensor_tensor(keyi[:, 1, :], wb, keyi[:, 0, :], ALU.bitwise_xor))
            step(dve.tensor_scalar(keyi[:, 2, :], keyi[:, 1, :], 16, None, ALU.logical_shift_right), False)
            step(dve.tensor_scalar(keyi[:, 3, :], keyi[:, 1, :], 65535, None, ALU.bitwise_and), False)
            step(dve.tensor_copy(iota15[:, :], iota_b[:, 1:16]))
            step(dve.tensor_copy(keyf[:, 0, :], keyi[:, 2, :]), False)
            step(dve.tensor_copy(keyf[:, 1, :], keyi[:, 3, :]), False)
            step(dve.memset(thr[:, :, :], 0.0))
            rounds = 0
            for part in range(2):
                key = keyf[:, 0 if part == 0 else 2, :]
                for r in range(4):
                    unit = float(16 ** (3 - r))
                    step(dve.tensor_scalar(cand[:, :], iota15[:, :], unit, thr[:, part, r:r + 1], ALU.mult, ALU.add))
                    step(dve.tensor_tensor(cmpb[:, :, :], key.unsqueeze(1).to_broadcast([P, 15, T]),
                                           cand[:, :].unsqueeze(2).to_broadcast([P, 15, T]), ALU.is_ge))
                    dve.tensor_reduce(cnt[:, :], cmpb[:, :, :], AX.X, ALU.add).then_inc(S("cnt_ready"), 1)
                    rounds += 1
                    dve.wait_ge(S("cnt_total"), rounds)
                    step(dve.tensor_scalar(kc[:, 0:15], bank[0][:, 0:15], float(KEEP), None, ALU.is_ge))
                    step(dve.tensor_reduce(kc[:, 15:16], kc[:, 0:15], AX.X, ALU.add))
                    step(dve.tensor_scalar(thr[:, part, r + 1:r + 2], kc[:, 15:16], unit, thr[:, part, r:r + 1], ALU.mult, ALU.add))
                if part == 0:
                    t = thr[:, 0, 4:5]
                    step(dve.tensor_scalar(keyf[:, 3, :], keyf[:, 0, :], t, 131072.0, ALU.is_gt, ALU.mult), False)
                    step(dve.tensor_scalar(keyf[:, 2, :], keyf[:, 0, :], t, None, ALU.is_equal))
                    step(dve.tensor_scalar(keyf[:, 1, :], keyf[:, 1, :], 1.0, None, ALU.add))
                    step(dve.tensor_tensor(keyf[:, 1, :], keyf[:, 1, :], keyf[:, 2, :], ALU.mult))
                    step(dve.tensor_tensor(keyf[:, 2, :], keyf[:, 1, :], keyf[:, 3, :], ALU.add))
                    step(dve.tensor_scalar(keyf[:, 2, :], keyf[:, 2, :], -1.0, None, ALU.add))
            t = thr[:, 1, 4:5]
            step(dve.tensor_scalar(mask[:, :], keyf[:, 2, :], t, None, ALU.is_gt), False)
            step(dve.tensor_scalar(keyf[:, 0, :], keyf[:, 2, :], t, None, ALU.is_equal), False)
            step(dve.tensor_scalar(eqb[:, :], keyf[:, 2, :], t, None, ALU.is_equal))
            step(dve.tensor_reduce(kc[:, 0:1], mask[:, :], AX.X, ALU.add))
            dve.tensor_scalar(kc[:, 1:2], kc[:, 0:1], 1.0, None, ALU.mult).then_inc(S("eq_ready"), 1)
            dve.wait_ge(S("eq_done"), 1)
            step(dve.tensor_copy(keyf[:, 1, :], bank[0][:, 128:128 + T]))
            step(dve.tensor_tensor_scan(keyf[:, 3, :], keyf[:, 1, :], ones_f[:, 0:T], 0.0, ALU.add, ALU.mult))
            step(dve.tensor_tensor(keyf[:, 3, :], keyf[:, 3, :], keyf[:, 1, :], ALU.subtract))
            step(dve.tensor_tensor(keyf[:, 3, :], keyf[:, 3, :], bank[0][:, 64:64 + T], ALU.add))
            step(dve.tensor_scalar(keyf[:, 3, :], keyf[:, 3, :], bank[0][:, 200:201], float(KEEP), ALU.add, ALU.is_lt))
            step(dve.tensor_tensor(keyf[:, 3, :], keyf[:, 3, :], keyf[:, 0, :], ALU.mult))
            step(dve.tensor_tensor(mask[:, :], mask[:, :], keyf[:, 3, :], ALU.add))
            with dve.Fori(0, T) as i:
                dve.scalar_tensor_tensor(base[:, ds(i * D, D)], side[:, ds(i * D, D)], mask[:, ds(i, 1)],
                                         base[:, ds(i * D, D)], ALU.mult, ALU.add).then_inc(S("out_ready"), 1)

        @block.scalar
        def _(act):
            def dense_ln(q, par):
                i = 2 * q + par
                act.wait_ge(S("ln_var"), i + 1)
                act.activation(sd[:, 1:2], sd[:, 0:1], ACT.Sqrt).then_inc(S("ln_sd"), 1)
                act.wait_ge(S("xt_done"), i + 1)
                act.activation(xt[:, par, :, :].rearrange("p k n -> p (k n)"), psT[par], ACT.Copy).then_inc(S("xt_ready"), 1)
                act.wait_ge(S("kv_psum"), i + 1)
                wait(act, S("kv_ss"), i)
                act.activation(sq[:, :], bank[3 + par][:, :], ACT.Square).then_inc(S("kv_sq"), 1)
                act.wait_ge(S("kv_var"), i + 1)
                act.activation(kvs[:, 2, :], kvs[:, 1, :], ACT.Sqrt).then_inc(S("kv_sd"), 1)

            def mix(q, par):
                i = 2 * q + par
                act.wait_ge(S("mxt_done"), i + 1)
                act.activation(xt[:, par, :, :].rearrange("p k n -> p (k n)"), psT[par], ACT.Copy).then_inc(S("mxt_ready"), 1)
                act.wait_ge(S("h_psum"), i + 1)
                for f in range(KD):
                    act.activation(ht[:, par, f, :], bank[3][:, par * D + f * P:par * D + (f + 1) * P], ACT.Gelu,
                                   bias=b1p[:, f:f + 1]).then_inc(S("h_ready"), 1)
                act.wait_ge(S("mlp_psum"), i + 1)
                mp = bank[4 + par][:, 0:D]
                wait(act, S("l3_sum"), i - 1)
                act.activation(side[:, ds(i * D, D)], mp, ACT.Relu)
                act.activation(ml[:, par, :], mp, ACT.Relu).then_inc(S("mlp_ready"), 1)

            each_tile(act, dense_ln)
            act.wait_ge(S("w1p_ready"), 1)
            each_tile(act, mix)

            def stage(i, here, before1, before2, before3):
                if before2:
                    act.wait_ge(S("xt_psum"), i - 1)
                    act.activation(x2t[:, :, :].rearrange("p k n -> p (k n)"), bank[6][:, 0:D], ACT.Copy).then_inc(S("x2t_ready"), 1)
                if here:
                    act.wait_ge(S("acc_a"), i + 1)
                    act.activation(agg[:, 0, :], bank[0][:, 0:D], ACT.Copy).then_inc(S("agg_a"), 1)
                if before1:
                    act.wait_ge(S("lg_ready"), i)
                    act.activation(sg[:, 0, :], lg[:, :], ACT.Tanh, scale=0.5).then_inc(S("sig_tanh"), 1)
                    act.wait_ge(S("att_in"), i)
                    act.activation(sg[:, 6, :], sg[:, 3, :], ACT.Tanh, bias=sg[:, 5, 0:1], scale=-1.0).then_inc(S("att_tanh"), 1)
                    act.wait_ge(S("x1_guess"), i)
                    y = nri[:, 1:2].bitcast(F32)
                    for r in range(3):
                        act.activation(nr[:, 2:3], y, ACT.Square).then_inc(S("newton"), 1)
                        act.wait_ge(S("newton"), 8 * (i - 1) + 3 * r + 1)
                        act.activation(nr[:, 3:4], nr[:, 2:3], ACT.Identity, bias=const_1_5[:, 0:1], scale=nr[:, 1:2]).then_inc(S("newton"), 1)
                        act.wait_ge(S("newton"), 8 * (i - 1) + 3 * r + 2)
                        o = nr[:, (4, 6, 4)[r]:(5, 7, 5)[r]]
                        act.activation(o, nr[:, 3:4], ACT.Copy, scale=y).then_inc(S("newton" if r < 2 else "x1_rs"), 1)
                        if r < 2:
                            act.wait_ge(S("newton"), 8 * (i - 1) + 3 * r + 3)
                        y = o
                if before2:
                    act.wait_ge(S("f1_psum"), i - 1)
                    for f in range(KF):
                        act.activation(fh[:, f, :], bank[4 + f // 4][:, (f % 4) * P:(f % 4 + 1) * P], ACT.Gelu_apprx_tanh,
                                       bias=b1f[:, f:f + 1]).then_inc(S("fh_ready"), 1)
                if here:
                    act.wait_ge(S("acc_b"), i + 1)
                    act.activation(agg[:, 1, :], bank[1][:, 0:D], ACT.Copy).then_inc(S("agg_b"), 1)
                    act.wait_ge(S("at_psum"), i + 1)
                    for k in range(KD):
                        ins = act.activation(aggt[:, k, :, :].rearrange("p v (h n) -> p v h n", h=2),
                                             bank[2][:, k * D:(k + 1) * D].rearrange("p (h v n) -> p v h n", h=2, v=2), ACT.Copy)
                    ins.then_inc(S("aggt_ready"), 1)
                    act.wait_ge(S("lh_psum"), i + 1)
                    wait(act, S("lh_used"), i)
                    act.activation(lh[:, :], bank[3][:, :], ACT.Relu).then_inc(S("lh_ready"), 1)

            pipeline(act, stage)

        @block.tensor
        def _(pe):
            def mm(out_, lhsT, rhs, start, stop, **kw):
                return pe.matmul(out_, lhsT, rhs, start=start, stop=stop, **kw)

            M = H1 * HALF
            pe.wait_ge(S("digits_ready"), 2 * HALF)
            mm(bank[7][0:M, 0:HALF * H2], oh1[:, 0:M], oh2[:, 0:HALF * H2], True, False, skip_group_check=True)
            with pe.Fori(1, SLOTS // HALF) as g:
                mm(bank[7][0:M, 0:HALF * H2], oh1[:, ds(g * M, M)], oh2[:, ds(g * (HALF * H2), HALF * H2)], False, False, skip_group_check=True)
            mm(bank[7][0:M, 0:HALF * H2], zero_b[:, 0:M], zero_b[:, 0:HALF * H2], False, True, skip_group_check=True).then_inc(S("hist_done"), 1)
            pe.wait_ge(S("hist_expanded"), 1)
            mm(bank[6][:, 0:H1 * H2], ones_f[0:M, :], hexp[0:M, :, :].rearrange("p a b -> p (a b)"), True, True).then_inc(S("counts_ready"), 1)
            pe.wait_ge(S("starts_ready"), 1)
            for r in range(2):
                mm(R[r], ones_f[0:1, :], starts[0:1, 0:NB], True, False, skip_group_check=True)
            pe.wait_ge(S("wkv_ready"), 1)
            mm(bank[5][:, 0:D], zero_b[:, 0:P], zero_b[:, :], True, False, skip_group_check=True)

            def rank(g, hf):
                tile0 = (2 * g + hf) * HALF
                o = [oh[:, hf, j, :] for j in range(HALF)]

                def add(r, w, j):
                    return mm(R[r], w[:, :], o[j], False, False, skip_group_check=True)

                pe.wait_ge(S(f"oh_ready{hf}"), g + 1)
                for j in range(HALF):
                    if j >= 2:
                        pe.wait_ge(S("rank_read"), tile0 + j - 1)
                        add(j % 2, notbefore, j - 2)
                    if j >= 1:
                        add(j % 2, ones_b, j - 1)
                    add(j % 2, before, j).then_inc(S("rank_ready"), 1)
                pe.wait_ge(S("rank_read"), tile0 + HALF - 1)
                add(0, notbefore, HALF - 2)
                add(0, ones_b, HALF - 1)
                pe.wait_ge(S("rank_read"), tile0 + HALF)
                add(1, notbefore, HALF - 1).then_inc(S(f"oh_used{hf}"), 1)

            def dense_kv(q, par):
                i = 2 * q + par
                n = TAIL if last(q) else P
                pe.wait_ge(S("xn_ready"), i + 1)
                for k in range(KD):
                    ins = pe.transpose(psT[par][:, k * P:(k + 1) * P], xs[:, par, k * P:(k + 1) * P], ident[:, :])
                ins.then_inc(S("xt_done"), 1)
                pe.wait_ge(S("xt_ready"), i + 1)
                wait(pe, S("kv_scaled"), i - 1)
                kv = bank[3 + par][:, :]
                mm(kv, ones_f[0:1, :], bkv[:, :], True, False)
                for k in range(KD):
                    ins = mm(kv, xt[:, par, k, :], wkv[:, k, :], False, k == KD - 1)
                ins.then_inc(S("kv_psum"), 1)

            def add_kv(q, par):
                i = 2 * q + par
                n = TAIL if last(q) else P
                pe.wait_ge(S("kn_ready"), i + 1)
                for j in range(KD):
                    ins = mm(bank[5][:, j * P:(j + 1) * P], kn[0:n, par, 0, j * P:(j + 1) * P], kn[0:n, par, 1, j * P:(j + 1) * P],
                             False, False, skip_group_check=True)
                ins.then_inc(S("kv_added"), 1)

            def mix(q, par):
                i = 2 * q + par
                pe.wait_ge(S(f"mix_loaded{par}"), 32 * q + 32)
                for k in range(KD):
                    ins = pe.transpose(psT[par][:, k * P:(k + 1) * P], xs[:, par, k * P:(k + 1) * P], ident[:, :])
                ins.then_inc(S("mxt_done"), 1)
                pe.wait_ge(S("mxt_ready"), i + 1)
                wait(pe, S("h_ready"), 2 * i - 2)
                for f in range(KD):
                    for k in range(KD):
                        ins = mm(bank[3][:, par * D + f * P:par * D + (f + 1) * P], w1p[:, k, f * P:(f + 1) * P], xt[:, par, k, :],
                                 k == 0, k == KD - 1)
                ins.then_inc(S("h_psum"), 1)
                wait(pe, S("mlp_ready"), i - 1)
                for k in range(KD):
                    ins = mm(bank[4 + par][:, 0:D], xt[:, par, k, :], wmlp[:, k, :], k == 0, k == KD - 1)
                ins.then_inc(S("mlp_psum"), 1)
                wait(pe, S("mix_read"), i - 1)
                mm(bank[6 + par][:, 0:D], ones_f[0:1, :], b2m[:, :], True, False)
                pe.wait_ge(S("h_ready"), 2 * i + 2)
                for f in range(KD):
                    ins = mm(bank[6 + par][:, 0:D], ht[:, par, f, :], w2m[:, f, :], False, f == KD - 1)
                ins.then_inc(S("mix_psum"), 1)

            def loop1(q):
                rank(q, 0)
                dense_kv(q, 0)
                add_kv(q, 0)
                rank(q, 1)
                if not last(q):
                    dense_kv(q, 1)
                    add_kv(q, 1)

            loop1(0)
            with pe.Fori(1, Q) as q:
                loop1(q)
            loop1(Q)
            mm(bank[5][:, 0:D], zero_b[:, 0:P], zero_b[:, :], False, True, skip_group_check=True).then_inc(S("kv_summed"), 1)

            for j in range(KD):
                for k in range(KD):
                    ins = pe.transpose(bank[6][:, j * D + k * P:j * D + (k + 1) * P], wq[:, k, j * P:(j + 1) * P], ident[:, :])
            ins.then_inc(S("wq_transposed"), 1)
            pe.wait_ge(S("wqt_ready"), 1)
            for j in range(KD):
                mm(bank[7][:, j * D:(j + 1) * D], kvbd[:, j, :], wqt[:, j, :], True, True)
            pe.wait_ge(S("w_loaded"), 16 * 23)
            for j in range(KD):
                ins = mm(bank[3][:, j:j + 1], kvbd[:, j, :], bq[:, j:j + 1], True, True)
            ins.then_inc(S("at_done"), 1)
            pe.wait_ge(S("at_ready"), 1)
            for k in range(KD):
                for j in range(KD):
                    mm(bank[6][:, k * D:(k + 1) * D], atm[:, j, k * P:(k + 1) * P], w1m[:, j, :], j == 0, j == KD - 1)
            for f in range(KD):
                for j in range(KD):
                    ins = mm(bank[3][:, 8 + f:9 + f], w1m[:, j, f * P:(f + 1) * P], bp[:, j:j + 1], j == 0, j == KD - 1)
            ins.then_inc(S("w1p_done"), 1)
            pe.wait_ge(S("w1p_ready"), 1)

            def loop2(q):
                rank(Q + 1 + q, 0)
                mix(q, 0)
                rank(Q + 1 + q, 1)
                if not last(q):
                    mix(q, 1)

            loop2(0)
            with pe.Fori(1, Q) as q:
                loop2(q)
            loop2(Q)
            for g in (SORTS - 2, SORTS - 1):
                rank(g, 0)
                rank(g, 1)

            pe.wait_ge(S("ptab_ready"), 1)
            pe.wait_ge(S("ffn_loaded"), 32)
            pe.wait_ge(S("rank_read"), SLOTS)

            def sum_pair(b, pair, k, acc):
                ready = pe.snap(2 * (pair + b) + 2)
                at = (pair % (GR // 2)) * (2 * D)
                gathered = [gring[:, :, :].rearrange("p s d -> p (s d)")[:, ds(at + j * D, D)] for j in range(2)]
                for j in range(2):
                    pe.wait_ge(S("sel_ready"), ready + j + 1)
                    mm(acc[:, 0:D], msel[:, 2 * k + j, :], gathered[j], False, False, skip_group_check=True).then_inc(S("sel_used"), 1)

            def bucket(b, lo, hi, acc, done):
                mm(acc[:, 0:D], zero_b[:, 0:P], zero_b[:, :], True, False, skip_group_check=True)
                bucket_pairs(pe, lo, hi, lambda pair, k, first: sum_pair(b, pair, k, acc))
                mm(acc[:, 0:D], zero_b[:, 0:P], zero_b[:, :], False, True, skip_group_check=True).then_inc(S(done), 1)

            def stage(i, here, before1, before2, before3):
                if here:
                    lo, mid, hi = pair_ranges(pe, i)
                    wait(pe, S("agg_a"), i)
                    bucket(2 * i, lo, mid, bank[0], "acc_a")
                if before3:
                    wait(pe, S("y_read"), i - 3)
                    pe.wait_ge(S("fh_ready"), (i - 2) * KF)
                    for f in range(KF):
                        ins = mm(bank[7][:, 0:D], fh[:, f, :], w2f[:, f, :], f == 0, f == KF - 1)
                    ins.then_inc(S("y_psum"), 1)
                if before2:
                    pe.wait_ge(S("x2t_ready"), i - 1)
                    for f in range(KF):
                        for k in range(KD):
                            ins = mm(bank[4 + f // 4][:, (f % 4) * P:(f % 4 + 1) * P], w1f[:, k, f * P:(f + 1) * P], x2t[:, k, :],
                                     k == 0, k == KD - 1)
                    ins.then_inc(S("f1_psum"), 1)
                if here:
                    wait(pe, S("agg_b"), i)
                    bucket(2 * i + 1, mid, hi, bank[1], "acc_b")
                    pe.wait_ge(S("agg_b"), i + 1)
                    for k in range(KD):
                        for h in range(2):
                            ins = pe.transpose(bank[2][:, k * D + h * P:k * D + (h + 1) * P], agg[:, h, k * P:(k + 1) * P], ident[:, :])
                    ins.then_inc(S("at_psum"), 1)
                    pe.wait_ge(S("aggt_ready"), i + 1)
                    wait(pe, S("lh_ready"), i)
                    for v, w in enumerate((wlow, whigh)):
                        for k in range(KD):
                            ins = mm(bank[3][:, v * D:(v + 1) * D], aggt[:, k, v, :], w[:, k, :], k == 0, k == KD - 1)
                    ins.then_inc(S("lh_psum"), 1)
                if before1:
                    pe.wait_ge(S("x2_ready"), i)
                    for k in range(KD):
                        ins = pe.transpose(bank[6][:, k * P:(k + 1) * P], x2n[:, k * P:(k + 1) * P], ident[:, :])
                    ins.then_inc(S("xt_psum"), 1)

            pe.sem_inc(S("sel_used"), 2)
            pipeline(pe, stage)

            for r in range(8):
                pe.wait_ge(S("cnt_ready"), r + 1)
                mm(bank[0][:, 0:15], ones_f[:, :], cnt[:, :], True, True).then_inc(S("cnt_total"), 1)
            pe.wait_ge(S("eq_ready"), 1)
            mm(bank[0][:, 64:64 + T], before[:, :], eqb[:, :], True, True)
            mm(bank[0][:, 128:128 + T], ones_b[:, :], eqb[:, :], True, True)
            mm(bank[0][:, 200:201], ones_f[:, :], kc[:, 1:2], True, True).then_inc(S("eq_done"), 1)


_INS = ["x", "src", "dst", "edge_weight", "edge_weight_n2",
        "L0_gnn_weight_low", "L0_gnn_weight_high", "L0_gnn_weight_mlp",
        "L0_gnn_att_vec_low", "L0_gnn_att_vec_high", "L0_gnn_att_vec_mlp", "L0_gnn_att_vec",
        "L0_mix_w_qkv", "L0_mix_b_qkv", "L0_mix_kln_g", "L0_mix_kln_b", "L0_mix_vln_g", "L0_mix_vln_b",
        "L0_mix_w1", "L0_mix_b1", "L0_mix_w2", "L0_mix_b2",
        "L0_ffn_wr", "L0_ffn_br", "L0_ffn_w1", "L0_ffn_b1", "L0_ffn_w2", "L0_ffn_b2"]


def kernel(**inputs):
    import numpy as np
    import concourse.bacc as bacc
    from concourse.bass_utils import run_bass_kernel_spmd

    nc = bacc.Bacc("TRN2", target_bir_lowering=False, num_devices=1)
    arrays, args = {}, {}
    for name in _INS:
        v = np.ascontiguousarray(inputs[name])
        arrays[f"in_{name}"] = v
        args[name] = nc.dram_tensor(f"in_{name}", v.shape, mybir.dt.from_np(v.dtype), kind="ExternalInput").ap()
    out = nc.dram_tensor("out_0", inputs["x"].shape, F32, kind="ExternalOutput").ap()
    build(nc, args, out)
    r = run_bass_kernel_spmd(nc, [arrays], core_ids=[0])
    return r.results[0]["out_0"]
```

```python
from contextlib import ExitStack

import concourse.bass as bass
from concourse import mybir

F32 = mybir.dt.float32
I32 = mybir.dt.int32
BF16 = mybir.dt.bfloat16
ALU = mybir.AluOpType
ACT = mybir.ActivationFunctionType
AX = mybir.AxisListType

P = 128
BK = 64
HALF = 8
H1, H2 = 13, 8
GR = 16
RR = 32
EPS = 1e-5
SENTINEL = -3.0e38


def ds(start, size):
    return bass.ds(start, size)


def wait(eng, sem, value):
    if isinstance(value, int) and value <= 0:
        return
    eng.wait_ge(sem, value)


def build(nc, a, out):
    N, D = a["x"].shape
    E = a["src"].shape[0]
    HID = a["L0_ffn_w1"].shape[1]
    T = -(-N // P)
    TAIL = N - (T - 1) * P
    NB = 2 * T
    KD = D // P
    KF = HID // P
    HEADS, HC = 8, 32
    SLOTS = -(-E // (P * 2 * HALF)) * 2 * HALF
    FULL = E // P
    REST = E - FULL * P
    HALVES = SLOTS // HALF
    SORTS = SLOTS // (2 * HALF)
    PAIRS = SLOTS // 2
    PBITS = (PAIRS - 1).bit_length()
    LEAD = 2
    MIX0 = LEAD + T + 2
    NG = SLOTS // HALF
    KEEP = max(1, int(0.5 * N)) - 1
    Q = T // 2
    assert D == 256 and HID == 1024 and T % 2 == 1 and NB < H1 * H2 and HALVES == 2 * T + 6
    assert HALVES % 8 == 0 and SLOTS % RR == 0 and FULL < SLOTS

    xn_dram = nc.dram_tensor("xn_rows", (N, D), F32).ap()
    rec_dram = nc.dram_tensor("sorted_records", (SLOTS * P, 4), F32).ap()

    with ExitStack() as ctx:
        sems = {}

        def S(name):
            if name not in sems:
                sems[name] = ctx.enter_context(nc.semaphore(name))
            return sems[name]

        def sb(name, shape, dt=F32):
            return ctx.enter_context(nc.sbuf_tensor(name, shape, dt))

        arena_a = sb("arena", [P, 12 * 1024 + 1024])
        arena_at = {}

        def carve(phase, name, shape, dt=F32):
            width = 1
            for n in shape[1:]:
                width *= n
            at = arena_at.get(phase, 0)
            arena_at[phase] = at + width
            assert at + width <= arena_a.shape[1], (phase, name, at + width)
            flat = arena_a[0:shape[0], at:at + width]
            if len(shape) == 2:
                return flat
            names = "abc"[:len(shape) - 1]
            return flat.rearrange(f"p ({' '.join(names)}) -> p {' '.join(names)}", **dict(zip(names, shape[1:])))

        rec = sb("rec", [P, SLOTS, 4])
        bkt = sb("bkt", [P, SLOTS], BF16)
        base = sb("base", [P, T * D])
        side = sb("side", [P, T * D])
        iota_nodes = sb("iota_nodes", [P, T * P], mybir.dt.uint16)
        raw = base[:, 0:4 * SLOTS].rearrange("p (a t) -> p a t", a=4)
        digit = base[:, 4 * SLOTS:8 * SLOTS].rearrange("p (a t) -> p a t", a=4)
        n1, n2 = SLOTS * H1, SLOTS * H2
        oh1 = side[:, 0:n1 // 2].bitcast(BF16)
        oh2 = base[:, 8 * SLOTS:8 * SLOTS + n2 // 2].bitcast(BF16)
        assert 8 * SLOTS + n2 // 2 <= T * D and n1 // 2 <= T * D

        ident = sb("ident", [P, P])
        ones_f = sb("ones_f", [P, P])
        ones_b = sb("ones_b", [P, P], BF16)
        earlier = sb("earlier", [P, HALF, HALF], BF16)
        before = sb("before", [P, P], BF16)
        notbefore = sb("notbefore", [P, P], BF16)
        zero_b = sb("zero_b", [P, D + 2 * KD], BF16)
        iota_b = sb("iota_b", [P, H1 * H2], BF16)
        iota15 = sb("iota15", [P, 15])
        ramp = sb("ramp", [P, H1 * H2], I32)
        jmask = sb("jmask", [P, HALF])
        hmask = sb("hmask", [P, H1])

        wqkv = carve("first", "wqkv", [P, KD, 3 * D])
        wq = carve("first", "wq", [P, KD, D])
        wkv = carve("first", "wkv", [P, KD, 2 * D])
        wmean = sb("wmean", [P, 2 * KD * HEADS])
        bqkv = carve("first", "bqkv", [P, 3 * D])
        bkv = carve("first", "bkv", [P, 2 * D])
        bkv3 = carve("first", "bkv3", [P, D]).bitcast(BF16)
        b2m3 = carve("first", "b2m3", [P, D // 2]).bitcast(BF16)
        bmean = sb("bmean", [P, 2 * HEADS])
        bq = sb("bq", [P, KD])
        gam_v = sb("gam_v", [P, HC])
        bet_v = sb("bet_v", [P, HC])
        gam_k = sb("gam_k", [P, 1])
        bet_k = sb("bet_k", [P, 1])
        w1m = carve("first", "w1m", [P, KD, D])
        w2m = carve("first", "w2m", [P, KD, D])
        b1m = sb("b1m", [P, KD])
        b2m = carve("first", "b2m", [P, D])
        wmlp = carve("first", "wmlp", [P, KD, D])
        wlow = sb("wlow", [P, KD, D])
        whigh = sb("whigh", [P, KD, D])
        att_rows = sb("att_rows", [P, 3, D])
        att9 = sb("att9", [P, 9])
        wr = sb("wr", [P, D])
        br = sb("br", [P, 1])
        w1f = carve("second", "w1f", [P, KD, HID])
        w2f = carve("second", "w2f", [P, KF, D])
        b1f = sb("b1f", [P, KF])
        b2f3 = sb("b2f3", [P, D], BF16)

        oh = sb("oh", [P, 2, HALF, NB], BF16)
        junk = sb("junk", [P, HALF, NB], BF16)
        pos = sb("pos", [P, 2, HALF])
        ibits = sb("ibits", [P, 6, HALF], I32)
        same = sb("same", [P, 2, HALF, HALF], BF16)
        tied = sb("tied", [P, HALF])
        idx = sb("idx", [P, 2, HALF], I32)
        rstage = sb("rstage", [P, 2, HALF, 4])
        hsel = sb("hsel", [P, HALF, H2])
        hcnt = sb("hcnt", [P, H2])
        hexp = sb("hexp", [P, H1, H2])
        counts = sb("counts", [P, H1 * H2])
        incl = sb("incl", [P, H1 * H2])
        starts = sb("starts", [P, H1 * H2])
        pclip = sb("pclip", [1, H1 * H2])
        pint = sb("pint", [1, H1 * H2], I32)
        ptab = sb("ptab", [1, H1 * H2], I32)
        pparts = sb("pparts", [1, 3, T], I32)
        packed = sb("packed", [1, T], I32)

        xl = carve("first", "xl", [P, 2, D])
        xs = carve("first", "xs", [P, 2, D])
        st6 = sb("st6", [P, 6])
        mv = sb("mv", [P, 2])
        sd = sb("sd", [P, 2])
        xt = carve("first", "xt", [P, 2, KD, P])
        kv_sum = sb("kv_sum", [P, 2 * KD])
        kv_row = sb("kv_row", [P, 2 * KD])
        fold = carve("first", "fold", [P, 2, KD, P])
        sq = carve("first", "sq", [P, 2 * D])
        kvs = sb("kvs", [P, 3, 2 * HEADS])
        kn = carve("first", "kn", [P, 2, 2, D])
        kvbd = carve("first", "kvbd", [P, KD, P])
        wqt = carve("first", "wqt", [P, KD, D])
        atm = carve("first", "atm", [P, KD, D])
        w1p = carve("first", "w1p", [P, KD, D])
        bp = sb("bp", [P, KD])
        b1p = sb("b1p", [P, KD])
        ht = carve("first", "ht", [P, 2, KD, P])
        ml = carve("first", "ml", [P, 2, D])
        tmp = sb("tmp", [P, D])
        lg = sb("lg", [P, 3])
        lgc = sb("lgc", [P, 3])
        l3 = sb("l3", [P, T])

        gring = carve("second", "gring", [P, GR, D])
        rring = sb("rring", [P, RR, 4])
        msel = carve("second", "msel", [P, 4, P])
        cur = sb("cur", [P, 2, 2, 4])
        here_nodes = sb("here_nodes", [P, 2, BK])
        agg = carve("second", "agg", [P, 2, D])
        aggt = carve("second", "aggt", [P, KD, 2, P])
        lh = carve("second", "lh", [P, 2 * D])
        sg = sb("sg", [P, 8, 3])
        x1 = carve("second", "x1", [P, D])
        x2n = carve("second", "x2n", [P, D])
        x2t = carve("second", "x2t", [P, KD, P])
        nr = sb("nr", [P, 8])
        nri = sb("nri", [P, 2], I32)
        const_1_5 = sb("const_1_5", [P, 1])
        lg_prod = carve("second", "lg_prod", [P, 2, D])
        att_neg = sb("att_neg", [P, 3, 3])
        att_prod = sb("att_prod", [P, 3, 3])
        fh = carve("second", "fh", [P, KF, P])
        wall = sb("wall", [P, T])
        ybuf = sb("ybuf", [P, D])
        keyi = sb("keyi", [P, 4, T], I32)
        keyf = sb("keyf", [P, 4, T])
        cand = sb("cand", [P, 15])
        cmpb = carve("second", "cmpb", [P, 15, T])
        cnt = sb("cnt", [P, 15])
        kc = sb("kc", [P, 16])
        thr = sb("thr", [P, 2, 5])
        eqb = sb("eqb", [P, T], BF16)
        mask = sb("mask", [P, T])

        bank = [ctx.enter_context(nc.psum_tensor(f"bank{i}", [P, 512], F32)) for i in range(8)]
        psT = [bank[2][:, 0:256], bank[2][:, 256:512]]
        R = bank[0][:, 0:NB]

        block = ctx.enter_context(nc.Block())

        def each_tile(eng, body, first_peeled=True):
            body(0, 0)
            body(0, 1)
            with eng.Fori(1, Q) as q:
                body(q, 0)
                body(q, 1)
            body(Q, 0)

        def pair_ranges(eng, i):
            v = eng.value_load(packed[0:1, ds(i, 1)], min_val=0, max_val=2 ** (3 * PBITS) - 1)
            one = 2 ** PBITS
            return [eng.snap(e, min_val=0, max_val=PAIRS - 1) for e in (v % one, (v // one) % one, v // (one * one))]

        def bucket_pairs(eng, lo, hi, body):
            body(lo, 0, True)
            more = eng.snap(hi - lo, min_val=0, max_val=PAIRS - 1)
            twos = eng.snap(more // 2, min_val=0, max_val=PAIRS // 2)
            with eng.If(twos > 0):
                with eng.Fori(0, twos) as t:
                    body(lo + 2 * t + 1, 1, False)
                    body(lo + 2 * t + 2, 0, False)
            with eng.If(more % 2 > 0):
                body(hi, 1, False)

        def pipeline(eng, stage):
            stage(0, True, False, False, False)
            stage(1, True, True, False, False)
            stage(2, True, True, True, False)
            with eng.Fori(3, T) as i:
                stage(i, True, True, True, True)
            stage(T, False, True, True, True)
            stage(T + 1, False, False, True, True)
            stage(T + 2, False, False, False, True)

        def rows(dram, i, n=P):
            return dram[ds(i * P, n), :] if not isinstance(i, int) else dram[i * P:i * P + n, :]

        def last(q):
            return isinstance(q, int) and q == Q

        @block.sync
        def _(sp):
            sp.wait_ge(S("raw_padded"), 4)
            for k, name in enumerate(("src", "dst", "edge_weight", "edge_weight_n2")):
                v = a[name]
                dst = raw[:, k, :] if k > 1 else raw[:, k, :].bitcast(I32)
                with nc.allow_non_contiguous_dma(reason="the few edges beyond whole columns"):
                    sp.dma_start(dst[:, 0:FULL], v[0:FULL * P].rearrange("(p t) -> p t", p=P)).then_inc(S("raw_loaded"), 16)
                    sp.dma_start(dst[0:REST, FULL:FULL + 1], v[FULL * P:E].rearrange("(p t) -> p t", t=1)).then_inc(S("raw_loaded"), 16)
            sp.dma_start(wqkv[:, :, :], a["L0_mix_w_qkv"].rearrange("(k p) n -> p k n", p=P)).then_inc(S("qkv_loaded"), 16)
            sp.dma_start(bqkv[:, :], a["L0_mix_b_qkv"].rearrange("(o n) -> o n", o=1).to_broadcast([P, 3 * D])).then_inc(S("qkv_loaded"), 16)

            def load_x(q, par):
                i = 2 * q + par
                wait(sp, S("xn_ready"), i - 1)
                n = TAIL if last(q) else P
                if last(q):
                    sp.wait_ge(S("tail_zeroed"), 1)
                sp.dma_start(xl[0:n, par, :], rows(a["x"], i, n)).then_inc(S(f"x_loaded{par}"), 16)

            def store_xn(q, par):
                i = 2 * q + par
                n = TAIL if last(q) else P
                sp.wait_ge(S("xn_ready"), i + 1)
                sp.dma_start(rows(xn_dram, i, n), xs[0:n, par, :]).then_inc(S(f"xn_stored{par}"), 16)

            load_x(0, 0)
            load_x(0, 1)
            store_xn(0, 0)
            load_x(1, 0)
            store_xn(0, 1)
            load_x(1, 1)
            with sp.Fori(1, Q - 1) as q:
                store_xn(q, 0)
                load_x(q + 1, 0)
                store_xn(q, 1)
                load_x(q + 1, 1)
            store_xn(Q - 1, 0)
            load_x(Q, 0)
            store_xn(Q - 1, 1)
            store_xn(Q, 0)

            cols = dict(reason="biases by partition")
            big = [(w1m, "L0_mix_w1"), (w2m, "L0_mix_w2"), (wmlp, "L0_gnn_weight_mlp"),
                   (wlow, "L0_gnn_weight_low"), (whigh, "L0_gnn_weight_high")]
            for t, name in big:
                sp.dma_start(t[:, :, :], a[name].rearrange("(k p) n -> p k n", p=P)).then_inc(S("w_loaded"), 16)
            for k, name in enumerate(("L0_gnn_att_vec_low", "L0_gnn_att_vec_high", "L0_gnn_att_vec_mlp")):
                sp.dma_start(att_rows[:, k, :], a[name].rearrange("d o -> o d").to_broadcast([P, D])).then_inc(S("w_loaded"), 16)
            sp.dma_start(wr[:, :], a["L0_ffn_wr"].rearrange("d o -> o d").to_broadcast([P, D])).then_inc(S("w_loaded"), 16)
            sp.dma_start(br[:, :], a["L0_ffn_br"].rearrange("(o n) -> o n", o=1).to_broadcast([P, 1])).then_inc(S("w_loaded"), 16)
            sp.dma_start(att9[:, :], a["L0_gnn_att_vec"].rearrange("(o a) b -> o (a b)", o=1).to_broadcast([P, 9])).then_inc(S("w_loaded"), 16)
            sp.dma_start(b2m[:, :], a["L0_mix_b2"].rearrange("(o n) -> o n", o=1).to_broadcast([P, D])).then_inc(S("w_loaded"), 16)
            for r, t in ((a["L0_mix_vln_g"], gam_v), (a["L0_mix_vln_b"], bet_v)):
                sp.dma_start(t[:, :], r.rearrange("(o n) -> o n", o=1).to_broadcast([P, HC])).then_inc(S("w_loaded"), 16)
            with nc.allow_non_contiguous_dma(**cols):
                sp.dma_start(b1m[:, :], a["L0_mix_b1"].rearrange("(k p) -> p k", p=P)).then_inc(S("w_loaded"), 16)
                sp.dma_start(b1f[:, :], a["L0_ffn_b1"].rearrange("(k p) -> p k", p=P)).then_inc(S("w_loaded"), 16)
                for hh in range(P // HC):
                    for r, t in ((a["L0_mix_kln_g"], gam_k), (a["L0_mix_kln_b"], bet_k)):
                        sp.dma_start(t[hh * HC:(hh + 1) * HC, :], r.rearrange("(p o) -> p o", o=1)).then_inc(S("w_loaded"), 16)
                for h in range(HEADS):
                    j, hh = h // 4, h % 4
                    sp.dma_start(bq[hh * HC:hh * HC + HC, j:j + 1],
                                 a["L0_mix_b_qkv"][h * 3 * HC:h * 3 * HC + HC].rearrange("(p o) -> p o", o=1)).then_inc(S("w_loaded"), 16)

            sp.wait_ge(S("xn_stored0"), 16 * (Q + 1))
            sp.wait_ge(S("xn_stored1"), 16 * Q)

            def load_mix(q, par):
                i = 2 * q + par
                wait(sp, S("mix_read"), i - 1)
                n = TAIL if last(q) else P
                if isinstance(q, int) and q == 0:
                    sp.wait_ge(S("kv_summed"), 1)
                sp.dma_start(xs[0:n, par, :], rows(xn_dram, i, n)).then_inc(S(f"mix_loaded{par}"), 16)
                sp.dma_start(xl[0:n, par, :], rows(a["x"], i, n)).then_inc(S(f"mix_loaded{par}"), 16)

            each_tile(sp, load_mix)

            sp.wait_ge(S("mix_read"), T)
            sp.wait_ge(S("l3_ready"), T)
            for t, name in ((w1f, "L0_ffn_w1"), (w2f, "L0_ffn_w2")):
                sp.dma_start(t[:, :, :], a[name].rearrange("(k p) n -> p k n", p=P)).then_inc(S("ffn_loaded"), 16)
            sp.dma_start(x1[:, :], a["L0_ffn_b2"].rearrange("(o n) -> o n", o=1).to_broadcast([P, D])).then_inc(S("b2f_loaded"), 16)

            for hf in range(2):
                sp.wait_ge(S(f"scattered{hf}"), 16 * HALF * SORTS)

            def load_records(group, ring):
                src = rec_dram[ds(group * (P * HALF), P * HALF), :] if not isinstance(group, int) else \
                    rec_dram[group * P * HALF:(group + 1) * P * HALF, :]
                sp.dma_start(rring[:, ring * HALF:(ring + 1) * HALF, :].rearrange("p s f -> p (s f)"),
                             src.rearrange("(p s) f -> p (s f)", p=P)).then_inc(S(f"records{ring}"), 16)

            for r in range(4):
                load_records(r, r)

            def relay(kk, u):
                k = 2 * kk + u
                for j in range(GR):
                    sp.wait_ge(S(f"gathered{j}"), 16 * k + 16)
                    sp.sem_inc(S("g_ready"), 1)
                    if j == GR // 2 - 1 and not (isinstance(k, int) and k in (0, NG // 2 - 1)):
                        sp.wait_ge(S("pair_free"), 8 * k + 1)
                        for v in range(2):
                            load_records(2 * k + 2 + v, 2 * (1 - u) + v)

            relay(0, 0)
            relay(0, 1)
            with sp.Fori(1, SLOTS // RR - 1) as kk:
                relay(kk, 0)
                relay(kk, 1)
            relay(SLOTS // RR - 1, 0)
            relay(SLOTS // RR - 1, 1)

            for g in range(T // 7):
                sp.wait_ge(S("out_ready"), 7 * (g + 1))
                t0, t1 = 7 * g, 7 * (g + 1)
                full = min(t1, T - 1)
                sp.dma_start(out[t0 * P:full * P, :].rearrange("(t p) d -> p t d", p=P),
                             base[:, t0 * D:full * D].rearrange("p (t d) -> p t d", d=D)).then_inc(S("out_stored"), 16)
            sp.dma_start(out[(T - 1) * P:N, :], base[0:TAIL, (T - 1) * D:T * D]).then_inc(S("out_stored"), 16)
            sp.wait_ge(S("out_stored"), 16 * (T // 7 + 1))

        @block.gpsimd
        def _(pool):
            def const(ins):
                ins.then_inc(S("const"), 1)

            pool.memset(raw[:, 0, :].bitcast(I32)[:, FULL:SLOTS], N - 1).then_inc(S("raw_padded"), 1)
            pool.memset(raw[:, 1, :].bitcast(I32)[:, FULL:SLOTS], 0).then_inc(S("raw_padded"), 1)
            pool.memset(raw[:, 2:4, FULL:SLOTS], 0.0).then_inc(S("raw_padded"), 1)
            pool.iota(ramp[:, :], pattern=[[1, H1 * H2]], base=0, channel_multiplier=0).then_inc(S("raw_padded"), 1)
            const(pool.memset(ident[:, :], 0.0))
            const(pool.memset(ones_f[:, :], 1.0))
            const(pool.memset(ones_b[:, :], 1.0))
            const(pool.memset(before[:, :], 1.0))
            const(pool.memset(notbefore[:, :], 1.0))
            const(pool.memset(zero_b[:, :], 0.0))
            const(pool.memset(hmask[:, :], 1.0))
            const(pool.iota(ibits[:, 0, :], pattern=[[-1, HALF]], base=HALF * P, channel_multiplier=1))
            const(pool.iota(ibits[:, 1, :], pattern=[[1, HALF]], base=1, channel_multiplier=0))
            const(pool.iota(ibits[:, 2, :], pattern=[[1, HALF]], base=1 + HALF, channel_multiplier=0))
            pool.wait_ge(S("const"), 10)
            const(pool.affine_select(out=ident[:, :], in_=ident[:, :], compare_op=ALU.not_equal, fill=1.0,
                                     base=0, pattern=[[-1, P]], channel_multiplier=1))
            const(pool.affine_select(out=before[:, :], in_=before[:, :], compare_op=ALU.is_ge, fill=0.0,
                                     base=-1, pattern=[[1, P]], channel_multiplier=-1))
            const(pool.affine_select(out=notbefore[:, :], in_=notbefore[:, :], compare_op=ALU.is_ge, fill=0.0,
                                     base=0, pattern=[[-1, P]], channel_multiplier=1))
            const(pool.affine_select(out=hmask[:, :], in_=hmask[:, :], compare_op=ALU.is_ge, fill=0.0,
                                     base=0, pattern=[[-HALF, H1]], channel_multiplier=1))
            pool.wait_ge(S("const"), 14)
            const(pool.affine_select(out=hmask[:, :], in_=hmask[:, :], compare_op=ALU.is_ge, fill=0.0,
                                     base=HALF - 1, pattern=[[HALF, H1]], channel_multiplier=-1))
            pool.iota(iota_nodes[:, :], pattern=[[1, T * P]], base=0, channel_multiplier=0,
                      allow_small_or_imprecise_dtypes=True).then_inc(S("nodes_ready"), 1)

            def scatter(g, hf):
                pool.wait_ge(S(f"idx_ready{hf}"), 2 * g + 2)
                pool.sem_inc(S("pool_tick"), 1)
                for j in range(HALF):
                    pool.indirect_dma_start(
                        rec_dram, bass.IndirectOffsetOnAxis(ap=idx[:, hf, j:j + 1], axis=0),
                        rstage[:, hf, j, :], None).then_inc(S(f"scattered{hf}"), 16)

            with pool.Fori(0, SORTS) as g:
                scatter(g, 0)
                scatter(g, 1)

            pool.wait_ge(S("xn_stored0"), 16 * (Q + 1))
            pool.wait_ge(S("xn_stored1"), 16 * Q)
            pool.wait_ge(S("mix_read"), T)
            pool.wait_ge(S("l3_ready"), T)

            def gather(kk):
                for v in range(RR):
                    if v % HALF == 0:
                        pool.wait_ge(S(f"records{v // HALF}"), 16 * kk + 16)
                        pool.sem_inc(S("pool_tick"), 1)
                    free = 16 * kk + v // 2 - GR // 2 + 2
                    if v % 2 == 0 and not (isinstance(free, int) and free <= 1):
                        pool.wait_ge(S("pair_free"), free)
                        pool.sem_inc(S("pool_tick"), 1)
                    pool.indirect_dma_start(
                        gring[:, v % GR, :], None, xn_dram,
                        bass.IndirectOffsetOnAxis(ap=rring[:, v, 1:2].bitcast(I32), axis=0)).then_inc(S(f"gathered{v % GR}"), 16)

            gather(0)
            with pool.Fori(1, SLOTS // RR) as kk:
                gather(kk)

            pool.wait_ge(S("y_ready"), T)
            pool.affine_select(out=wall[:, T - 1:T], in_=wall[:, T - 1:T], compare_op=ALU.is_ge, fill=SENTINEL,
                               base=TAIL - 1, pattern=[[0, 1]], channel_multiplier=-1).then_inc(S("w_masked"), 1)

        @block.vector
        def _(dve):
            chain = [0]

            def step(ins, do_wait=True):
                chain[0] += 1
                ins.then_inc(S("dve_step"), 1)
                if do_wait:
                    dve.wait_ge(S("dve_step"), chain[0])

            dve.wait_ge(S("raw_padded"), 4)
            dve.wait_ge(S("const"), 15)
            dve.wait_ge(S("raw_loaded"), 16 * 8)
            src_i = raw[:, 0, :].bitcast(I32)
            dig_i = [digit[:, k, :].bitcast(I32) for k in range(3)]
            step(dve.tensor_scalar(dig_i[0], src_i, 6, None, ALU.logical_shift_right), False)
            step(dve.tensor_scalar(dig_i[1], src_i, 9, None, ALU.logical_shift_right), False)
            step(dve.tensor_scalar(dig_i[2], src_i, 6, H2 - 1, ALU.logical_shift_right, ALU.bitwise_and), False)
            step(dve.tensor_copy(iota_b[:, :], ramp[:, :]))
            h12 = digit[:, 3, :].bitcast(BF16).rearrange("p (a t) -> p a t", a=2)
            step(dve.tensor_copy(h12[:, 0, :], dig_i[1]), False)
            step(dve.tensor_copy(h12[:, 1, :], dig_i[2]))
            for k, (o, w) in enumerate(((oh1, H1), (oh2, H2))):
                ov = o.rearrange("p (g h j) -> p g h j", h=w, j=HALF)
                for v in range(w):
                    dve.tensor_scalar(ov[:, :, v, :], h12[:, k, :].rearrange("p (g j) -> p g j", j=HALF), float(v), None,
                                      ALU.is_equal).then_inc(S("digits_ready"), 1)
            step(dve.tensor_copy(bkt[:, :], dig_i[0]), False)
            step(dve.tensor_copy(rec[:, :, 0], src_i), False)
            step(dve.tensor_copy(rec[:, :, 1], raw[:, 1, :]), False)
            step(dve.tensor_copy(rec[:, :, 2], raw[:, 2, :]), False)
            step(dve.tensor_copy(rec[:, :, 3], raw[:, 3, :]), False)
            step(dve.tensor_scalar(ibits[:, 3, :], ibits[:, 0, :], HALF - 1, None, ALU.bitwise_and))
            step(dve.tensor_scalar(jmask[:, :], ibits[:, 3, :], 0.0, None, ALU.is_equal))

            M = H1 * HALF
            dve.wait_ge(S("hist_done"), 1)
            step(dve.tensor_tensor(hsel[0:M, :, :], bank[7][0:M, 0:HALF * H2].rearrange("p (h j) -> p j h", j=HALF),
                                   jmask[0:M, :].unsqueeze(2).to_broadcast([M, HALF, H2]), ALU.mult))
            step(dve.tensor_reduce(hcnt[0:M, :], hsel[0:M, :, :].rearrange("p j h -> p h j"), AX.X, ALU.add))
            dve.tensor_tensor(hexp[0:M, :, :], hcnt[0:M, :].unsqueeze(1).to_broadcast([M, H1, H2]),
                              hmask[0:M, :].unsqueeze(2).to_broadcast([M, H1, H2]), ALU.mult).then_inc(S("hist_expanded"), 1)
            dve.wait_ge(S("counts_ready"), 1)
            step(dve.tensor_copy(counts[:, :], bank[6][:, 0:H1 * H2]))
            step(dve.tensor_tensor_scan(incl[:, :], counts[:, :], ones_f[:, 0:H1 * H2], 0.0, ALU.add, ALU.mult))
            dve.tensor_tensor(starts[:, :], incl[:, :], counts[:, :], ALU.subtract).then_inc(S("starts_ready"), 1)
            dve.wait_ge(S("starts_ready"), 1)
            step(dve.tensor_scalar(pclip[:, :], starts[0:1, :], float(SLOTS * P - 1), None, ALU.min))
            step(dve.tensor_copy(pint[:, :], pclip[:, :]))
            step(dve.tensor_scalar(ptab[:, :], pint[:, :], 8, None, ALU.logical_shift_right))
            for k in range(3):
                part = ptab[:, k:k + 2 * T].rearrange("p (t u) -> p t u", u=2)[:, :, 0]
                step(dve.tensor_scalar(pparts[:, k, :], part, PBITS * k, None, ALU.logical_shift_left))
            step(dve.tensor_tensor(packed[:, :], pparts[:, 0, :], pparts[:, 1, :], ALU.bitwise_or))
            dve.tensor_tensor(packed[:, :], packed[:, :], pparts[:, 2, :], ALU.bitwise_or).then_inc(S("ptab_ready"), 1)

            def one_hot(h, hf):
                wait(dve, S("oh_used"), h - 1)
                dve.tensor_tensor(oh[:, hf, :, :], bkt[:, ds(h * HALF, HALF)].unsqueeze(2).to_broadcast([P, HALF, NB]),
                                  iota_b[:, 0:NB].unsqueeze(1).to_broadcast([P, HALF, NB]), ALU.is_equal).then_inc(S("oh_ready"), 1)

            def read_rank(h, hf, j0, j1):
                dve.wait_ge(S("oh_ready"), h + 1)
                dve.wait_ge(S("rank_ready"), h + 1)
                for j in range(j0, j1):
                    ins = dve.tensor_tensor_reduce(out=junk[:, j, :], in0=R, in1=oh[:, hf, j, :], scale=1.0, scalar=0.0,
                                                   op0=ALU.mult, op1=ALU.add, accum_out=pos[:, hf, j:j + 1])
                ins.then_inc(S("rank_read"), 1)

            def find_ties(h):
                b = bkt[:, ds(h * HALF, HALF)]
                dve.tensor_tensor(same[:, 0, :, :], b.unsqueeze(2).to_broadcast([P, HALF, HALF]),
                                  b.unsqueeze(1).to_broadcast([P, HALF, HALF]), ALU.is_equal).then_inc(S("idx_step"), 1)
                dve.wait_ge(S("idx_step"), 6 * h + 1)
                dve.tensor_tensor(same[:, 1, :, :], same[:, 0, :, :], earlier[:, :, :], ALU.mult).then_inc(S("idx_step"), 1)
                dve.wait_ge(S("idx_step"), 6 * h + 2)
                dve.tensor_reduce(tied[:, :], same[:, 1, :, :], AX.X, ALU.add).then_inc(S("idx_step"), 1)

            def place(h, hf, k):
                dve.wait_ge(S("rank_read"), 2 * h + 2)
                dve.wait_ge(S("idx_step"), 6 * h + 3)
                dve.tensor_tensor(ibits[:, 0, :], pos[:, hf, :], tied[:, :], ALU.add).then_inc(S("idx_step"), 1)
                wait(dve, S(f"scattered{hf}"), 16 * HALF * k)
                dve.tensor_copy(rstage[:, hf, :, :].rearrange("p j f -> p (j f)"),
                                rec[:, :, :].rearrange("p t f -> p (t f)")[:, ds(h * (HALF * 4), HALF * 4)]).then_inc(S(f"idx_ready{hf}"), 1)
                dve.wait_ge(S("idx_step"), 6 * h + 4)
                dve.tensor_scalar(ibits[:, 1, :], ibits[:, 0, :], 10, 10, ALU.logical_shift_right, ALU.logical_shift_left)
                dve.tensor_scalar(ibits[:, 2, :], ibits[:, 0, :], P - 1, 3, ALU.bitwise_and, ALU.logical_shift_left)
                dve.tensor_scalar(ibits[:, 3, :], ibits[:, 0, :], 7, HALF - 1, ALU.logical_shift_right, ALU.bitwise_and).then_inc(S("idx_step"), 1)
                dve.wait_ge(S("idx_step"), 6 * h + 5)
                dve.tensor_tensor(ibits[:, 4, :], ibits[:, 1, :], ibits[:, 2, :], ALU.bitwise_or).then_inc(S("idx_step"), 1)
                dve.wait_ge(S("idx_step"), 6 * h + 6)
                dve.tensor_tensor(idx[:, hf, :], ibits[:, 4, :], ibits[:, 3, :], ALU.bitwise_or).then_inc(S(f"idx_ready{hf}"), 1)

            def rank(h, more=True):
                read_rank(h, h % 2, 0, HALF // 2)
                read_rank(h, h % 2, HALF // 2, HALF)
                if more:
                    one_hot(h + 1, 1 - h % 2)
                find_ties(h)
                place(h, h % 2, h // 2)

            step(dve.tensor_tensor(earlier[:, :, :], iota_b[:, 0:HALF].unsqueeze(2).to_broadcast([P, HALF, HALF]),
                                   iota_b[:, 0:HALF].unsqueeze(1).to_broadcast([P, HALF, HALF]), ALU.is_gt))
            one_hot(0, 0)
            for h in range(LEAD):
                rank(h)

            def three_parts(rows3, v, rest, part):
                step(dve.memset(rows3, 0.0))
                for k in range(3):
                    step(dve.tensor_copy(rows3[32 * k:32 * k + 1, :], v[32 * k:32 * k + 1, :]))
                    if k < 2:
                        step(dve.tensor_copy(part, v))
                        step(dve.tensor_tensor(rest, v, part, ALU.subtract))
                        v = rest

            dve.wait_ge(S("qkv_loaded"), 32)
            for k in range(KD):
                wv = wqkv[:, k, :].rearrange("p (h s c) -> p h s c", h=HEADS, s=3)[:, :, 1:3, :]
                mk = wmean[:, k * 16:(k + 1) * 16].rearrange("p (h s) -> p h s", s=2)
                step(dve.tensor_reduce(mk, wv, AX.X, ALU.add))
                step(dve.tensor_scalar(mk, mk, 1.0 / HC, None, ALU.mult))
                step(dve.tensor_tensor(wkv[:, k, :].rearrange("p (h s c) -> p h s c", h=HEADS, s=2), wv,
                                       mk.unsqueeze(3).to_broadcast([P, HEADS, 2, HC]), ALU.subtract), False)
                step(dve.tensor_copy(wq[:, k, :].rearrange("p (h c) -> p h c", h=HEADS),
                                     wqkv[:, k, :].rearrange("p (h s c) -> p h s c", h=HEADS, s=3)[:, :, 0, :]), False)
            bv = bqkv[:, :].rearrange("p (h s c) -> p h s c", h=HEADS, s=3)[:, :, 1:3, :]
            bm = bmean[:, :].rearrange("p (h s) -> p h s", s=2)
            step(dve.tensor_reduce(bm, bv, AX.X, ALU.add))
            step(dve.tensor_scalar(bm, bm, 1.0 / HC, None, ALU.mult))
            step(dve.tensor_tensor(bkv[:, :].rearrange("p (h s c) -> p h s c", h=HEADS, s=2), bv,
                                   bm.unsqueeze(3).to_broadcast([P, HEADS, 2, HC]), ALU.subtract))
            three_parts(bkv3[:, :], bkv[:, :], sq[:, :], kn[:, 0, 0, :].bitcast(BF16))
            dve.memset(kvbd[:, :, :], 0.0).then_inc(S("wkv_ready"), 1)

            def scale_kv(i, par):
                dve.wait_ge(S("kv_rs"), i + 1)
                wait(dve, S("kv_added"), i - 1)
                dve.tensor_tensor(kn[:, par, :, :].rearrange("p s (h c) -> p h s c", h=HEADS),
                                  bank[3 + par][:, :].rearrange("p (h s c) -> p h s c", h=HEADS, s=2),
                                  kvs[:, 0, :].rearrange("p (h s) -> p h s", s=2).unsqueeze(3).to_broadcast([P, HEADS, 2, HC]),
                                  ALU.mult).then_inc(S("kn_ready"), 1)

            def kv_squares(i):
                dve.wait_ge(S("kv_sq"), i + 1)
                wait(dve, S("kn_ready"), i)
                dve.tensor_reduce(kvs[:, 0, :], sq[:, :].rearrange("p (g c) -> p g c", c=HC), AX.X, ALU.add).then_inc(S("kv_ss"), 1)

            def kv_variance(i):
                dve.wait_ge(S("kv_ss"), i + 1)
                dve.tensor_scalar(kvs[:, 1, :], kvs[:, 0, :], 1.0 / HC, EPS, ALU.mult, ALU.add).then_inc(S("kv_var"), 1)

            def kv_inverse(i):
                dve.wait_ge(S("kv_sd"), i + 1)
                dve.reciprocal(kvs[:, 0, :], kvs[:, 2, :]).then_inc(S("kv_rs"), 1)

            def normalise(q, par):
                i = 2 * q + par
                h = LEAD + i
                first = isinstance(i, int) and i == 0
                if last(q):
                    dve.wait_ge(S("xn_ready"), i)
                    dve.memset(xl[:, par, :], 0.0).then_inc(S("tail_zeroed"), 1)
                dve.wait_ge(S(f"x_loaded{par}"), 16 * q + 16)
                dve.bn_stats(st6[:, :], xl[:, par, :]).then_inc(S("ln_stats"), 1)
                read_rank(h, par, 0, HALF // 2)
                dve.wait_ge(S("ln_stats"), i + 1)
                dve.sem_inc(S("dve_tick"), 1)
                dve.bn_aggr(mv[:, :], st6[:, :]).then_inc(S("ln_aggr"), 1)
                dve.wait_ge(S("ln_aggr"), i + 1)
                dve.tensor_scalar(sd[:, 0:1], mv[:, 1:2], EPS, None, ALU.add).then_inc(S("ln_var"), 1)
                read_rank(h, par, HALF // 2, HALF)
                dve.wait_ge(S("ln_sd"), i + 1)
                dve.reciprocal(sd[:, 0:1], sd[:, 1:2]).then_inc(S("ln_rs"), 1)
                dve.wait_ge(S("ln_rs"), i + 1)
                if not (isinstance(q, int) and q == 0):
                    dve.wait_ge(S(f"xn_stored{par}"), 16 * q)
                    dve.wait_ge(S("xt_done"), i - 1)
                dve.tensor_scalar(xs[:, par, :], xl[:, par, :], mv[:, 0:1], sd[:, 0:1], ALU.subtract, ALU.mult).then_inc(S("xn_ready"), 1)
                one_hot(h + 1, 1 - par)
                find_ties(h)
                if not first:
                    kv_squares(i - 1)
                    kv_variance(i - 1)
                place(h, par, q + LEAD // 2)
                if not first:
                    kv_inverse(i - 1)
                    scale_kv(i - 1, 1 - par)

            def mix_out(i, q, par):
                dve.wait_ge(S(f"mix_loaded{par}"), 32 * q + 32)
                dve.tensor_tensor(tmp[:, :], xl[:, par, :], xs[:, par, :], ALU.add).then_inc(S("mix_sum"), 1)
                dve.wait_ge(S("mlp_ready"), i + 1)
                dve.tensor_tensor_reduce(out=ybuf[:, :], in0=ml[:, par, :], in1=att_rows[:, 2, :], scale=1.0, scalar=0.0,
                                         op0=ALU.mult, op1=ALU.add, accum_out=lg[:, 2:3]).then_inc(S("l3_sum"), 1)
                dve.wait_ge(S("mix_sum"), i + 1)
                dve.wait_ge(S("mix_psum"), i + 1)
                dve.tensor_tensor(base[:, ds(i * D, D)], tmp[:, :], bank[6 + par][:, 0:D], ALU.add).then_inc(S("mix_read"), 1)
                dve.wait_ge(S("l3_sum"), i + 1)
                dve.tensor_copy(l3[:, ds(i, 1)], lg[:, 2:3]).then_inc(S("l3_ready"), 1)
                dve.wait_ge(S("l3_ready"), i + 1)

            each_tile(dve, normalise)
            kv_squares(T - 1)
            kv_variance(T - 1)
            kv_inverse(T - 1)
            scale_kv(T - 1, 0)

            dve.wait_ge(S("w_loaded"), 16 * 32)
            dve.wait_ge(S("kv_summed"), 1)
            three_parts(b2m3[:, :], b2m[:, :], sq[:, 0:D], kn[:, 0, 0, 0:D // 2].bitcast(BF16))
            step(dve.tensor_copy(kv_sum[:, :], bank[5][:, D:D + 2 * KD]))
            for j in range(KD):
                step(dve.tensor_scalar(fold[:, 1, j, :], ident[:, :], kv_sum[:, KD + j:KD + j + 1], None, ALU.mult), False)
            dve.memset(kv_row[:, :], 0.0).then_inc(S("v_sum_diag"), 1)
            f4 = fold[:, :, :, :].rearrange("p a j (h c) -> p a (j h) c", c=HC)
            nh = KD * P // HC
            gv = gam_v[:, :].unsqueeze(1).to_broadcast([P, nh, HC])
            bv1 = bet_v[:, :].unsqueeze(1).to_broadcast([P, P // HC, HC])
            step(dve.tensor_tensor(f4[:, 0], bank[5][:, 0:D].rearrange("p (g c) -> p g c", c=HC), gv, ALU.mult))
            step(dve.tensor_scalar(fold[:, 0, :, :], fold[:, 0, :, :], gam_k[:, 0:1], None, ALU.mult), False)
            dve.wait_ge(S("v_sum_diag"), 1)
            step(dve.tensor_scalar(kv_row[:, KD:2 * KD], bet_k[:, 0:1].to_broadcast([P, KD]), float(N), None, ALU.mult))
            step(dve.scalar_tensor_tensor(kv_row[:, 0:KD], kv_sum[:, 0:KD], gam_k[:, 0:1], kv_row[:, KD:2 * KD], ALU.mult, ALU.add))
            for j in range(KD):
                blk = fold[:, 0, j, :].rearrange("p (h c) -> p h c", c=HC)
                step(dve.scalar_tensor_tensor(blk, bv1, kv_row[:, j:j + 1], blk, ALU.mult, ALU.add))
            dve.wait_ge(S("v_sum_rows"), 1)
            step(dve.tensor_tensor(f4[:, 1], bank[4][:, 0:D].rearrange("p (g c) -> p g c", c=HC), gv, ALU.mult))
            step(dve.scalar_tensor_tensor(fold[:, 0, :, :], fold[:, 1, :, :], bet_k[:, 0:1], fold[:, 0, :, :], ALU.mult, ALU.add))
            for j in range(KD):
                for hh in range(P // HC):
                    s = slice(hh * HC, (hh + 1) * HC)
                    step(dve.tensor_scalar(kvbd[s, j, s], fold[s, 0, j, s], 1.0 / N, None, ALU.mult), False)
            dve.wait_ge(S("dve_step"), chain[0])
            dve.wait_ge(S("wq_transposed"), 1)
            dve.tensor_copy(wqt[:, :, :].rearrange("p j c -> p (j c)"), bank[6][:, :]).then_inc(S("wqt_ready"), 1)
            rank(LEAD + T)
            dve.wait_ge(S("at_done"), 1)
            step(dve.tensor_copy(atm[:, :, :].rearrange("p j c -> p (j c)"), bank[7][:, :]), False)
            step(dve.tensor_copy(bp[:, :], bank[3][:, 0:KD]))
            for j in range(KD):
                step(dve.tensor_tensor(atm[:, j, j * P:(j + 1) * P], atm[:, j, j * P:(j + 1) * P], ident[:, :], ALU.add))
            dve.memset(nr[:, :], 0.0).then_inc(S("at_ready"), 1)
            rank(LEAD + T + 1)
            dve.wait_ge(S("w1p_done"), 1)
            step(dve.tensor_copy(w1p[:, :, :].rearrange("p j c -> p (j c)"), bank[6][:, :]), False)
            step(dve.tensor_tensor(b1p[:, :], bank[3][:, 8:8 + KD], b1m[:, :], ALU.add))
            dve.memset(nr[:, 0:1], 0.0).then_inc(S("w1p_ready"), 1)

            def sort_and_mix(q, par):
                i = 2 * q + par
                h = MIX0 + i
                hf = (MIX0 + par) % 2
                read_rank(h, hf, 0, HALF // 2)
                read_rank(h, hf, HALF // 2, HALF)
                one_hot(h + 1, 1 - hf)
                find_ties(h)
                place(h, hf, q + (MIX0 + par) // 2)
                if not (isinstance(i, int) and i == 0):
                    mix_out(i - 1, q if par == 1 else q - 1, 1 - par)

            each_tile(dve, sort_and_mix)
            mix_out(T - 1, Q, 0)
            for h in range(MIX0 + T, HALVES):
                rank(h, more=h < HALVES - 1)

            dve.wait_ge(S("ptab_ready"), 1)
            dve.wait_ge(S("nodes_ready"), 1)

            def select(b, pair, k, first):
                it = dve.snap(pair + b)
                gathered = dve.snap(2 * pair + 2)
                at = (pair % (RR // 2)) * 8
                free = dve.snap(2 * it + 2 if first else 2 * it)
                copied = dve.snap(it + 1)
                dve.wait_ge(S("g_ready"), gathered)
                dve.wait_ge(S("sel_ready"), free)
                dve.tensor_copy(cur[:, k, :, :].rearrange("p s f -> p (s f)"),
                                rring[:, :, :].rearrange("p s f -> p (s f)")[:, ds(at, 8)]).then_inc(S("rec_copied"), 1)
                dve.wait_ge(S("rec_copied"), copied)
                dve.wait_ge(S("sel_used"), free)
                for j in range(2):
                    dve.scalar_tensor_tensor(msel[:, 2 * k + j, :].rearrange("p (v n) -> p v n", v=2), here_nodes[:, :, :],
                                             cur[:, k, j, 0:1], cur[:, k, j, 2:4].unsqueeze(2).to_broadcast([P, 2, BK]),
                                             ALU.is_equal, ALU.mult).then_inc(S("sel_ready"), 1)
                if not first:
                    dve.sem_inc(S("pair_free"), 1)

            def bucket(b, lo, hi):
                if not (isinstance(b, int) and b == 0):
                    dve.wait_ge(S("sel_ready"), 2 * (lo + b) + 2)
                dve.tensor_copy(here_nodes[:, :, :], iota_nodes[:, ds(b * BK, BK)].unsqueeze(1).to_broadcast([P, 2, BK])).then_inc(S("nodes_set"), 1)
                dve.wait_ge(S("nodes_set"), b + 1)
                bucket_pairs(dve, lo, hi, lambda pair, k, first: select(b, pair, k, first))

            def post_a(i):
                n0 = 13 * i

                def nxt(ins, k):
                    ins.then_inc(S("pa"), 1)
                    dve.wait_ge(S("pa"), n0 + k)

                dve.tensor_copy(lg[:, 2:3], l3[:, ds(i, 1)])
                dve.wait_ge(S("lh_ready"), i + 1)
                for k in range(2):
                    ins = dve.tensor_tensor_reduce(out=lg_prod[:, k, :], in0=lh[:, k * D:(k + 1) * D], in1=att_rows[:, k, :], scale=1.0,
                                                   scalar=0.0, op0=ALU.mult, op1=ALU.add, accum_out=lg[:, k:k + 1])
                ins.then_inc(S("lg_ready"), 1)
                dve.wait_ge(S("sig_tanh"), i + 1)
                nxt(dve.scalar_tensor_tensor(att_prod[:, :, :], sg[:, 0, :].unsqueeze(1).to_broadcast([P, 3, 3]), 1.0, att_neg[:, :, :],
                                             ALU.add, ALU.mult), 1)
                nxt(dve.tensor_reduce(sg[:, 3, :], att_prod[:, :, :], AX.X, ALU.add), 2)
                dve.tensor_reduce(sg[:, 5, 0:1], sg[:, 3, :], AX.X, ALU.min).then_inc(S("att_in"), 1)
                dve.wait_ge(S("att_tanh"), i + 1)
                dve.tensor_scalar(sg[:, 1, :], sg[:, 6, :], 1.0, None, ALU.add)
                nxt(dve.tensor_scalar(sg[:, 2, :], sg[:, 6, :], -1.0, 1.0, ALU.mult, ALU.add), 3)
                nxt(dve.reciprocal(sg[:, 0, :], sg[:, 2, :]), 4)
                nxt(dve.tensor_tensor_reduce(out=sg[:, 4, :], in0=sg[:, 0, :], in1=sg[:, 1, :], scale=1.0, scalar=0.0,
                                             op0=ALU.mult, op1=ALU.add, accum_out=sg[:, 7, 0:1]), 5)
                nxt(dve.reciprocal(sg[:, 7, 1:2], sg[:, 7, 0:1]), 6)
                nxt(dve.tensor_scalar(sg[:, 1, :], sg[:, 4, :], sg[:, 7, 1:2], 3.0, ALU.mult, ALU.mult), 7)
                nxt(dve.scalar_tensor_tensor(x1[:, :], lh[:, 0:D], sg[:, 1, 0:1], base[:, ds(i * D, D)], ALU.mult, ALU.add), 8)
                dve.scalar_tensor_tensor(ybuf[:, :], lh[:, D:2 * D], sg[:, 1, 1:2], x1[:, :], ALU.mult, ALU.add).then_inc(S("lh_used"), 1)
                dve.wait_ge(S("lh_used"), i + 1)
                nxt(dve.scalar_tensor_tensor(x1[:, :], side[:, ds(i * D, D)], sg[:, 1, 2:3], ybuf[:, :], ALU.mult, ALU.add), 9)
                nxt(dve.bn_stats(st6[:, :], x1[:, :]), 10)
                dve.sem_inc(S("dve_tick"), 1)
                nxt(dve.bn_aggr(mv[:, :], st6[:, :]), 11)
                dve.tensor_scalar(nr[:, 1:2], mv[:, 1:2], EPS, -0.5, ALU.add, ALU.mult)
                nxt(dve.tensor_scalar(nr[:, 0:1], mv[:, 1:2], EPS, None, ALU.add), 12)
                nxt(dve.tensor_scalar(nri[:, 0:1], nr[:, 0:1].bitcast(I32), 1, None, ALU.logical_shift_right), 13)
                dve.tensor_scalar(nri[:, 1:2], nri[:, 0:1], -1.0, float(0x5F3759DF), ALU.mult, ALU.add).then_inc(S("x1_guess"), 1)

            def post_b(i):
                dve.wait_ge(S("x1_rs"), i + 1)
                wait(dve, S("xt_psum"), i)
                dve.tensor_scalar(x2n[:, :], x1[:, :], mv[:, 0:1], nr[:, 4:5], ALU.subtract, ALU.mult).then_inc(S("x2_ready"), 1)
                dve.wait_ge(S("x2_ready"), i + 1)
                dve.tensor_tensor(base[:, ds(i * D, D)], x1[:, :], x2n[:, :], ALU.add)
                dve.tensor_tensor_reduce(out=ybuf[:, :], in0=x2n[:, :], in1=wr[:, :], scale=1.0, scalar=0.0,
                                         op0=ALU.mult, op1=ALU.add, accum_out=nr[:, 5:6]).then_inc(S("w_sum"), 1)
                dve.wait_ge(S("w_sum"), i + 1)
                dve.tensor_scalar(wall[:, ds(i, 1)], nr[:, 5:6], br[:, 0:1], None, ALU.add).then_inc(S("w_ready"), 1)
                dve.wait_ge(S("w_ready"), i + 1)

            def stage(i, here, before1, before2, before3):
                if here:
                    dve.sem_inc(S("dve_tick"), 1)
                    lo, mid, hi = pair_ranges(dve, i)
                if before2:
                    post_b(i - 2)
                if here:
                    bucket(2 * i, lo, mid)
                if before1:
                    post_a(i - 1)
                if here:
                    bucket(2 * i + 1, mid, hi)

            dve.wait_ge(S("b2f_loaded"), 16)
            three_parts(b2f3[:, :], x1[:, :], x2n[:, :], ybuf[:, 0:D // 2].bitcast(BF16))
            dve.sem_inc(S("b2f_ready"), 1)
            step(dve.tensor_scalar(att_neg[:, :, :], att9[:, :].rearrange("p (a b) -> p b a", a=3), -1.0 / 12.0, None, ALU.mult))
            step(dve.memset(const_1_5[:, :], 1.5))
            dve.sem_inc(S("sel_ready"), 2)
            pipeline(dve, stage)

            dve.wait_ge(S("w_masked"), 1)
            dve.wait_ge(S("y_ready"), T)
            wb = wall[:, :].bitcast(I32)
            step(dve.tensor_scalar(keyi[:, 0, :], wb, 31, -2147483648, ALU.arith_shift_right, ALU.bitwise_or))
            step(dve.tensor_tensor(keyi[:, 1, :], wb, keyi[:, 0, :], ALU.bitwise_xor))
            step(dve.tensor_scalar(keyi[:, 2, :], keyi[:, 1, :], 16, None, ALU.logical_shift_right), False)
            step(dve.tensor_scalar(keyi[:, 3, :], keyi[:, 1, :], 65535, None, ALU.bitwise_and), False)
            step(dve.tensor_copy(iota15[:, :], iota_b[:, 1:16]))
            step(dve.tensor_copy(keyf[:, 0, :], keyi[:, 2, :]), False)
            step(dve.tensor_copy(keyf[:, 1, :], keyi[:, 3, :]), False)
            step(dve.memset(thr[:, :, :], 0.0))
            rounds = 0
            for part in range(2):
                key = keyf[:, 0 if part == 0 else 2, :]
                for r in range(4):
                    unit = float(16 ** (3 - r))
                    step(dve.tensor_scalar(cand[:, :], iota15[:, :], unit, thr[:, part, r:r + 1], ALU.mult, ALU.add))
                    step(dve.tensor_tensor(cmpb[:, :, :], key.unsqueeze(1).to_broadcast([P, 15, T]),
                                           cand[:, :].unsqueeze(2).to_broadcast([P, 15, T]), ALU.is_ge))
                    dve.tensor_reduce(cnt[:, :], cmpb[:, :, :], AX.X, ALU.add).then_inc(S("cnt_ready"), 1)
                    rounds += 1
                    dve.wait_ge(S("cnt_total"), rounds)
                    step(dve.tensor_scalar(kc[:, 0:15], bank[0][:, 0:15], float(KEEP), None, ALU.is_ge))
                    step(dve.tensor_reduce(kc[:, 15:16], kc[:, 0:15], AX.X, ALU.add))
                    step(dve.tensor_scalar(thr[:, part, r + 1:r + 2], kc[:, 15:16], unit, thr[:, part, r:r + 1], ALU.mult, ALU.add))
                if part == 0:
                    t = thr[:, 0, 4:5]
                    step(dve.tensor_scalar(keyf[:, 3, :], keyf[:, 0, :], t, 131072.0, ALU.is_gt, ALU.mult), False)
                    step(dve.tensor_scalar(keyf[:, 2, :], keyf[:, 0, :], t, None, ALU.is_equal))
                    step(dve.tensor_scalar(keyf[:, 1, :], keyf[:, 1, :], 1.0, None, ALU.add))
                    step(dve.tensor_tensor(keyf[:, 1, :], keyf[:, 1, :], keyf[:, 2, :], ALU.mult))
                    step(dve.tensor_tensor(keyf[:, 2, :], keyf[:, 1, :], keyf[:, 3, :], ALU.add))
                    step(dve.tensor_scalar(keyf[:, 2, :], keyf[:, 2, :], -1.0, None, ALU.add))
            t = thr[:, 1, 4:5]
            step(dve.tensor_scalar(mask[:, :], keyf[:, 2, :], t, None, ALU.is_gt), False)
            step(dve.tensor_scalar(keyf[:, 0, :], keyf[:, 2, :], t, None, ALU.is_equal), False)
            step(dve.tensor_scalar(eqb[:, :], keyf[:, 2, :], t, None, ALU.is_equal))
            step(dve.tensor_reduce(kc[:, 0:1], mask[:, :], AX.X, ALU.add))
            dve.tensor_scalar(kc[:, 1:2], kc[:, 0:1], 1.0, None, ALU.mult).then_inc(S("eq_ready"), 1)
            dve.wait_ge(S("eq_done"), 1)
            step(dve.tensor_copy(keyf[:, 1, :], bank[0][:, 128:128 + T]))
            step(dve.tensor_tensor_scan(keyf[:, 3, :], keyf[:, 1, :], ones_f[:, 0:T], 0.0, ALU.add, ALU.mult))
            step(dve.tensor_tensor(keyf[:, 3, :], keyf[:, 3, :], keyf[:, 1, :], ALU.subtract))
            step(dve.tensor_tensor(keyf[:, 3, :], keyf[:, 3, :], bank[0][:, 64:64 + T], ALU.add))
            step(dve.tensor_scalar(keyf[:, 3, :], keyf[:, 3, :], bank[0][:, 200:201], float(KEEP), ALU.add, ALU.is_lt))
            step(dve.tensor_tensor(keyf[:, 3, :], keyf[:, 3, :], keyf[:, 0, :], ALU.mult))
            step(dve.tensor_tensor(mask[:, :], mask[:, :], keyf[:, 3, :], ALU.add))
            with dve.Fori(0, T) as i:
                dve.scalar_tensor_tensor(base[:, ds(i * D, D)], side[:, ds(i * D, D)], mask[:, ds(i, 1)],
                                         base[:, ds(i * D, D)], ALU.mult, ALU.add).then_inc(S("out_ready"), 1)

        @block.scalar
        def _(act):
            def dense_ln(q, par):
                i = 2 * q + par
                act.wait_ge(S("ln_var"), i + 1)
                act.activation(sd[:, 1:2], sd[:, 0:1], ACT.Sqrt).then_inc(S("ln_sd"), 1)
                act.wait_ge(S("xt_done"), i + 1)
                act.activation(xt[:, par, :, :].rearrange("p k n -> p (k n)"), psT[par], ACT.Copy).then_inc(S("xt_ready"), 1)
                if not (isinstance(i, int) and i == 0):
                    kv_sqrt(i - 1)
                act.wait_ge(S("kv_psum"), i + 1)
                wait(act, S("kv_ss"), i)
                act.activation(sq[:, :], bank[3 + par][:, :], ACT.Square).then_inc(S("kv_sq"), 1)

            def kv_sqrt(i):
                act.wait_ge(S("kv_var"), i + 1)
                act.activation(kvs[:, 2, :], kvs[:, 1, :], ACT.Sqrt).then_inc(S("kv_sd"), 1)

            def mix(q, par):
                i = 2 * q + par
                act.wait_ge(S("mxt_done"), i + 1)
                act.activation(xt[:, par, :, :].rearrange("p k n -> p (k n)"), psT[par], ACT.Copy).then_inc(S("mxt_ready"), 1)
                act.wait_ge(S("h_psum"), i + 1)
                for f in range(KD):
                    act.activation(ht[:, par, f, :], bank[3][:, par * D + f * P:par * D + (f + 1) * P], ACT.Gelu,
                                   bias=b1p[:, f:f + 1]).then_inc(S("h_ready"), 1)
                act.wait_ge(S("mlp_psum"), i + 1)
                mp = bank[4 + par][:, 0:D]
                wait(act, S("l3_sum"), i - 1)
                act.activation(side[:, ds(i * D, D)], mp, ACT.Relu)
                act.activation(ml[:, par, :], mp, ACT.Relu).then_inc(S("mlp_ready"), 1)

            each_tile(act, dense_ln)
            kv_sqrt(T - 1)
            act.wait_ge(S("w1p_ready"), 1)
            each_tile(act, mix)

            def gelu(i, part):
                act.wait_ge(S("f1_psum"), 2 * i + part + 1)
                for f in range(part * KF // 2, (part + 1) * KF // 2):
                    act.activation(fh[:, f, :], bank[4 + part][:, (f % 4) * P:(f % 4 + 1) * P], ACT.Gelu_apprx_tanh,
                                   bias=b1f[:, f:f + 1]).then_inc(S("fh_ready"), 1)

            def stage(i, here, before1, before2, before3):
                if before1:
                    act.wait_ge(S("acc_b"), i)
                    act.activation(agg[:, 1, :], bank[1][:, 0:D], ACT.Copy).then_inc(S("agg_b"), 1)
                    act.wait_ge(S("at_psum"), i)
                    for k in range(KD):
                        ins = act.activation(aggt[:, k, :, :].rearrange("p v (h n) -> p v h n", h=2),
                                             bank[2][:, k * D:(k + 1) * D].rearrange("p (h v n) -> p v h n", h=2, v=2), ACT.Copy)
                    ins.then_inc(S("aggt_ready"), 1)
                    act.wait_ge(S("lh_psum"), i)
                    wait(act, S("lh_used"), i - 1)
                    act.activation(lh[:, :], bank[3][:, :], ACT.Relu).then_inc(S("lh_ready"), 1)
                if before2:
                    act.wait_ge(S("xt_psum"), i - 1)
                    act.activation(x2t[:, :, :].rearrange("p k n -> p (k n)"), bank[6][:, 0:D], ACT.Copy).then_inc(S("x2t_ready"), 1)
                if here:
                    act.wait_ge(S("acc_a"), i + 1)
                    act.activation(agg[:, 0, :], bank[0][:, 0:D], ACT.Copy).then_inc(S("agg_a"), 1)
                if before1:
                    act.wait_ge(S("lg_ready"), i)
                    act.activation(sg[:, 0, :], lg[:, :], ACT.Tanh, scale=0.5).then_inc(S("sig_tanh"), 1)
                    act.wait_ge(S("att_in"), i)
                    act.activation(sg[:, 6, :], sg[:, 3, :], ACT.Tanh, bias=sg[:, 5, 0:1], scale=-1.0).then_inc(S("att_tanh"), 1)
                    act.wait_ge(S("x1_guess"), i)
                    y = nri[:, 1:2].bitcast(F32)
                    for r in range(3):
                        act.activation(nr[:, 2:3], y, ACT.Square).then_inc(S("newton"), 1)
                        act.wait_ge(S("newton"), 8 * (i - 1) + 3 * r + 1)
                        act.activation(nr[:, 3:4], nr[:, 2:3], ACT.Identity, bias=const_1_5[:, 0:1], scale=nr[:, 1:2]).then_inc(S("newton"), 1)
                        act.wait_ge(S("newton"), 8 * (i - 1) + 3 * r + 2)
                        o = nr[:, (4, 6, 4)[r]:(5, 7, 5)[r]]
                        act.activation(o, nr[:, 3:4], ACT.Copy, scale=y).then_inc(S("newton" if r < 2 else "x1_rs"), 1)
                        if r < 2:
                            act.wait_ge(S("newton"), 8 * (i - 1) + 3 * r + 3)
                        y = o
                if before3:
                    act.wait_ge(S("y_psum"), i - 2)
                    act.wait_ge(S("w_ready"), i - 2)
                    act.activation(side[:, ds((i - 3) * D, D)], bank[7][:, 0:D], ACT.Copy, scale=wall[:, ds(i - 3, 1)]).then_inc(S("y_ready"), 1)
                if before2:
                    gelu(i - 2, 0)
                    gelu(i - 2, 1)

            pipeline(act, stage)

        @block.tensor
        def _(pe):
            def mm(out_, lhsT, rhs, start, stop, **kw):
                return pe.matmul(out_, lhsT, rhs, start=start, stop=stop, **kw)

            M = H1 * HALF
            pe.wait_ge(S("digits_ready"), H1 + H2)
            for g in range(HALVES):
                ins = mm(bank[7][0:M, 0:HALF * H2], oh1[:, g * M:(g + 1) * M], oh2[:, g * HALF * H2:(g + 1) * HALF * H2],
                         g == 0, g == HALVES - 1)
            ins.then_inc(S("hist_done"), 1)
            pe.wait_ge(S("hist_expanded"), 1)
            mm(bank[6][:, 0:H1 * H2], ones_f[0:M, :], hexp[0:M, :, :].rearrange("p a b -> p (a b)"), True, True).then_inc(S("counts_ready"), 1)
            pe.wait_ge(S("starts_ready"), 1)
            mm(R, ones_f[0:1, :], starts[0:1, 0:NB], True, False, skip_group_check=True)

            def open_half(h, hf):
                pe.wait_ge(S("oh_ready"), h + 1)
                for j in range(HALF):
                    ins = mm(R, before[:, :], oh[:, hf, j, :], False, False, skip_group_check=True)
                ins.then_inc(S("rank_ready"), 1)

            def close_half(h, hf):
                pe.wait_ge(S("rank_read"), 2 * h + 2)
                for j in range(HALF):
                    ins = mm(R, notbefore[:, :], oh[:, hf, j, :], False, False, skip_group_check=True)
                ins.then_inc(S("oh_used"), 1)

            def next_half(h, hf, more=True):
                close_half(h, hf)
                if more:
                    open_half(h + 1, 1 - hf)

            open_half(0, 0)
            for h in range(LEAD):
                next_half(h, h % 2)
            pe.wait_ge(S("wkv_ready"), 1)
            mm(bank[5][:, 0:D + 2 * KD], zero_b[:, 0:P], zero_b[:, :], True, False, skip_group_check=True)

            def normalise(q, par):
                i = 2 * q + par
                pe.wait_ge(S("xn_ready"), i + 1)
                for k in range(KD):
                    ins = pe.transpose(psT[par][:, k * P:(k + 1) * P], xs[:, par, k * P:(k + 1) * P], ident[:, :])
                ins.then_inc(S("xt_done"), 1)
                next_half(LEAD + i, par)
                pe.wait_ge(S("xt_ready"), i + 1)
                wait(pe, S("kn_ready"), i - 1)
                kv = bank[3 + par][:, :]
                mm(kv, ones_b[0:65, :], bkv3[0:65, :], True, False)
                for k in range(KD):
                    ins = mm(kv, xt[:, par, k, :], wkv[:, k, :], False, k == KD - 1)
                ins.then_inc(S("kv_psum"), 1)
                if not (isinstance(i, int) and i == 0):
                    add_kv(i - 1, 1 - par, P)

            def add_kv(i, par, n):
                pe.wait_ge(S("kn_ready"), i + 1)
                for j in range(KD):
                    k_j = kn[0:n, par, 0, j * P:(j + 1) * P]
                    v_j = kn[0:n, par, 1, j * P:(j + 1) * P]
                    mm(bank[5][:, j * P:(j + 1) * P], k_j, v_j, False, False, skip_group_check=True)
                    mm(bank[5][:, D + j:D + j + 1], k_j, ones_f[0:n, 0:1], False, False, skip_group_check=True)
                    ins = mm(bank[5][:, D + KD + j:D + KD + j + 1], v_j, ones_f[0:n, 0:1], False, False, skip_group_check=True)
                ins.then_inc(S("kv_added"), 1)

            def mix(q, par):
                i = 2 * q + par
                pe.wait_ge(S(f"mix_loaded{par}"), 32 * q + 32)
                for k in range(KD):
                    ins = pe.transpose(psT[par][:, k * P:(k + 1) * P], xs[:, par, k * P:(k + 1) * P], ident[:, :])
                ins.then_inc(S("mxt_done"), 1)
                next_half(MIX0 + i, (MIX0 + par) % 2)
                if not (isinstance(i, int) and i == 0):
                    mix_end(i - 1, 1 - par)
                pe.wait_ge(S("mxt_ready"), i + 1)
                for f in range(KD):
                    for k in range(KD):
                        ins = mm(bank[3][:, par * D + f * P:par * D + (f + 1) * P], w1p[:, k, f * P:(f + 1) * P], xt[:, par, k, :],
                                 k == 0, k == KD - 1)
                ins.then_inc(S("h_psum"), 1)
                wait(pe, S("mlp_ready"), i - 1)
                for k in range(KD):
                    ins = mm(bank[4 + par][:, 0:D], xt[:, par, k, :], wmlp[:, k, :], k == 0, k == KD - 1)
                ins.then_inc(S("mlp_psum"), 1)

            def mix_end(i, par):
                wait(pe, S("mix_read"), i - 1)
                mm(bank[6 + par][:, 0:D], ones_b[0:65, :], b2m3[0:65, :], True, False)
                pe.wait_ge(S("h_ready"), 2 * i + 2)
                for f in range(KD):
                    ins = mm(bank[6 + par][:, 0:D], ht[:, par, f, :], w2m[:, f, :], False, f == KD - 1)
                ins.then_inc(S("mix_psum"), 1)

            each_tile(pe, normalise)
            add_kv(T - 1, 0, TAIL)
            W = D + 2 * KD
            mm(bank[5][:, 0:W], zero_b[:, 0:P], zero_b[:, 0:W], False, True, skip_group_check=True).then_inc(S("kv_summed"), 1)

            for j in range(KD):
                for k in range(KD):
                    ins = pe.transpose(bank[6][:, j * D + k * P:j * D + (k + 1) * P], wq[:, k, j * P:(j + 1) * P], ident[:, :])
            ins.then_inc(S("wq_transposed"), 1)
            pe.wait_ge(S("v_sum_diag"), 1)
            for j in range(KD):
                ins = mm(bank[4][:, j * P:(j + 1) * P], ones_f[:, :], fold[:, 1, j, :], True, True)
            ins.then_inc(S("v_sum_rows"), 1)
            pe.wait_ge(S("wqt_ready"), 1)
            for j in range(KD):
                mm(bank[7][:, j * D:(j + 1) * D], kvbd[:, j, :], wqt[:, j, :], True, True)
            pe.wait_ge(S("w_loaded"), 16 * 32)
            for j in range(KD):
                ins = mm(bank[3][:, j:j + 1], kvbd[:, j, :], bq[:, j:j + 1], True, True)
            ins.then_inc(S("at_done"), 1)
            next_half(LEAD + T, (LEAD + T) % 2)
            pe.wait_ge(S("at_ready"), 1)
            for k in range(KD):
                for j in range(KD):
                    mm(bank[6][:, k * D:(k + 1) * D], atm[:, j, k * P:(k + 1) * P], w1m[:, j, :], j == 0, j == KD - 1)
            for f in range(KD):
                for j in range(KD):
                    ins = mm(bank[3][:, 8 + f:9 + f], w1m[:, j, f * P:(f + 1) * P], bp[:, j:j + 1], j == 0, j == KD - 1)
            ins.then_inc(S("w1p_done"), 1)
            next_half(LEAD + T + 1, (LEAD + T + 1) % 2)
            pe.wait_ge(S("w1p_ready"), 1)

            each_tile(pe, mix)
            mix_end(T - 1, 0)
            for h in range(MIX0 + T, HALVES):
                next_half(h, h % 2, more=h < HALVES - 1)

            pe.wait_ge(S("ptab_ready"), 1)
            pe.wait_ge(S("ffn_loaded"), 32)
            pe.wait_ge(S("rank_read"), 2 * HALVES)

            def sum_pair(b, pair, k, acc):
                ready = pe.snap(2 * (pair + b) + 2)
                at = (pair % (GR // 2)) * (2 * D)
                gathered = [gring[:, :, :].rearrange("p s d -> p (s d)")[:, ds(at + j * D, D)] for j in range(2)]
                for j in range(2):
                    pe.wait_ge(S("sel_ready"), ready + j + 1)
                    mm(acc[:, 0:D], msel[:, 2 * k + j, :], gathered[j], False, False, skip_group_check=True).then_inc(S("sel_used"), 1)

            def bucket(b, lo, hi, acc, done):
                mm(acc[:, 0:D], zero_b[:, 0:P], zero_b[:, 0:D], True, False, skip_group_check=True)
                bucket_pairs(pe, lo, hi, lambda pair, k, first: sum_pair(b, pair, k, acc))
                mm(acc[:, 0:D], zero_b[:, 0:P], zero_b[:, 0:D], False, True, skip_group_check=True).then_inc(S(done), 1)

            def up(part):
                for f in range(part * KF // 2, (part + 1) * KF // 2):
                    for k in range(KD):
                        ins = mm(bank[4 + part][:, (f % 4) * P:(f % 4 + 1) * P], w1f[:, k, f * P:(f + 1) * P], x2t[:, k, :],
                                 k == 0, k == KD - 1)
                return ins

            def stage(i, here, before1, before2, before3):
                if here:
                    lo, mid, hi = pair_ranges(pe, i)
                if before1:
                    pe.wait_ge(S("agg_b"), i)
                    for k in range(KD):
                        for h in range(2):
                            ins = pe.transpose(bank[2][:, k * D + h * P:k * D + (h + 1) * P], agg[:, h, k * P:(k + 1) * P], ident[:, :])
                    ins.then_inc(S("at_psum"), 1)
                if before1:
                    pe.wait_ge(S("aggt_ready"), i)
                    wait(pe, S("lh_ready"), i - 1)
                    for v, w in enumerate((wlow, whigh)):
                        for k in range(KD):
                            ins = mm(bank[3][:, v * D:(v + 1) * D], aggt[:, k, v, :], w[:, k, :], k == 0, k == KD - 1)
                    ins.then_inc(S("lh_psum"), 1)
                if before2:
                    pe.wait_ge(S("x2_ready"), i - 1)
                    for k in range(KD):
                        ins = pe.transpose(bank[6][:, k * P:(k + 1) * P], x2n[:, k * P:(k + 1) * P], ident[:, :])
                    ins.then_inc(S("xt_psum"), 1)
                if here:
                    wait(pe, S("agg_a"), i)
                    bucket(2 * i, lo, mid, bank[0], "acc_a")
                if before3:
                    wait(pe, S("y_ready"), i - 3)
                    mm(bank[7][:, 0:D], ones_b[0:65, :], b2f3[0:65, :], True, False)
                    pe.wait_ge(S("fh_ready"), (i - 2) * KF)
                    for f in range(KF):
                        ins = mm(bank[7][:, 0:D], fh[:, f, :], w2f[:, f, :], False, f == KF - 1)
                    ins.then_inc(S("y_psum"), 1)
                if before2:
                    pe.wait_ge(S("x2t_ready"), i - 1)
                    for part in range(2):
                        up(part).then_inc(S("f1_psum"), 1)
                if here:
                    wait(pe, S("agg_b"), i)
                    bucket(2 * i + 1, mid, hi, bank[1], "acc_b")

            pe.wait_ge(S("b2f_ready"), 1)
            pe.sem_inc(S("sel_used"), 2)
            pipeline(pe, stage)

            for r in range(8):
                pe.wait_ge(S("cnt_ready"), r + 1)
                mm(bank[0][:, 0:15], ones_f[:, :], cnt[:, :], True, True).then_inc(S("cnt_total"), 1)
            pe.wait_ge(S("eq_ready"), 1)
            mm(bank[0][:, 64:64 + T], before[:, :], eqb[:, :], True, True)
            mm(bank[0][:, 128:128 + T], ones_b[:, :], eqb[:, :], True, True)
            mm(bank[0][:, 200:201], ones_f[:, :], kc[:, 1:2], True, True).then_inc(S("eq_done"), 1)


_INS = ["x", "src", "dst", "edge_weight", "edge_weight_n2",
        "L0_gnn_weight_low", "L0_gnn_weight_high", "L0_gnn_weight_mlp",
        "L0_gnn_att_vec_low", "L0_gnn_att_vec_high", "L0_gnn_att_vec_mlp", "L0_gnn_att_vec",
        "L0_mix_w_qkv", "L0_mix_b_qkv", "L0_mix_kln_g", "L0_mix_kln_b", "L0_mix_vln_g", "L0_mix_vln_b",
        "L0_mix_w1", "L0_mix_b1", "L0_mix_w2", "L0_mix_b2",
        "L0_ffn_wr", "L0_ffn_br", "L0_ffn_w1", "L0_ffn_b1", "L0_ffn_w2", "L0_ffn_b2"]


def kernel(**inputs):
    import numpy as np
    import concourse.bacc as bacc
    from concourse.bass_utils import run_bass_kernel_spmd

    nc = bacc.Bacc("TRN2", target_bir_lowering=False, num_devices=1)
    arrays, args = {}, {}
    for name in _INS:
        v = np.ascontiguousarray(inputs[name])
        arrays[f"in_{name}"] = v
        args[name] = nc.dram_tensor(f"in_{name}", v.shape, mybir.dt.from_np(v.dtype), kind="ExternalInput").ap()
    out = nc.dram_tensor("out_0", inputs["x"].shape, F32, kind="ExternalOutput").ap()
    build(nc, args, out)
    r = run_bass_kernel_spmd(nc, [arrays], core_ids=[0])
    return r.results[0]["out_0"]
```
